# Optimizing a Trainium2 kernel written in Bass

```python
import numpy as np
import jax
import jax.numpy as jnp

def _softmax(x, axis=-1):
    return jax.nn.softmax(x, axis=axis)

def _gelu(x):
    return jax.nn.gelu(x, approximate=True)

def _silu(x):
    return jax.nn.silu(x)

def _sigmoid(x):
    return jax.nn.sigmoid(x)

def _layernorm(x, axis=-1, eps=1e-05):
    m = jnp.mean(x, axis=axis, keepdims=True)
    v = jnp.var(x, axis=axis, keepdims=True)
    return (x - m) / jnp.sqrt(v + eps)

def _scatter_add(tgt, idx, src, axis=0):
    return tgt.at[idx].add(src)

def _segment_sum(src, seg, n):
    return jax.ops.segment_sum(src, seg, n)
kernel_name = 'mk_gnn_resnorm_d4_gnn_r64_78f78f'

def setup_inputs(seed: int=0):
    np.random.seed(seed)
    _w = jnp.asarray

    def _rec_inputs():
        import jax
        import jax.numpy as jnp
        _gk = jax.random.key(seed)
        x = -0.0003713 + 1 * jax.random.normal(jax.random.fold_in(_gk, 1), (100000, 128), jnp.float32)
        src = jax.random.randint(jax.random.fold_in(_gk, 2), (25000,), 0, 100000, jnp.int32)
        dst = jax.random.randint(jax.random.fold_in(_gk, 3), (25000,), 0, 100000, jnp.int32)
        _o = jnp.argsort(dst, stable=True)
        src = src[_o]
        dst = dst[_o]
        edge_weight = jax.random.uniform(jax.random.fold_in(_gk, 12), (25000,), jnp.float32, 0.0, 0.999999)
        return (x, src, dst, edge_weight)
    x, src, dst, edge_weight = _rec_inputs()

    def _L0_gnn_setup():
        import jax, jax.numpy as jnp
        import numpy as np
        N = 100000
        E = 9375
        D = 128
        EPS = 1e-05

        def _graph_conv(x, src, dst, ew, W, b, norm_src, norm_dst):
            h = x * norm_src[:, None]
            msg = h[src] * ew[:, None]
            agg = jax.ops.segment_sum(msg, dst, num_segments=N)
            out = agg @ W
            return out * norm_dst[:, None] + b

        def _batch_norm(h, gamma, beta):
            mean = jnp.mean(h, axis=0)
            var = jnp.mean(jnp.square(h - mean), axis=0)
            return gamma * (h - mean) * jax.lax.rsqrt(var + EPS) + beta
        key = jax.random.key(seed)
        ks = jax.random.split(key, 12)
        x = jax.random.normal(ks[0], (N, D), dtype=jnp.float32)
        edge_src = jax.random.randint(ks[1], (E,), 0, N, dtype=jnp.int32)
        edge_dst = jax.random.randint(ks[2], (E,), 0, N, dtype=jnp.int32)
        edge_weight = jax.random.uniform(ks[3], (E,), dtype=jnp.float32)
        W1 = 0.1 * jax.random.normal(ks[4], (D, D), dtype=jnp.float32)
        W2 = 0.1 * jax.random.normal(ks[5], (D, D), dtype=jnp.float32)
        W3 = 0.1 * jax.random.normal(ks[6], (D, D), dtype=jnp.float32)
        b1 = jnp.zeros((D,), jnp.float32)
        b2 = jnp.zeros((D,), jnp.float32)
        b3 = jnp.zeros((D,), jnp.float32)
        gamma = jnp.ones((D,), jnp.float32)
        beta = jnp.zeros((D,), jnp.float32)
        return dict(x=x, edge_src=edge_src, edge_dst=edge_dst, edge_weight=edge_weight, W1=W1, b1=b1, W2=W2, b2=b2, W3=W3, b3=b3, gamma=gamma, beta=beta)
    _L0_gnn_all = _L0_gnn_setup()
    _L0_gnn_in = {k: v for k, v in _L0_gnn_all.items() if k in ('W1', 'b1', 'W2', 'b2', 'W3', 'b3', 'gamma', 'beta')}
    del _L0_gnn_all

    def _L1_gnn_setup():
        import jax, jax.numpy as jnp
        import numpy as np
        N_NODES = 100000
        N_EDGES = 25000
        IN_FEATS = 128
        OUT_FEATS = 128
        key = jax.random.key(seed)
        k1, k2, k3, k4, k5, k6 = jax.random.split(key, 6)
        feat = jax.random.normal(k1, (N_NODES, IN_FEATS), dtype=jnp.float32)
        src = jax.random.randint(k2, (N_EDGES,), 0, N_NODES, dtype=jnp.int32)
        dst = jax.random.randint(k3, (N_EDGES,), 0, N_NODES, dtype=jnp.int32)
        gain = float(np.sqrt(2.0))
        limit = gain * float(np.sqrt(6.0 / (IN_FEATS + OUT_FEATS)))
        w_neigh = jax.random.uniform(k4, (OUT_FEATS, IN_FEATS), minval=-limit, maxval=limit, dtype=jnp.float32)
        w_self = jax.random.uniform(k5, (OUT_FEATS, IN_FEATS), minval=-limit, maxval=limit, dtype=jnp.float32)
        b_self = jax.random.uniform(k6, (OUT_FEATS,), minval=-0.05, maxval=0.05, dtype=jnp.float32)
        return {'feat': feat, 'w_neigh': w_neigh, 'w_self': w_self, 'b_self': b_self, 'src': src, 'dst': dst}
    _L1_gnn_all = _L1_gnn_setup()
    _L1_gnn_in = {k: v for k, v in _L1_gnn_all.items() if k in ('w_neigh', 'w_self', 'b_self')}
    del _L1_gnn_all

    def _L2_gnn_setup():
        import jax, jax.numpy as jnp
        import numpy as np
        N_NODES = 100000
        N_EDGES = 25000
        IN_DIM = 128
        HID_DIM = 128
        OUT_DIM = 128

        def _deg_norm(idx, n):
            deg = jax.ops.segment_sum(jnp.ones(idx.shape[0], jnp.float32), idx, num_segments=n)
            return jnp.clip(deg, 1.0, None) ** (-0.5)

        def gcn_layer(x, W, b, src, dst, norm_src, norm_dst, n):
            h = x * norm_src[:, None]
            msg = jnp.take(h, src, axis=0)
            agg = jax.ops.segment_sum(msg, dst, num_segments=n)
            agg = agg * norm_dst[:, None]
            return agg @ W + b
        key = jax.random.key(seed)
        ks = jax.random.split(key, 16)
        x = jax.random.normal(ks[0], (N_NODES, IN_DIM), jnp.float32)
        src = jax.random.randint(ks[1], (N_EDGES,), 0, N_NODES)
        dst = jax.random.randint(ks[2], (N_EDGES,), 0, N_NODES)

        def lin(k, di, do):
            s = 1.0 / np.sqrt(di)
            k1, k2 = jax.random.split(k)
            return (jax.random.uniform(k1, (di, do), jnp.float32, -s, s), jax.random.uniform(k2, (do,), jnp.float32, -s, s))
        W1, b1 = lin(ks[3], IN_DIM, HID_DIM)
        W2, b2 = lin(ks[4], HID_DIM, HID_DIM)
        W3, b3 = lin(ks[5], HID_DIM, HID_DIM)
        W4, b4 = lin(ks[6], HID_DIM, OUT_DIM)
        gamma = jnp.ones((OUT_DIM,), jnp.float32)
        beta = jnp.zeros((OUT_DIM,), jnp.float32)
        return {'x': x, 'src': src, 'dst': dst, 'W1': W1, 'b1': b1, 'W2': W2, 'b2': b2, 'W3': W3, 'b3': b3, 'W4': W4, 'b4': b4, 'gamma': gamma, 'beta': beta}
    _L2_gnn_all = _L2_gnn_setup()
    _L2_gnn_in = {k: v for k, v in _L2_gnn_all.items() if k in ('W1', 'b1', 'W2', 'b2', 'W3', 'b3', 'W4', 'b4', 'gamma', 'beta')}
    del _L2_gnn_all

    def _L3_gnn_setup():
        import jax, jax.numpy as jnp
        import numpy as np
        N_NODES = 10000
        N_EDGES = 10000
        IN, HID, OUT = (128, 256, 128)

        def _mean_agg(h, src, dst, n_nodes):
            summed = jax.ops.segment_sum(h[src], dst, num_segments=n_nodes)
            deg = jax.ops.segment_sum(jnp.ones_like(dst, dtype=h.dtype), dst, num_segments=n_nodes)
            return summed / jnp.maximum(deg, 1.0)[:, None]

        def _sage_layer(h, src, dst, w_self, w_neigh, b):
            neigh = _mean_agg(h, src, dst, h.shape[0])
            return h @ w_self + neigh @ w_neigh + b
        key = jax.random.key(seed)
        ks = jax.random.split(key, 8)
        scale_in = 1.0 / np.sqrt(IN)
        scale_hid = 1.0 / np.sqrt(HID)
        return {'x': jax.random.normal(ks[0], (N_NODES, IN), dtype=jnp.float32), 'w_self1': jax.random.normal(ks[1], (IN, HID), dtype=jnp.float32) * scale_in, 'w_neigh1': jax.random.normal(ks[2], (IN, HID), dtype=jnp.float32) * scale_in, 'b1': jnp.zeros((HID,), dtype=jnp.float32), 'w_self2': jax.random.normal(ks[3], (HID, OUT), dtype=jnp.float32) * scale_hid, 'w_neigh2': jax.random.normal(ks[4], (HID, OUT), dtype=jnp.float32) * scale_hid, 'b2': jnp.zeros((OUT,), dtype=jnp.float32), 'src': jax.random.randint(ks[5], (N_EDGES,), 0, N_NODES, dtype=jnp.int64 if jax.config.jax_enable_x64 else jnp.int32), 'dst': jax.random.randint(ks[6], (N_EDGES,), 0, N_NODES, dtype=jnp.int64 if jax.config.jax_enable_x64 else jnp.int32)}
    _L3_gnn_all = _L3_gnn_setup()
    _L3_gnn_in = {k: v for k, v in _L3_gnn_all.items() if k in ('w_self1', 'w_neigh1', 'b1', 'w_self2', 'w_neigh2', 'b2')}
    del _L3_gnn_all
    return {'x': x, 'src': src, 'dst': dst, 'edge_weight': edge_weight, 'L0_gnn_W1': _L0_gnn_in['W1'], 'L0_gnn_b1': _L0_gnn_in['b1'], 'L0_gnn_W2': _L0_gnn_in['W2'], 'L0_gnn_b2': _L0_gnn_in['b2'], 'L0_gnn_W3': _L0_gnn_in['W3'], 'L0_gnn_b3': _L0_gnn_in['b3'], 'L0_gnn_gamma': _L0_gnn_in['gamma'], 'L0_gnn_beta': _L0_gnn_in['beta'], 'L1_gnn_w_neigh': _L1_gnn_in['w_neigh'], 'L1_gnn_w_self': _L1_gnn_in['w_self'], 'L1_gnn_b_self': _L1_gnn_in['b_self'], 'L2_gnn_W1': _L2_gnn_in['W1'], 'L2_gnn_b1': _L2_gnn_in['b1'], 'L2_gnn_W2': _L2_gnn_in['W2'], 'L2_gnn_b2': _L2_gnn_in['b2'], 'L2_gnn_W3': _L2_gnn_in['W3'], 'L2_gnn_b3': _L2_gnn_in['b3'], 'L2_gnn_W4': _L2_gnn_in['W4'], 'L2_gnn_b4': _L2_gnn_in['b4'], 'L2_gnn_gamma': _L2_gnn_in['gamma'], 'L2_gnn_beta': _L2_gnn_in['beta'], 'L3_gnn_w_self1': _L3_gnn_in['w_self1'], 'L3_gnn_w_neigh1': _L3_gnn_in['w_neigh1'], 'L3_gnn_b1': _L3_gnn_in['b1'], 'L3_gnn_w_self2': _L3_gnn_in['w_self2'], 'L3_gnn_w_neigh2': _L3_gnn_in['w_neigh2'], 'L3_gnn_b2': _L3_gnn_in['b2']}

def reference(x, src, dst, edge_weight, L0_gnn_W1, L0_gnn_b1, L0_gnn_W2, L0_gnn_b2, L0_gnn_W3, L0_gnn_b3, L0_gnn_gamma, L0_gnn_beta, L1_gnn_w_neigh, L1_gnn_w_self, L1_gnn_b_self, L2_gnn_W1, L2_gnn_b1, L2_gnn_W2, L2_gnn_b2, L2_gnn_W3, L2_gnn_b3, L2_gnn_W4, L2_gnn_b4, L2_gnn_gamma, L2_gnn_beta, L3_gnn_w_self1, L3_gnn_w_neigh1, L3_gnn_b1, L3_gnn_w_self2, L3_gnn_w_neigh2, L3_gnn_b2):
    import jax
    import jax.numpy as jnp

    def _L0_gnn_ref(x, edge_src, edge_dst, edge_weight, W1, b1, W2, b2, W3, b3, gamma, beta):
        import jax, jax.numpy as jnp
        import numpy as np
        N = 100000
        E = 9375
        D = 128
        EPS = 1e-05

        def _graph_conv(x, src, dst, ew, W, b, norm_src, norm_dst):
            h = x * norm_src[:, None]
            msg = h[src] * ew[:, None]
            agg = jax.ops.segment_sum(msg, dst, num_segments=N)
            out = agg @ W
            return out * norm_dst[:, None] + b

        def _batch_norm(h, gamma, beta):
            mean = jnp.mean(h, axis=0)
            var = jnp.mean(jnp.square(h - mean), axis=0)
            return gamma * (h - mean) * jax.lax.rsqrt(var + EPS) + beta
        ones = jnp.ones((edge_src.shape[0],), x.dtype)
        deg_out = jnp.clip(jax.ops.segment_sum(ones, edge_src, num_segments=N), 1.0)
        deg_in = jnp.clip(jax.ops.segment_sum(ones, edge_dst, num_segments=N), 1.0)
        ns = jax.lax.rsqrt(deg_out)
        nd = jax.lax.rsqrt(deg_in)
        h = _graph_conv(x, edge_src, edge_dst, edge_weight, W1, b1, ns, nd)
        h = jax.nn.elu(_batch_norm(h, gamma, beta))
        h = _graph_conv(h, edge_src, edge_dst, edge_weight, W2, b2, ns, nd)
        h = jax.nn.elu(_batch_norm(h, gamma, beta))
        h = _graph_conv(h, edge_src, edge_dst, edge_weight, W3, b3, ns, nd)
        h = _batch_norm(h, gamma, beta)
        return h

    def _L1_gnn_ref(feat, w_neigh, w_self, b_self, src, dst):
        import jax, jax.numpy as jnp
        import numpy as np
        N_NODES = 100000
        N_EDGES = 25000
        IN_FEATS = 128
        OUT_FEATS = 128
        h = jnp.einsum('ni,oi->no', feat, w_neigh)
        msg = h[src]
        summed = jax.ops.segment_sum(msg, dst, num_segments=N_NODES)
        deg = jax.ops.segment_sum(jnp.ones((src.shape[0],), feat.dtype), dst, num_segments=N_NODES)
        h_neigh = summed / jnp.maximum(deg, 1.0)[:, None]
        rst = jnp.einsum('ni,oi->no', feat, w_self) + b_self + h_neigh
        return rst

    def _L2_gnn_ref(x, src, dst, W1, b1, W2, b2, W3, b3, W4, b4, gamma, beta):
        import jax, jax.numpy as jnp
        import numpy as np
        N_NODES = 100000
        N_EDGES = 25000
        IN_DIM = 128
        HID_DIM = 128
        OUT_DIM = 128

        def _deg_norm(idx, n):
            deg = jax.ops.segment_sum(jnp.ones(idx.shape[0], jnp.float32), idx, num_segments=n)
            return jnp.clip(deg, 1.0, None) ** (-0.5)

        def gcn_layer(x, W, b, src, dst, norm_src, norm_dst, n):
            h = x * norm_src[:, None]
            msg = jnp.take(h, src, axis=0)
            agg = jax.ops.segment_sum(msg, dst, num_segments=n)
            agg = agg * norm_dst[:, None]
            return agg @ W + b
        n = x.shape[0]
        norm_src = _deg_norm(src, n)
        norm_dst = _deg_norm(dst, n)
        h = x
        for W, b in ((W1, b1), (W2, b2), (W3, b3)):
            h = jax.nn.gelu(gcn_layer(h, W, b, src, dst, norm_src, norm_dst, n), approximate=False)
        h = gcn_layer(h, W4, b4, src, dst, norm_src, norm_dst, n)
        mu = jnp.mean(h, axis=-1, keepdims=True)
        var = jnp.mean((h - mu) ** 2, axis=-1, keepdims=True)
        return (h - mu) * jax.lax.rsqrt(var + 1e-05) * gamma + beta

    def _L3_gnn_ref(x, w_self1, w_neigh1, b1, w_self2, w_neigh2, b2, src, dst):
        import jax, jax.numpy as jnp
        import numpy as np
        N_NODES = 10000
        N_EDGES = 10000
        IN, HID, OUT = (128, 256, 128)

        def _mean_agg(h, src, dst, n_nodes):
            summed = jax.ops.segment_sum(h[src], dst, num_segments=n_nodes)
            deg = jax.ops.segment_sum(jnp.ones_like(dst, dtype=h.dtype), dst, num_segments=n_nodes)
            return summed / jnp.maximum(deg, 1.0)[:, None]

        def _sage_layer(h, src, dst, w_self, w_neigh, b):
            neigh = _mean_agg(h, src, dst, h.shape[0])
            return h @ w_self + neigh @ w_neigh + b
        h = _sage_layer(x, src, dst, w_self1, w_neigh1, b1)
        h = jax.nn.relu(h)
        h = _sage_layer(h, src, dst, w_self2, w_neigh2, b2)
        return h
    x = _layernorm(x + _L0_gnn_ref(x, src, dst, edge_weight, L0_gnn_W1, L0_gnn_b1, L0_gnn_W2, L0_gnn_b2, L0_gnn_W3, L0_gnn_b3, L0_gnn_gamma, L0_gnn_beta), axis=-1)
    x = _layernorm(x + _L1_gnn_ref(x, L1_gnn_w_neigh, L1_gnn_w_self, L1_gnn_b_self, src, dst), axis=-1)
    x = _layernorm(x + _L2_gnn_ref(x, src, dst, L2_gnn_W1, L2_gnn_b1, L2_gnn_W2, L2_gnn_b2, L2_gnn_W3, L2_gnn_b3, L2_gnn_W4, L2_gnn_b4, L2_gnn_gamma, L2_gnn_beta), axis=-1)
    x = _layernorm(x + _L3_gnn_ref(x, L3_gnn_w_self1, L3_gnn_w_neigh1, L3_gnn_b1, L3_gnn_w_self2, L3_gnn_w_neigh2, L3_gnn_b2, src, dst), axis=-1)
    return x

_drawn_inputs = setup_inputs


def setup_inputs(seed=0):
    import zlib

    import numpy as np

    out = dict(_drawn_inputs(seed))
    spreads = {'L0_gnn_b1': (0.0, 0.8),
     'L0_gnn_b2': (0.0, 0.8),
     'L0_gnn_b3': (0.0, 0.8),
     'L0_gnn_gamma': (1.0, 0.6),
     'L0_gnn_beta': (0.0, 0.1),
     'L2_gnn_gamma': (1.0, 0.2),
     'L2_gnn_beta': (0.0, 0.1),
     'L3_gnn_b1': (0.0, 0.1),
     'L3_gnn_b2': (0.0, 0.1)}
    factors = {'L1_gnn_b_self': 4.557,
     'L2_gnn_W1': 8.0,
     'L2_gnn_b1': 8.0,
     'L2_gnn_W2': 7.985,
     'L2_gnn_b2': 5.891,
     'L2_gnn_W3': 4.84}
    for name, (base, spread) in spreads.items():
        noise = np.random.default_rng([zlib.crc32(name.encode()), seed]).standard_normal(out[name].shape)
        drawn = base * np.exp(spread * noise) if base else spread * noise
        out[name] = jnp.asarray(drawn.astype(out[name].dtype))
    for name, factor in factors.items():
        out[name] = (out[name] * factor).astype(out[name].dtype)
    return out
```

```python
from contextlib import ExitStack

import concourse.bass as bass
from concourse import mybir

F32 = mybir.dt.float32
I32 = mybir.dt.int32
BF16 = mybir.dt.bfloat16
F16 = mybir.dt.float16
ALU = mybir.AluOpType
ACT = mybir.ActivationFunctionType

P = 128
GT = 4
GE = GT * P
EPS = 1e-5
LO = 512
ABSENT = 1 << 20


class Signals:

    def __init__(self, nc):
        self.nc, self.sems, self.stage = nc, {}, 0

    def __call__(self, name, lane=0):
        key = f"{name}{lane}"
        if key not in self.sems:
            self.sems[key] = self.nc.alloc_semaphore(f"{key}_stage{self.stage}")
        return self.sems[key]

    def close(self):
        self.nc.clear_and_free_semaphores(list(self.sems.values()))
        self.nc.all_engine_barrier()
        self.sems = {}
        self.stage += 1


class Chain:

    def __init__(self, eng, sem):
        self.eng, self.sem, self.per_body, self.base, self.k = eng, sem, 0, 0, 0

    def body(self, i):
        if isinstance(i, int) and i == 0:
            self.k = 0
            self.base = 0
        else:
            if not self.per_body:
                self.per_body = self.k
            self.base, self.k = i * self.per_body, 0

    def step(self, ins):
        self.k += 1
        return ins.then_inc(self.sem, 1)

    def wait(self):
        self.eng.wait_ge(self.sem, self.base + self.k)


def first(i):
    return isinstance(i, int) and i == 0


def gnn_stack(nc, A, out):
    N, E = A["x"].shape[0], A["src"].shape[0]
    NT = -(-E // P)
    NG = -(-NT // GT)
    EP = NG * GE
    assert NT == NG * GT
    NPAIR, ODD = NG // 2, NG % 2
    TAIL = E - (NT - 1) * P
    T1 = NT - P
    NHI = -(-N // LO)
    H1 = NHI - P
    NONE_ROW = EP
    CH = EP // 7
    assert CH * 7 == EP
    IDXW = NT + 2 * GT

    def dram(name, shape, dt):
        return nc.dram_tensor(name, shape, dt, kind="Internal").ap()

    dst_lin = dram("dst_lin", [EP + 1, 1], I32)
    cnt_lin = dram("cnt_lin", [NT, P], F32)
    w0_lin = dram("w0_lin", [NT, P], F32)
    node_tab = dram("node_tab", [NHI * LO, 2], I32)
    tabs = {n: dram(f"tab_{n}", [EP + 1, P], F32)
            for n in ("z1", "z2", "z3", "a1", "g1", "g2", "g3", "a2", "n1", "a4")}
    xs = {n: dram(f"xs_{n}", [EP, P], F32) for n in ("x0", "x1", "x2", "x3")}
    x0d = dram("x0d", [EP, P], F32)

    def rows(ap, g, n=1):
        return ap[bass.ds(g * GE, GE), :].rearrange("(t p) f -> p t f", p=P)

    with ExitStack() as ctx:
        def sb(name, shape, dt=F32):
            return ctx.enter_context(nc.sbuf_tensor(name, shape, dt))

        def lanes(name, shape, dt=F32):
            return [sb(f"{name}_{l}", shape, dt) for l in range(2)]

        bank = [ctx.enter_context(nc.psum_tensor(f"bank{b}", [P, 512], F32)) for b in range(8)]

        ident = sb("ident", [P, P])
        ones_col = sb("ones_col", [P, 1])
        ones_mat = sb("ones_mat", [P, P])
        eps_col = sb("eps_col", [P, 1])
        zero_bf = sb("zero_bf", [P, LO], BF16)
        zero_f = sb("zero_f", [P, P])
        w = {n: sb(f"w_{n}", [P, P]) for n in
             ("L0_gnn_W1", "L0_gnn_W2", "L0_gnn_W3", "L2_gnn_W1", "L2_gnn_W2", "L2_gnn_W3", "L2_gnn_W4",
              "L1_gnn_w_neigh", "L1_gnn_w_self")}
        wnT = sb("wnT", [P, P])
        wsI = sb("wsI", [P, P])
        ws1 = sb("ws1", [P, 2 * P])
        wn1 = sb("wn1", [P, 2 * P])
        ws2 = sb("ws2", [P, 2, P])
        wn2 = sb("wn2", [P, 2, P])
        row = {n: sb(f"r_{n}", [P, P]) for n in
               ("L1_gnn_b_self", "L2_gnn_b1", "L2_gnn_b2", "L2_gnn_b3", "L2_gnn_b4", "L2_gnn_gamma", "L2_gnn_beta",
                "L3_gnn_b2")}
        a3_row = sb("a3_row", [P, P])
        c3_row = sb("c3_row", [P, P])
        a2_row = sb("a2_row", [P, P])
        none_rows = sb("none_rows", [P, 4, P])
        gam_col = sb("gam_col", [P, 1])
        bet_col = sb("bet_col", [P, 1])
        b1_col = sb("b1_col", [P, 2])
        bn_a = sb("bn_a", [P, 1])
        bn_c = sb("bn_c", [P, 1])
        bn_na = sb("bn_na", [P, 1])
        bn_nc = sb("bn_nc", [P, 1])
        bn_t = sb("bn_t", [P, 8])
        diag = sb("diag", [P, 2, P])

        same = sb("same", [P, EP], BF16)
        src_idx = sb("src_idx", [P, IDXW], I32)
        slot_idx = sb("slot_idx", [P, IDXW], I32)
        dst_idx = sb("dst_idx", [P, IDXW], I32)
        put_idx = sb("put_idx", [P, IDXW], I32)
        w0_c = sb("w0_c", [P, NT])
        nsrc_c = sb("nsrc_c", [P, NT])
        rdeg_c = sb("rdeg_c", [P, NT])
        nd_c = sb("nd_c", [P, NT])
        ndrep_c = sb("ndrep_c", [P, NT])
        rep_c = sb("rep_c", [P, NT])
        dst_c = sb("dst_c", [P, NT])
        ew_c = sb("ew_c", [P, NT])

        S = Signals(nc)

        with ExitStack() as scratch:
            def tmp(name, shape, dt=F32):
                return scratch.enter_context(nc.sbuf_tensor(name, shape, dt))

            src_t = tmp("src_t", [P, 2, P], I32)
            dst_t = tmp("dst_t", [P, 2, P], I32)
            nxt_t = tmp("nxt_t", [P, 2, P], I32)
            edge_f = tmp("edge_f", [P, 4, 2, P])
            nxt_f = tmp("nxt_f", [P, 2, P])
            with nc.Block() as block:
                @block.sync
                def _(sp):
                    sp.wait_ge(S("cleared"), 4)
                    n0 = P * P
                    for t, a, off in ((src_t, A["src"], 0), (dst_t, A["dst"], 0), (nxt_t, A["dst"], 1),
                                      (edge_f[:, 3], A["edge_weight"], 0)):
                        full = (T1 - 1) * P
                        sp.dma_start(t[:, 0, :], a[off:off + n0].rearrange("(t e) -> t e", e=P)
                                     ).then_inc(S("edges_in"), 16)
                        sp.dma_start(t[0:T1 - 1, 1, :], a[off + n0:off + n0 + full].rearrange("(t e) -> t e", e=P)
                                     ).then_inc(S("edges_in"), 16)
                        sp.dma_start(t[T1 - 1:T1, 1, 0:TAIL - off], a[off + n0 + full:E].rearrange("(t e) -> t e", t=1)
                                     ).then_inc(S("edges_in"), 16)
                    sp.wait_ge(S("edges_in"), 12 * 16)
                    body = dst_lin[1:EP + 1, :].rearrange("(t e) o -> t (e o)", e=P)
                    sp.dma_start(body[0:P, :], dst_t[:, 0, :]).then_inc(S("dst_out"), 16)
                    sp.dma_start(body[P:NT, :], dst_t[0:T1, 1, :]).then_inc(S("dst_out"), 16)
                    sp.dma_start(dst_lin[0:1, :], dst_t[T1:T1 + 1, 1, 0:1]).then_inc(S("dst_out"), 16)
                    sp.wait_ge(S("dst_out"), 48)

                @block.scalar
                def _(act):
                    for n in w:
                        act.dma_start(w[n][:, :], A[n]).then_inc(S("weights_in"), 16)
                    act.dma_start(ws1[:, :], A["L3_gnn_w_self1"]).then_inc(S("weights_in"), 16)
                    act.dma_start(wn1[:, :], A["L3_gnn_w_neigh1"]).then_inc(S("weights_in"), 16)
                    act.dma_start(ws2[:, :, :], A["L3_gnn_w_self2"].rearrange("(c p) f -> p c f", p=P)
                                  ).then_inc(S("weights_in"), 16)
                    act.dma_start(wn2[:, :, :], A["L3_gnn_w_neigh2"].rearrange("(c p) f -> p c f", p=P)
                                  ).then_inc(S("weights_in"), 16)
                    for n in row:
                        act.dma_start(row[n][:, :], A[n].rearrange("(o f) -> o f", o=1).broadcast_to([P, P])
                                      ).then_inc(S("weights_in"), 16)
                    act.dma_start(gam_col[:, :], A["L0_gnn_gamma"].rearrange("(p o) -> p o", o=1)
                                  ).then_inc(S("weights_in"), 16)
                    act.dma_start(bet_col[:, :], A["L0_gnn_beta"].rearrange("(p o) -> p o", o=1)
                                  ).then_inc(S("weights_in"), 16)
                    for c in range(2):
                        act.dma_start(b1_col[:, c:c + 1], A["L3_gnn_b1"][c * P:(c + 1) * P].rearrange("(p o) -> p o", o=1)
                                      ).then_inc(S("weights_in"), 16)
                    n_in = (len(w) + 4 + len(row) + 4) * 16
                    act.wait_ge(S("weights_in"), n_in)
                    act.sem_inc(S("weights_ready"), 1)

                @block.gpsimd
                def _(pool):
                    pool.memset(src_t[:, :, :], 0).then_inc(S("cleared"), 1)
                    pool.memset(dst_t[:, :, :], -1).then_inc(S("cleared"), 1)
                    pool.memset(nxt_t[:, :, :], -1).then_inc(S("cleared"), 1)
                    pool.memset(edge_f[:, 3], 0.0).then_inc(S("cleared"), 1)
                    pool.memset(ident[:, :], 0.0).then_inc(S("ident_zero"), 1)
                    pool.wait_ge(S("ident_zero"), 1)
                    pool.affine_select(out=ident[:, :], in_=ident[:, :], compare_op=ALU.not_equal, fill=1.0, base=0,
                                       pattern=[[-1, P]], channel_multiplier=1).then_inc(S("ident_ready"), 1)

                @block.vector
                def _(dve):
                    dve.memset(ones_col[:, :], 1.0)
                    dve.memset(ones_mat[:, :], 1.0)
                    dve.memset(eps_col[:, :], EPS)
                    dve.memset(zero_f[:, :], 0.0)
                    dve.memset(zero_bf[:, :], 0.0)
                    dve.memset(src_idx[:, :], 0).then_inc(S("idx_zero"), 1)
                    dve.memset(slot_idx[:, :], 0)
                    dve.memset(dst_idx[:, :], 0)
                    dve.memset(put_idx[:, :], 0).then_inc(S("idx_zero"), 1)
                    dve.wait_ge(S("edges_in"), 12 * 16)
                    dve.tensor_copy(edge_f[:, 0], src_t[:, :, :])
                    dve.tensor_copy(edge_f[:, 1], dst_t[:, :, :]).then_inc(S("as_float"), 1)
                    dve.tensor_copy(nxt_f[:, :, :], nxt_t[:, :, :]).then_inc(S("as_float"), 1)
                    dve.wait_ge(S("as_float"), 2)
                    dve.tensor_tensor(edge_f[:, 2], edge_f[:, 1], nxt_f[:, :, :], ALU.not_equal
                                      ).then_inc(S("edges_float"), 1)
                    dve.wait_ge(S("turned"), 1)
                    dve.wait_ge(S("idx_zero"), 2)
                    dve.tensor_copy(src_idx[:, 0:NT], bank[0][:, 0:NT])
                    dve.tensor_copy(dst_c[:, :], bank[1][:, 0:NT])
                    dve.tensor_copy(rep_c[:, :], bank[2][:, 0:NT])
                    dve.tensor_copy(ew_c[:, :], bank[3][:, 0:NT])
                    dve.tensor_copy(wnT[:, :], bank[4][:, 0:P])
                    dve.tensor_tensor(wsI[:, :], bank[4][:, P:2 * P], ident[:, :], ALU.add)

                @block.tensor
                def _(pe):
                    pe.wait_ge(S("ident_ready"), 1)
                    pe.wait_ge(S("weights_ready"), 1)
                    pe.transpose(bank[4][:, 0:P], w["L1_gnn_w_neigh"][:, :], ident[:, :])
                    pe.transpose(bank[4][:, P:2 * P], w["L1_gnn_w_self"][:, :], ident[:, :])
                    pe.wait_ge(S("edges_float"), 1)
                    for n in range(4):
                        pe.transpose(bank[n][:, 0:P], edge_f[:, n, 0, :], ident[:, :])
                        last = pe.transpose(bank[n][:, P:NT], edge_f[0:T1, n, 1, :], ident[0:T1, 0:T1])
                    last.then_inc(S("turned"), 1)
            S.close()

        with ExitStack() as scratch:
            def tmp(name, shape, dt=F32):
                return scratch.enter_context(nc.sbuf_tensor(name, shape, dt))

            chunk = [tmp(f"chunk_{l}", [P, CH + 1], I32) for l in range(2)]
            ones_row = tmp("ones_row", [1, CH])
            cnt = [tmp(f"cnt_{l}", [1, CH]) for l in range(2)]
            cnt_t = tmp("cnt_t", [P, 2, P])
            with nc.Block() as block:
                @block.sync
                def _(sp):
                    def load(c):
                        l = c % 2
                        if c >= 2:
                            sp.wait_ge(S("mask_ready"), c - 1)
                        sp.dma_start(chunk[l][:, :], dst_lin[c * CH:(c + 1) * CH + 1, :].rearrange("e o -> o e")
                                     .broadcast_to([P, CH + 1])).then_inc(S("chunk_in", l), 16)

                    load(0)
                    load(1)
                    for c in range(7):
                        sp.wait_ge(S("count_ready"), c + 1)
                        sp.dma_start(cnt_lin.rearrange("t e -> (t e)")[c * CH:(c + 1) * CH].rearrange("(o e) -> o e", o=1),
                                     cnt[c % 2][:, :]).then_inc(S("count_out", c % 2), 16)
                        if c + 2 < 7:
                            load(c + 2)
                    sp.wait_ge(S("count_out", 0), 4 * 16)
                    sp.wait_ge(S("count_out", 1), 3 * 16)
                    sp.dma_start(cnt_t[:, 0, :], cnt_lin[0:P, :]).then_inc(S("count_in"), 16)
                    sp.dma_start(cnt_t[0:T1, 1, :], cnt_lin[P:NT, :]).then_inc(S("count_in"), 16)

                @block.vector
                def _(dve):
                    dve.memset(ones_row[:, :], 1.0)
                    for c in range(7):
                        l = c % 2
                        part = slice(c * CH, (c + 1) * CH)
                        dve.wait_ge(S("chunk_in", l), 16 * (c // 2 + 1))
                        dve.tensor_tensor(same[:, part], chunk[l][:, 1:CH + 1], chunk[l][:, 0:CH], ALU.is_equal
                                          ).then_inc(S("mask_ready"), 1)
                        dve.wait_ge(S("mask_ready"), c + 1)
                        if c:
                            dve.wait_ge(S("count_ready"), c)
                        if c >= 2:
                            dve.wait_ge(S("count_out", l), 16 * (c // 2))
                        dve.tensor_tensor_scan(cnt[l][:, :], same[0:1, part], ones_row[:, :],
                                               cnt[1 - l][:, CH - 1:CH] if c else 0.0, ALU.mult, ALU.add
                                               ).then_inc(S("count_ready"), 1)
                    dve.wait_ge(S("turned"), 1)
                    dve.reciprocal(rdeg_c[:, :], bank[0][:, 0:NT]).then_inc(S("rdeg_ready"), 1)
                    dve.wait_ge(S("nd_ready"), 1)
                    dve.tensor_tensor(ndrep_c[:, :], nd_c[:, :], rep_c[:, :], ALU.mult)

                @block.tensor
                def _(pe):
                    pe.wait_ge(S("count_in"), 32)
                    pe.transpose(bank[0][:, 0:P], cnt_t[:, 0, :], ident[:, :])
                    pe.transpose(bank[0][:, P:NT], cnt_t[0:T1, 1, :], ident[0:T1, 0:T1]).then_inc(S("turned"), 1)

                @block.scalar
                def _(act):
                    act.wait_ge(S("rdeg_ready"), 1)
                    act.activation(nd_c[:, :], rdeg_c[:, :], ACT.Sqrt).then_inc(S("nd_ready"), 1)
            S.close()

        with ExitStack() as scratch:
            def tmp(name, shape, dt=F32):
                return scratch.enter_context(nc.sbuf_tensor(name, shape, dt))

            iota_i = tmp("iota_i", [P, LO], I32)
            iota_h = tmp("iota_h", [P, LO], F16)
            tile_no = tmp("tile_no", [P, NT], I32)
            lane_no = tmp("lane_no", [P, NT], I32)
            tile_w = tmp("tile_w", [P, NT])
            lane_w = tmp("lane_w", [P, NT])
            bits = tmp("bits", [P, 4, NT], I32)
            part = tmp("part", [P, 4, NT])
            dst_i = tmp("dst_i", [P, NT], I32)
            hot = [tmp(f"hot_{l}", [P, 3, 2 * P], BF16) for l in range(2)]
            low = [tmp(f"low_{l}", [P, 2, LO], BF16) for l in range(2)]
            place = [tmp(f"place_{h}", [P, LO]) for h in range(2)]
            empty = [tmp(f"empty_{h}", [P, LO]) for h in range(2)]
            tab = [tmp(f"tab_{h}", [P, LO, 2], I32) for h in range(2)]
            got = [tmp(f"got_{l}", [P, GT, 2], I32) for l in range(2)]
            idx4 = [tmp(f"idx4n_{l}", [P, GT], I32) for l in range(2)]
            node = tmp("node", [P, NT + 2 * GT, 2], I32)
            f0 = tmp("f0", [P, NT])
            w0_t = tmp("w0_t", [P, 2, P])
            hi_rows = (P, H1)
            with nc.Block() as block:
                @block.gpsimd
                def _(pool):
                    pool.iota(iota_i[:, :], pattern=[[1, LO]], base=0, channel_multiplier=0).then_inc(S("iota_ready"), 1)
                    pool.iota(tile_no[:, :], pattern=[[1, NT]], base=1, channel_multiplier=0).then_inc(S("iota_ready"), 1)
                    pool.iota(lane_no[:, :], pattern=[[0, NT]], base=0, channel_multiplier=1).then_inc(S("iota_ready"), 1)

                @block.vector
                def _(dve):
                    chain = Chain(dve, S("dve_step"))
                    dve.wait_ge(S("iota_ready"), 3)
                    dve.tensor_copy(iota_h[:, :], iota_i[:, :])
                    dve.tensor_tensor(tile_w[:, :], tile_no[:, :], rep_c[:, :], ALU.mult)
                    dve.tensor_tensor(lane_w[:, :], lane_no[:, :], rep_c[:, :], ALU.mult)
                    chain.step(dve.tensor_copy(dst_i[:, :], dst_c[:, :]))
                    chain.wait()
                    for n, i in ((0, src_idx[:, 0:NT]), (2, dst_i[:, :])):
                        dve.tensor_scalar(bits[:, n, :], i, 9, None, ALU.arith_shift_right)
                        chain.step(dve.tensor_scalar(bits[:, n + 1, :], i, LO - 1, None, ALU.bitwise_and))
                    chain.wait()
                    chain.step(dve.tensor_copy(part[:, :, :], bits[:, :, :]))
                    chain.step(dve.tensor_scalar(f0[:, :], dst_c[:, :], -float(ABSENT), None, ALU.add))
                    chain.wait()
                    chain.step(dve.tensor_tensor(f0[:, :], f0[:, :], rep_c[:, :], ALU.mult))
                    chain.wait()
                    dve.tensor_scalar(put_idx[:, 0:NT], f0[:, :], float(ABSENT), None, ALU.add)
                    chain.step(dve.tensor_scalar(dst_idx[:, 0:NT], dst_c[:, :], 0.0, None, ALU.max))
                    chain.wait()

                    def one_hot(i):
                        for l in range(2):
                            t = i * 2 + l
                            if not first(i):
                                dve.wait_ge(S("counted", l), i)
                            col = [part[:, n, bass.ds(t, 1)] for n in range(4)]
                            dve.tensor_scalar(hot[l][:, 0, :], iota_h[:, 0:2 * P], col[0], None, ALU.is_equal)
                            dve.tensor_scalar(low[l][:, 0, :], iota_h[:, :], col[1], None, ALU.is_equal)
                            dve.tensor_scalar(hot[l][:, 1, :], iota_h[:, 0:2 * P], col[2], tile_w[:, bass.ds(t, 1)],
                                              ALU.is_equal, ALU.mult)
                            dve.tensor_scalar(hot[l][:, 2, :], iota_h[:, 0:2 * P], col[2], lane_w[:, bass.ds(t, 1)],
                                              ALU.is_equal, ALU.mult)
                            dve.tensor_scalar(low[l][:, 1, :], iota_h[:, :], col[3], None, ALU.is_equal
                                              ).then_inc(S("hot_ready", l), 1)

                    one_hot(0)
                    with dve.Fori(1, NT // 2) as i:
                        one_hot(i)
                    dve.wait_ge(S("all_counted"), 1)
                    for h in range(2):
                        chain.step(dve.tensor_copy(place[h][:, :], bank[4 + h][:, :]))
                    chain.wait()
                    for h in range(2):
                        chain.step(dve.scalar_tensor_tensor(place[h][:, :], bank[2 + h][:, :], float(P), place[h][:, :],
                                                            ALU.mult, ALU.add))
                    chain.wait()
                    for h in range(2):
                        chain.step(dve.tensor_scalar(empty[h][:, :], place[h][:, :], 0.0, float(NONE_ROW + P),
                                                     ALU.is_equal, ALU.mult))
                    chain.wait()
                    for h in range(2):
                        dve.scalar_tensor_tensor(tab[h][:, :, 0], place[h][:, :], -float(P), empty[h][:, :],
                                                 ALU.add, ALU.add)
                        dve.tensor_copy(tab[h][:, :, 1], bank[h][:, :]).then_inc(S("tab_ready"), 1)

                    def stage(i, l):
                        dve.tensor_scalar(idx4[l][:, :], src_idx[:, bass.ds((i * 2 + l) * GT, GT)], 0, None, ALU.add
                                          ).then_inc(S("idx_ready", l), 1)

                    def keep(i, on):
                        for l in on:
                            dve.wait_ge(S("got_in", l), i * 64 + 64)
                            dve.tensor_scalar(node[:, bass.ds((i * 2 + l) * GT, GT), :], got[l][:, :, :], 0, None, ALU.add
                                              ).then_inc(S("kept", l), 1)
                            stage(i + 1, l)

                    for l in range(2):
                        stage(0, l)
                    with dve.Fori(0, NPAIR) as i:
                        keep(i, (0, 1))
                    if ODD:
                        keep(NPAIR, (0,))
                    dve.wait_ge(S("kept", 0), NG - NPAIR)
                    dve.wait_ge(S("kept", 1), NPAIR)
                    dve.tensor_copy(slot_idx[:, 0:NT], node[:, 0:NT, 0])
                    chain.step(dve.tensor_copy(f0[:, :], node[:, 0:NT, 1]))
                    chain.wait()
                    chain.step(dve.tensor_scalar(f0[:, :], f0[:, :], 1.0, None, ALU.max))
                    chain.wait()
                    dve.reciprocal(f0[:, :], f0[:, :]).then_inc(S("rout_ready"), 1)
                    dve.wait_ge(S("nsrc_ready"), 1)
                    dve.tensor_tensor(w0_c[:, :], nsrc_c[:, :], ew_c[:, :], ALU.mult).then_inc(S("w0_ready"), 1)
                    dve.wait_ge(S("w0_turned"), 1)
                    dve.tensor_copy(w0_t[:, 0, :], bank[6][:, 0:P])
                    dve.tensor_copy(w0_t[0:T1, 1, :], bank[6][0:T1, P:2 * P]).then_inc(S("w0_rows"), 1)

                @block.tensor
                def _(pe):
                    for b in range(6):
                        pe.matmul(bank[b][:, :], zero_bf[:, 0:P], zero_bf[:, :], start=True, stop=False,
                                  skip_group_check=True)

                    def count(i):
                        for l in range(2):
                            pe.wait_ge(S("hot_ready", l), i + 1)
                            for n in range(3):
                                for h in range(2):
                                    last = pe.matmul(bank[2 * n + h][:, :], hot[l][:, n, h * P:(h + 1) * P],
                                                     low[l][:, min(n, 1), :], start=False, stop=False,
                                                     skip_group_check=True)
                            last.then_inc(S("counted", l), 1)

                    with pe.Fori(0, NT // 2) as i:
                        count(i)
                    for b in range(6):
                        last = pe.matmul(bank[b][:, :], zero_bf[:, 0:P], zero_bf[:, :], start=False, stop=True,
                                         skip_group_check=True)
                    last.then_inc(S("all_counted"), 1)
                    pe.wait_ge(S("w0_ready"), 1)
                    pe.transpose(bank[6][:, 0:P], w0_c[:, 0:P], ident[:, :])
                    pe.transpose(bank[6][0:T1, P:2 * P], w0_c[:, P:NT], ident[:, :]).then_inc(S("w0_turned"), 1)

                @block.scalar
                def _(act):
                    act.wait_ge(S("rout_ready"), 1)
                    act.activation(nsrc_c[:, :], f0[:, :], ACT.Sqrt).then_inc(S("nsrc_ready"), 1)

                @block.sync
                def _(sp):
                    sp.wait_ge(S("tab_ready"), 2)
                    nt = node_tab.rearrange("(h o) c -> h (o c)", o=LO)
                    sp.dma_start(nt[0:P, :], tab[0][:, :, :].rearrange("p o c -> p (o c)")).then_inc(S("tab_out"), 16)
                    sp.dma_start(nt[P:NHI, :], tab[1][0:H1, :, :].rearrange("p o c -> p (o c)")).then_inc(S("tab_out"), 16)
                    sp.wait_ge(S("w0_rows"), 1)
                    sp.dma_start(w0_lin[0:P, :], w0_t[:, 0, :]).then_inc(S("w0_out"), 16)
                    sp.dma_start(w0_lin[P:NT, :], w0_t[0:T1, 1, :]).then_inc(S("w0_out"), 16)
                    sp.wait_ge(S("w0_out"), 32)

                @block.gpsimd
                def _(pool):
                    def fetch(i, on):
                        for l in on:
                            if not first(i):
                                pool.wait_ge(S("kept", l), i)
                            pool.wait_ge(S("idx_ready", l), i + 1)
                            pool.sem_inc(S("fetching", l), 1)
                            for j in range(GT):
                                pool.indirect_dma_start(
                                    out=got[l][:, j, :], out_offset=None, in_=node_tab,
                                    in_offset=bass.IndirectOffsetOnAxis(ap=idx4[l][:, j:j + 1], axis=0)
                                ).then_inc(S("got_in", l), 16)

                    pool.wait_ge(S("tab_out"), 32)
                    fetch(0, (0, 1))
                    with pool.Fori(1, NPAIR) as i:
                        fetch(i, (0, 1))
                    if ODD:
                        fetch(NPAIR, (0,))
            S.close()

        idx4 = lanes("idx4", [P, GT], I32)
        raw = lanes("raw", [P, GT, P])
        xin = lanes("xin", [P, GT, P])
        wr = lanes("wr", [P, GT, P])
        xnew = lanes("xnew", [P, GT, P])
        u = lanes("u", [P, GT, P])
        agg = lanes("agg", [P, GE])
        outr = lanes("outr", [P, GT, P])
        xT = lanes("xT", [P, GE])
        nT = lanes("nT", [P, GE])
        hT = lanes("hT", [P, 2, GE])
        wb = lanes("wb", [P, GE])
        st = lanes("st", [P, GT, 6])
        mv = lanes("mv", [P, 5, GT])
        sd = lanes("sd", [P, GT])
        rs = lanes("rs", [P, GT])
        nm = lanes("nm", [P, GT])
        psT, psZ, psX, psU = bank[0:2], bank[2:4], bank[4:6], bank[6:8]

        def tiles(ap):
            return ap.rearrange("p (t f) -> p t f", f=P)

        def over(r):
            return r[:, :].rearrange("p (o f) -> p o f", o=1).broadcast_to([P, GT, P])

        def ln_stats(dve, chain, l, src, tag):
            for j in range(GT):
                last = dve.bn_stats(st[l][:, j, :], src[:, j, :])
            chain.step(last)
            chain.wait()
            dve.tensor_tensor(mv[l][:, 0, :], st[l][:, :, 1], st[l][:, :, 4], ALU.add)
            dve.tensor_tensor(mv[l][:, 2, :], st[l][:, :, 2], st[l][:, :, 5], ALU.add)
            chain.step(dve.tensor_tensor(mv[l][:, 1, :], st[l][:, :, 1], st[l][:, :, 4], ALU.subtract))
            chain.wait()
            chain.step(dve.scalar_tensor_tensor(mv[l][:, 3, :], mv[l][:, 1, :], P / 4.0, mv[l][:, 1, :],
                                                ALU.mult, ALU.mult))
            chain.wait()
            dve.tensor_tensor(mv[l][:, 4, :], mv[l][:, 3, :], mv[l][:, 2, :], ALU.add
                              ).then_inc(S(f"{tag}_mean_var", l), 1)

        def ln_root(act, i, l, tag):
            act.wait_ge(S(f"{tag}_mean_var", l), i + 1)
            act.activation(sd[l][:, :], mv[l][:, 4, :], ACT.Sqrt, bias=eps_col[:, :], scale=1.0 / P
                           ).then_inc(S(f"{tag}_root", l), 1)

        def ln_scale(dve, chain, i, l, tag):
            dve.wait_ge(S(f"{tag}_root", l), i + 1)
            chain.step(dve.reciprocal(rs[l][:, :], sd[l][:, :]))
            chain.wait()
            dve.scalar_tensor_tensor(nm[l][:, :], mv[l][:, 0, :], -0.5, rs[l][:, :], ALU.mult, ALU.mult
                                     ).then_inc(S(f"{tag}_scale", l), 1)

        def ln_apply(act, i, l, src, dst, tag):
            act.wait_ge(S(f"{tag}_scale", l), i + 1)
            for j in range(GT):
                last = act.activation(dst[:, j, :], src[:, j, :], ACT.Identity, bias=nm[l][:, j:j + 1],
                                      scale=rs[l][:, j:j + 1])
            last.then_inc(S(f"{tag}_done", l), 1)

        def pairs(eng, body):
            body(0, (0, 1))
            with eng.Fori(1, NPAIR) as i:
                body(i, (0, 1))
            if ODD:
                body(NPAIR, (0,))

        def hop(table, idx, front, weight, post, dest, x_from=None, x_to=None, col=None, bias=None, none=None):
            bn = front == "bn_elu"
            ln = front in ("ln_bn", "ln_self", "ln_add")
            stats = post == "stats"

            def wr2(l):
                return tiles(nT[l][:, :])

            def xT_tiles(l):
                return tiles(xT[l][:, :])

            with nc.Block() as block:
                @block.gpsimd
                def _(pool):
                    def fetch(i, on):
                        for l in on:
                            if not first(i):
                                pool.wait_ge(S("raw_used", l), i)
                                if x_to is not None and front == "weight":
                                    pool.wait_ge(S("x_out", l), i * 16)
                            pool.wait_ge(S("idx_ready", l), i + 1)
                            pool.sem_inc(S("fetching", l), 1)
                            for j in range(GT):
                                pool.indirect_dma_start(
                                    out=raw[l][:, j, :], out_offset=None, in_=table,
                                    in_offset=bass.IndirectOffsetOnAxis(ap=idx4[l][:, j:j + 1], axis=0)
                                ).then_inc(S("rows_in", l), 16)
                    pairs(pool, fetch)

                @block.sync
                def _(sp):
                    def load(i, l):
                        g = i * 2 + l
                        if x_from is not None:
                            if not first(i):
                                sp.wait_ge(S("xin_used", l), i)
                            sp.dma_start(xin[l][:, :, :], rows(x_from, g)).then_inc(S("x_in", l), 16)
                        if bn:
                            if not first(i):
                                sp.wait_ge(S("message", l), i)
                            sp.dma_start(wb[l][:, :], w0_lin.rearrange("t e -> (t e)")[bass.ds(g * GE, GE)]
                                         .rearrange("(o e) -> o e", o=1).broadcast_to([P, GE])
                                         ).then_inc(S("w0_in", l), 16)

                    def store(i, l):
                        g = i * 2 + l
                        if x_to is not None:
                            if front == "weight":
                                sp.wait_ge(S("rows_in", l), i * 64 + 64)
                                sp.dma_start(rows(x_to, g), raw[l][:, :, :]).then_inc(S("x_out", l), 16)
                            else:
                                sp.wait_ge(S("x_done", l), i + 1)
                                sp.dma_start(rows(x_to, g), xnew[l][:, :, :]).then_inc(S("x_out", l), 16)
                        sp.wait_ge(S("out_ready", l), i + 1)
                        sp.dma_start(rows(dest, g), outr[l][:, :, :]).then_inc(S("out_out", l), 16)

                    def turn(i, on, ahead):
                        for l in ahead:
                            load(i + 1, l)
                        for l in on:
                            store(i, l)

                    if none is not None:
                        sp.dma_start(dest[NONE_ROW:NONE_ROW + 1, :], none).then_inc(S("none_out"), 16)
                    for l in range(2):
                        load(0, l)
                    turn(0, (0, 1), (0, 1))
                    with sp.Fori(1, NPAIR - 1) as i:
                        turn(i, (0, 1), (0, 1))
                    turn(NPAIR - 1, (0, 1), (0,) if ODD else ())
                    if ODD:
                        turn(NPAIR, (0,), ())
                    for l, n in ((0, NPAIR + ODD), (1, NPAIR)):
                        sp.wait_ge(S("out_out", l), 16 * n)
                        if x_to is not None:
                            sp.wait_ge(S("x_out", l), 16 * n)
                    if none is not None:
                        sp.wait_ge(S("none_out"), 16)

                @block.tensor
                def _(pe):
                    def turn_over(l, dst, src):
                        for j in range(GT):
                            last = pe.transpose(dst[l][:, j * P:(j + 1) * P], src[:, j, :], ident[:, :])
                        return last

                    def body(i, on):
                        if front in ("ln_self", "sage"):
                            for l in on:
                                pe.wait_ge(S("x_in", l), i * 16 + 16)
                                turn_over(l, psX, xin[l]).then_inc(S("xin_turned", l), 1)
                        if front == "ln_self":
                            for l in on:
                                pe.wait_ge(S("xT_ready", l), i + 1)
                                if not first(i):
                                    pe.wait_ge(S("psU_used", l), i)
                                for j in range(GT):
                                    last = pe.matmul(psU[l][:, j * P:(j + 1) * P], xT[l][:, j * P:(j + 1) * P], wsI[:, :],
                                                     start=True, stop=True)
                                last.then_inc(S("self_done", l), 1)
                        if front == "sage":
                            for l in on:
                                pe.wait_ge(S("xT_ready", l), i + 1)
                                pe.wait_ge(S("rows_in", l), i * 64 + 64)
                                turn_over(l, psX, raw[l]).then_inc(S("raw_used", l), 1)
                            for l in on:
                                pe.wait_ge(S("nT_ready", l), i + 1)
                                if not first(i):
                                    pe.wait_ge(S("hidden_used", l), i)
                                for c, ps in ((0, psU[l]), (1, psX[l])):
                                    pe.matmul(ps[:, :], ws1[:, c * P:(c + 1) * P], xT[l][:, :], start=True, stop=False)
                                    pe.matmul(ps[:, :], wn1[:, c * P:(c + 1) * P], nT[l][:, :], start=False, stop=True
                                              ).then_inc(S("hidden", l), 1)
                            for l in on:
                                pe.wait_ge(S("hT_ready", l), i * 2 + 2)
                                if not first(i):
                                    pe.wait_ge(S("summed", l), i)
                                for c in range(2):
                                    last = pe.matmul(psT[l][:, :], wn2[:, c, :], hT[l][:, c, :], start=(c == 0), stop=(c == 1))
                                last.then_inc(S("turned", l), 1)
                        else:
                            for l in on:
                                if front == "bn_elu":
                                    pe.wait_ge(S("rows_in", l), i * 64 + 64)
                                    if not first(i):
                                        pe.wait_ge(S("elu_in", l), i)
                                elif front in ("ln_bn", "ln_add"):
                                    pe.wait_ge(S("x_done", l), i + 1)
                                    if not first(i):
                                        pe.wait_ge(S("summed", l), i)
                                else:
                                    pe.wait_ge(S("scaled", l), i + 1)
                                    if not first(i):
                                        pe.wait_ge(S("summed", l), i)
                                src = {"bn_elu": raw, "ln_bn": xnew, "ln_add": xnew}.get(front, wr)[l]
                                turn_over(l, psT, src).then_inc(S("turned", l), 1)
                        for l in on:
                            pe.wait_ge(S("summed", l), i + 1)
                            if not first(i):
                                pe.wait_ge(S("psZ_used", l), i)
                            for j in range(GT):
                                last = pe.matmul(psZ[l][:, j * P:(j + 1) * P], agg[l][:, j * P:(j + 1) * P], weight,
                                                 start=True, stop=True)
                            last.then_inc(S("product", l), 1)
                        if stats:
                            for l in on:
                                pe.wait_ge(S("squared", l), i + 1)
                                for j in range(GT):
                                    pe.matmul(psX[0][:, 0:1], outr[l][:, j, :], ones_col[:, :], start=False, stop=False,
                                              skip_group_check=True)
                                for j in range(GT):
                                    last = pe.matmul(psX[1][:, 0:1], u[l][:, j, :], ones_col[:, :], start=False, stop=False,
                                                     skip_group_check=True)
                                last.then_inc(S("stats_read", l), 1)

                    if stats:
                        for b in range(2):
                            pe.matmul(psX[b][:, 0:1], zero_f[:, :], ones_col[:, :], start=True, stop=False,
                                      skip_group_check=True)
                    pairs(pe, body)
                    if stats:
                        for b in range(2):
                            last = pe.matmul(psX[b][:, 0:1], zero_f[:, :], ones_col[:, :], start=False, stop=True,
                                             skip_group_check=True)
                        last.then_inc(S("stats_done"), 1)

                @block.scalar
                def _(act):
                    def scale_rows(i, l, src, dst, by):
                        for j in range(GT):
                            last = act.activation(dst[:, j, :], src[:, j, :], ACT.Copy,
                                                  scale=by[:, bass.ds((i * 2 + l) * GT + j, 1)])
                        return last

                    def body(i, on):
                        if front in ("ln_self", "sage"):
                            for l in on:
                                act.wait_ge(S("xin_turned", l), i + 1)
                                act.activation(xT[l][:, :], psX[l][:, :], ACT.Copy).then_inc(S("xT_ready", l), 1)
                        if front == "sage":
                            for l in on:
                                act.wait_ge(S("raw_used", l), i + 1)
                                act.activation(nT[l][:, :], psX[l][:, :], ACT.Copy).then_inc(S("nT_ready", l), 1)
                            for l in on:
                                for c, ps in ((0, psU[l]), (1, psX[l])):
                                    act.wait_ge(S("hidden", l), i * 2 + c + 1)
                                    if c == 0 and not first(i):
                                        act.wait_ge(S("turned", l), i)
                                    last = act.activation(hT[l][:, c, :], ps[:, :], ACT.Relu, bias=b1_col[:, c:c + 1])
                                    last.then_inc(S("hT_ready", l), 1)
                                act.wait_ge(S("hT_ready", l), i * 2 + 2)
                                act.sem_inc(S("hidden_used", l), 1)
                        if front == "weight":
                            for l in on:
                                act.wait_ge(S("rows_in", l), i * 64 + 64)
                                if not first(i):
                                    act.wait_ge(S("turned", l), i)
                                scale_rows(i, l, raw[l], wr[l], col).then_inc(S("scaled", l), 1)
                        if ln:
                            for l in on:
                                ln_root(act, i, l, "ln")
                            for l in on:
                                if not first(i):
                                    if x_to is not None:
                                        act.wait_ge(S("x_out", l), i * 16)
                                    act.wait_ge(S("turned", l), i)
                                act.wait_ge(S("ln_scale", l), i + 1)
                                for j in range(GT):
                                    last = act.activation(xnew[l][:, j, :], u[l][:, j, :], ACT.Identity,
                                                          bias=nm[l][:, j:j + 1], scale=rs[l][:, j:j + 1])
                                last.then_inc(S("x_done", l), 1)
                            if front == "ln_self":
                                for l in on:
                                    act.wait_ge(S("x_done", l), i + 1)
                                    scale_rows(i, l, xnew[l], wr[l], nsrc_c).then_inc(S("scaled", l), 1)
                        if bn:
                            for l in on:
                                act.wait_ge(S("turned", l), i + 1)
                                if not first(i):
                                    act.wait_ge(S("message", l), i)
                                act.activation(nT[l][:, :], psT[l][:, :], ACT.Relu, bias=bn_c[:, :], scale=bn_a[:, :])
                                act.activation(hT[l][:, 0, :], psT[l][:, :], ACT.Relu, bias=bn_nc[:, :],
                                               scale=bn_na[:, :]).then_inc(S("elu_in", l), 1)
                            for l in on:
                                act.wait_ge(S("elu_in", l), i + 1)
                                act.activation(xT[l][:, :], hT[l][:, 0, :], ACT.Exp, scale=-1.0
                                               ).then_inc(S("exp_done", l), 1)
                        for l in on:
                            if post in ("stats", "scale"):
                                act.wait_ge(S("product", l), i + 1)
                                if not first(i):
                                    act.wait_ge(S("out_out", l), i * 16)
                                    if stats:
                                        act.wait_ge(S("stats_read", l), i)
                                last = scale_rows(i, l, tiles(psZ[l][:, :]), outr[l], ndrep_c if stats else rdeg_c)
                                last.then_inc(S("out_ready", l), 1)
                            if post == "gelu":
                                act.wait_ge(S("psZ_used", l), i + 1)
                                if not first(i):
                                    act.wait_ge(S("out_out", l), i * 16)
                                act.activation(outr[l][:, :, :], wr2(l), ACT.Gelu).then_inc(S("out_ready", l), 1)
                        if post == "ln_affine":
                            for l in on:
                                ln_root(act, i, l, "pn")
                            for l in on:
                                if not first(i):
                                    act.wait_ge(S("affine", l), i)
                                ln_apply(act, i, l, u[l], xT_tiles(l), "pn")
                    pairs(act, body)

                @block.vector
                def _(dve):
                    chain = Chain(dve, S("dve_step"))

                    def stage(i, l):
                        dve.tensor_scalar(idx4[l][:, :], idx[:, bass.ds((i * 2 + l) * GT, GT)], 0, None, ALU.add
                                          ).then_inc(S("idx_ready", l), 1)

                    def body(i, on):
                        chain.body(i)
                        for l in on:
                            dve.wait_ge(S("rows_in", l), i * 64 + 64)
                            stage(i + 1, l)
                        if ln:
                            for l in on:
                                if front == "ln_self":
                                    dve.wait_ge(S("self_done", l), i + 1)
                                    dve.tensor_tensor(u[l][:, :, :], tiles(psU[l][:, :]), raw[l][:, :, :], ALU.add
                                                      ).then_inc(S("psU_used", l), 1)
                                    dve.wait_ge(S("psU_used", l), i + 1)
                                    dve.sem_inc(S("raw_used", l), 1)
                                if front == "ln_add":
                                    dve.wait_ge(S("x_in", l), i * 16 + 16)
                                    dve.tensor_tensor(u[l][:, :, :], xin[l][:, :, :], raw[l][:, :, :], ALU.add
                                                      ).then_inc(S("raw_used", l), 1)
                                    dve.wait_ge(S("raw_used", l), i + 1)
                                if front == "ln_bn":
                                    dve.tensor_tensor(u[l][:, :, :], raw[l][:, :, :], over(a3_row), ALU.mult
                                                      ).then_inc(S("raw_used", l), 1)
                                    dve.wait_ge(S("raw_used", l), i + 1)
                                    dve.wait_ge(S("x_in", l), i * 16 + 16)
                                    chain.step(dve.tensor_tensor(u[l][:, :, :], u[l][:, :, :], xin[l][:, :, :], ALU.add))
                                    chain.wait()
                                    dve.tensor_tensor(u[l][:, :, :], u[l][:, :, :], over(c3_row), ALU.add
                                                      ).then_inc(S("u_ready", l), 1)
                                    dve.wait_ge(S("u_ready", l), i + 1)
                                ln_stats(dve, chain, l, u[l], "ln")
                                if front == "ln_add" or front == "ln_bn":
                                    dve.sem_inc(S("xin_used", l), 1)
                            for l in on:
                                ln_scale(dve, chain, i, l, "ln")
                        if front == "ln_self":
                            for l in on:
                                dve.wait_ge(S("xin_turned", l), i + 1)
                                dve.sem_inc(S("xin_used", l), 1)
                        if front == "sage":
                            for l in on:
                                dve.wait_ge(S("xin_turned", l), i + 1)
                                dve.sem_inc(S("xin_used", l), 1)
                        if front == "weight":
                            for l in on:
                                dve.wait_ge(S("scaled", l), i + 1)
                                dve.sem_inc(S("raw_used", l), 1)
                        for l in on:
                            dve.wait_ge(S("turned", l), i + 1)
                            src = psT[l][:, :]
                            if bn:
                                dve.sem_inc(S("raw_used", l), 1)
                                dve.wait_ge(S("exp_done", l), i + 1)
                                chain.step(dve.scalar_tensor_tensor(hT[l][:, 1, :], xT[l][:, :], -1.0, nT[l][:, :],
                                                                    ALU.add, ALU.add))
                                chain.wait()
                                dve.wait_ge(S("w0_in", l), i * 16 + 16)
                                dve.tensor_tensor(hT[l][:, 1, :], hT[l][:, 1, :], wb[l][:, :], ALU.mult).then_inc(S("message", l), 1)
                                dve.wait_ge(S("message", l), i + 1)
                                src = hT[l][:, 1, :]
                            if not first(i):
                                dve.wait_ge(S("product", l), i)
                            if l:
                                dve.wait_ge(S("summed", 0), i + 1)
                            elif not first(i):
                                dve.wait_ge(S("summed", 1), i)
                            start = 0.0 if first(i) and l == 0 else agg[1 - l][:, GE - 1:GE]
                            dve.tensor_tensor_scan(agg[l][:, :], same[:, bass.ds((i * 2 + l) * GE, GE)], src, start,
                                                   ALU.mult, ALU.add).then_inc(S("summed", l), 1)
                        for l in on:
                            g4 = (i * 2 + l) * GT
                            if post in ("stats", "scale"):
                                dve.wait_ge(S("out_ready", l), i + 1)
                                dve.sem_inc(S("psZ_used", l), 1)
                                if stats:
                                    if not first(i):
                                        dve.wait_ge(S("stats_read", l), i)
                                    dve.tensor_tensor(u[l][:, :, :], outr[l][:, :, :], outr[l][:, :, :], ALU.mult
                                                      ).then_inc(S("squared", l), 1)
                            else:
                                dve.wait_ge(S("product", l), i + 1)
                                to = {"bias": outr[l], "gelu": wr2(l), "ln_affine": u[l]}[post]
                                by = rdeg_c if post == "bias" else nd_c
                                if not first(i):
                                    if post == "bias":
                                        dve.wait_ge(S("out_out", l), i * 16)
                                    if post == "gelu":
                                        dve.wait_ge(S("out_ready", l), i)
                                for j in range(GT):
                                    last = dve.scalar_tensor_tensor(to[:, j, :], psZ[l][:, j * P:(j + 1) * P],
                                                                    by[:, bass.ds(g4 + j, 1)], bias[:, :],
                                                                    ALU.mult, ALU.add)
                                last.then_inc(S("out_ready" if post == "bias" else "psZ_used", l), 1)
                                if post == "bias":
                                    dve.wait_ge(S("out_ready", l), i + 1)
                                    dve.sem_inc(S("psZ_used", l), 1)
                                if post == "ln_affine":
                                    dve.wait_ge(S("psZ_used", l), i + 1)
                                    ln_stats(dve, chain, l, u[l], "pn")
                        if post == "ln_affine":
                            for l in on:
                                ln_scale(dve, chain, i, l, "pn")
                            for l in on:
                                dve.wait_ge(S("pn_done", l), i + 1)
                                if not first(i):
                                    dve.wait_ge(S("out_out", l), i * 16)
                                dve.tensor_tensor(outr[l][:, :, :], xT_tiles(l), over(row["L2_gnn_gamma"]), ALU.mult
                                                  ).then_inc(S("affine", l), 1)
                                dve.wait_ge(S("affine", l), i + 1)
                                dve.tensor_tensor(outr[l][:, :, :], outr[l][:, :, :], over(row["L2_gnn_beta"]), ALU.add
                                                  ).then_inc(S("out_ready", l), 1)

                    for l in range(2):
                        stage(0, l)
                    pairs(dve, body)
                    if stats:
                        bn_finish(dve, chain)
            S.close()

        def bn_finish(dve, chain):
            dve.wait_ge(S("stats_done"), 1)
            chain.step(dve.tensor_scalar(bn_t[:, 0:1], psX[0][:, 0:1], 1.0 / N, None, ALU.mult))
            chain.step(dve.tensor_scalar(bn_t[:, 1:2], psX[1][:, 0:1], 1.0 / N, None, ALU.mult))
            chain.wait()
            chain.step(dve.tensor_tensor(bn_t[:, 2:3], bn_t[:, 0:1], bn_t[:, 0:1], ALU.mult))
            chain.wait()
            chain.step(dve.tensor_tensor(bn_t[:, 3:4], bn_t[:, 1:2], bn_t[:, 2:3], ALU.subtract))

        def bn_coefficients(rows_too):
            with nc.Block() as block:
                @block.scalar
                def _(act):
                    act.activation(bn_t[:, 4:5], bn_t[:, 3:4], ACT.Sqrt, bias=eps_col[:, :]).then_inc(S("bn_root"), 1)

                @block.vector
                def _(dve):
                    chain = Chain(dve, S("dve_step"))
                    dve.wait_ge(S("bn_root"), 1)
                    chain.step(dve.reciprocal(bn_t[:, 5:6], bn_t[:, 4:5]))
                    chain.wait()
                    chain.step(dve.tensor_tensor(bn_a[:, :], bn_t[:, 5:6], gam_col[:, :], ALU.mult))
                    chain.wait()
                    chain.step(dve.tensor_tensor(bn_t[:, 6:7], bn_a[:, :], bn_t[:, 0:1], ALU.mult))
                    chain.wait()
                    chain.step(dve.tensor_tensor(bn_c[:, :], bet_col[:, :], bn_t[:, 6:7], ALU.subtract))
                    dve.tensor_tensor(bn_nc[:, :], bn_t[:, 6:7], bet_col[:, :], ALU.subtract)
                    dve.tensor_scalar(bn_na[:, :], bn_a[:, :], -1.0, None, ALU.mult)
                    chain.wait()
                    if rows_too:
                        dve.tensor_scalar(diag[:, 0, :], ident[:, :], bn_a[:, :], None, ALU.mult)
                        dve.tensor_scalar(diag[:, 1, :], ident[:, :], bn_c[:, :], None, ALU.mult
                                          ).then_inc(S("diag_ready"), 1)
                        dve.wait_ge(S("bn_rows"), 1)
                        dve.tensor_copy(a3_row[:, :], psX[0][:, 0:P])
                        dve.tensor_copy(c3_row[:, :], psX[0][:, P:2 * P])

                @block.tensor
                def _(pe):
                    if rows_too:
                        pe.wait_ge(S("diag_ready"), 1)
                        pe.matmul(psX[0][:, 0:P], ones_mat[:, :], diag[:, 0, :], start=True, stop=True)
                        pe.matmul(psX[0][:, P:2 * P], ones_mat[:, :], diag[:, 1, :], start=True, stop=True
                                  ).then_inc(S("bn_rows"), 1)
            S.close()

        with nc.Block() as block:
            @block.scalar
            def _(act):
                for k, n in enumerate(("L2_gnn_b1", "L2_gnn_b2", "L2_gnn_b3")):
                    act.activation(none_rows[:, k, :], row[n][:, :], ACT.Gelu)
                ln_root(act, 0, 0, "c")
                act.wait_ge(S("c_scale", 0), 1)
                act.activation(none_rows[:, 3, :], row["L2_gnn_b4"][:, :], ACT.Identity, bias=nm[0][:, 0:1],
                               scale=rs[0][:, 0:1]).then_inc(S("c_done"), 1)

            @block.vector
            def _(dve):
                chain = Chain(dve, S("dve_step"))
                ln_stats(dve, chain, 0, over(row["L2_gnn_b4"]), "c")
                ln_scale(dve, chain, 0, 0, "c")
                dve.wait_ge(S("c_done"), 1)
                chain.step(dve.tensor_tensor(a2_row[:, :], none_rows[:, 3, :], row["L2_gnn_gamma"][:, :], ALU.mult))
                chain.wait()
                dve.tensor_tensor(a2_row[:, :], a2_row[:, :], row["L2_gnn_beta"][:, :], ALU.add)
        S.close()

        zero_row = zero_f[0:1, :]
        hop(A["x"], src_idx, "weight", w["L0_gnn_W1"][:, :], "stats", tabs["z1"], x_to=xs["x0"], col=w0_c, none=zero_row)
        bn_coefficients(False)
        hop(tabs["z1"], slot_idx, "bn_elu", w["L0_gnn_W2"][:, :], "stats", tabs["z2"], none=zero_row)
        bn_coefficients(False)
        hop(tabs["z2"], slot_idx, "bn_elu", w["L0_gnn_W3"][:, :], "stats", tabs["z3"], none=zero_row)
        bn_coefficients(True)
        hop(tabs["z3"], slot_idx, "ln_bn", wnT[:, :], "bias", tabs["a1"], x_from=xs["x0"], x_to=xs["x1"],
            bias=row["L1_gnn_b_self"], none=row["L1_gnn_b_self"][0:1, :])
        hop(tabs["a1"], slot_idx, "ln_self", w["L2_gnn_W1"][:, :], "gelu", tabs["g1"], x_from=xs["x1"], x_to=xs["x2"],
            bias=row["L2_gnn_b1"], none=none_rows[0:1, 0, :])
        hop(tabs["g1"], slot_idx, "weight", w["L2_gnn_W2"][:, :], "gelu", tabs["g2"], col=nsrc_c,
            bias=row["L2_gnn_b2"], none=none_rows[0:1, 1, :])
        hop(tabs["g2"], slot_idx, "weight", w["L2_gnn_W3"][:, :], "gelu", tabs["g3"], col=nsrc_c,
            bias=row["L2_gnn_b3"], none=none_rows[0:1, 2, :])
        hop(tabs["g3"], slot_idx, "weight", w["L2_gnn_W4"][:, :], "ln_affine", tabs["a2"], col=nsrc_c,
            bias=row["L2_gnn_b4"], none=a2_row[0:1, :])
        hop(tabs["a2"], slot_idx, "ln_add", ident[:, :], "scale", tabs["n1"], x_from=xs["x2"], x_to=xs["x3"],
            none=zero_row)
        hop(tabs["n1"], slot_idx, "sage", ident[:, :], "bias", tabs["a4"], x_from=xs["x3"],
            bias=row["L3_gnn_b2"])

        tz = lanes("tz", [P, GT, P])
        t1 = lanes("t1", [P, GT, P])
        t2 = lanes("t2", [P, GT, P])
        t4 = lanes("t4", [P, GT, P])
        put4 = lanes("put4", [P, GT], I32)

        def nodes(edges):
            n_groups = NG if edges else -(-N // GE)
            n_pair, odd = n_groups // 2, n_groups % 2
            xa, xc, xo, tn = xnew, wr, outr, agg

            def each(eng, body):
                body(0, (0, 1))
                with eng.Fori(1, n_pair - 1) as i:
                    body(i, (0, 1))
                body(n_pair - 1, (0, 1))
                if odd:
                    body(n_pair, (0,))

            def span(i, l):
                g = i * 2 + l
                if isinstance(g, int):
                    return bass.ds(min(g * GE, N - GE), GE)
                return bass.ds(g * GE, GE)

            with nc.Block() as block:
                @block.gpsimd
                def _(pool):
                    def load(i, on):
                        for l in on:
                            if not first(i):
                                pool.wait_ge(S("n1_done", l), i)
                            if edges:
                                pool.wait_ge(S("idx_ready", l), i + 1)
                                pool.sem_inc(S("fetching", l), 1)
                                for j in range(GT):
                                    pool.indirect_dma_start(
                                        out=xin[l][:, j, :], out_offset=None, in_=A["x"],
                                        in_offset=bass.IndirectOffsetOnAxis(ap=idx4[l][:, j:j + 1], axis=0)
                                    ).then_inc(S("x_in", l), 16)

                    def put(i, on):
                        for l in on:
                            pool.wait_ge(S("n4_done", l), i + 1)
                            pool.wait_ge(S("put_ready", l), i + 1)
                            pool.sem_inc(S("fetching", l), 1)
                            for j in range(GT):
                                pool.indirect_dma_start(
                                    out=out, out_offset=bass.IndirectOffsetOnAxis(ap=put4[l][:, j:j + 1], axis=0),
                                    in_=xo[l][:, j, :], in_offset=None, bounds_check=N - 1, oob_is_err=False
                                ).then_inc(S("x_out", l), 16)

                    def both(i, on):
                        load(i, on)
                        put(i, on)
                    if edges:
                        each(pool, both)
                        pool.wait_ge(S("x_out", 0), 64 * (n_pair + odd))
                        pool.wait_ge(S("x_out", 1), 64 * n_pair)

                @block.sync
                def _(sp):
                    def load(i, on):
                        for l in on:
                            g = i * 2 + l
                            if not edges:
                                if not first(i):
                                    sp.wait_ge(S("n1_done", l), i)
                                sp.dma_start(xin[l][:, :, :], A["x"][span(i, l), :].rearrange("(p t) f -> p t f", t=GT)
                                             ).then_inc(S("x_in", l), 16)
                            else:
                                for tab, to, free in (("z3", tz, "n1_done"), ("a1", t1, "n2_done"), ("a2", t2, "n3_done"),
                                                      ("n1", None, "tn_turned"), ("a4", t4, "n4_done")):
                                    if not first(i):
                                        sp.wait_ge(S(free, l), i)
                                    d = to[l][:, :, :] if to else tiles(tn[l][:, :])
                                    sp.dma_start(d, rows(tabs[tab], g)).then_inc(S(f"{tab}_in", l), 16)
                    each(sp, load)

                @block.scalar
                def _(act):
                    def body(i, on):
                        for l in on:
                            ln_root(act, i, l, "n1")
                        for l in on:
                            ln_apply(act, i, l, u[l], xa[l], "n1")
                        for l in on:
                            act.wait_ge(S("xa_turned", l), i + 1)
                            act.activation(xT[l][:, :], psX[l][:, :], ACT.Copy).then_inc(S("xT_ready", l), 1)
                        for l in on:
                            ln_root(act, i, l, "n2")
                        for l in on:
                            ln_apply(act, i, l, u[l], xa[l], "n2")
                        for l in on:
                            ln_root(act, i, l, "n3")
                        for l in on:
                            ln_apply(act, i, l, u[l], xc[l], "n3")
                        for l in on:
                            act.wait_ge(S("xc_turned", l), i + 1)
                            act.activation(xT[l][:, :], psX[l][:, :], ACT.Copy).then_inc(S("xcT_ready", l), 1)
                        if edges:
                            for l in on:
                                act.wait_ge(S("tn_turned", l), i + 1)
                                act.activation(nT[l][:, :], psZ[l][:, :], ACT.Copy).then_inc(S("nT_ready", l), 1)
                        for l in on:
                            for c, ps in ((0, psU[l]), (1, psZ[l])):
                                act.wait_ge(S("hidden", l), i * 2 + c + 1)
                                act.activation(hT[l][:, c, :], ps[:, :], ACT.Relu, bias=b1_col[:, c:c + 1]
                                               ).then_inc(S("hT_ready", l), 1)
                        for l in on:
                            ln_root(act, i, l, "n4")
                        for l in on:
                            if not first(i):
                                act.wait_ge(S("x_out", l), i * (64 if edges else 16))
                            ln_apply(act, i, l, u[l], xo[l], "n4")
                        if not edges:
                            for l in on:
                                act.wait_ge(S("n4_done", l), i + 1)
                                if isinstance(i, int) and i * 2 + l == n_groups - 1:
                                    act.wait_ge(S("x_out", 1 - l), 16 * (i + l))
                                act.dma_start(out[span(i, l), :].rearrange("(p t) f -> p t f", t=GT), xo[l][:, :, :]
                                              ).then_inc(S("x_out", l), 16)
                    each(act, body)
                    if not edges:
                        act.wait_ge(S("x_out", 0), 16 * (n_pair + odd))
                        act.wait_ge(S("x_out", 1), 16 * n_pair)

                @block.vector
                def _(dve):
                    chain = Chain(dve, S("dve_step"))

                    def stage(i, l):
                        cols = bass.ds((i * 2 + l) * GT, GT)
                        dve.tensor_scalar(idx4[l][:, :], dst_idx[:, cols], 0, None, ALU.add).then_inc(S("idx_ready", l), 1)

                    def body(i, on):
                        chain.body(i)
                        for l in on:
                            dve.wait_ge(S("x_in", l), (i * 64 + 64) if edges else (i * 16 + 16))
                            if not first(i):
                                dve.wait_ge(S("n4_done", l), i)
                            if edges:
                                stage(i + 1, l)
                                dve.wait_ge(S("z3_in", l), i * 16 + 16)
                                chain.step(dve.tensor_tensor(u[l][:, :, :], tz[l][:, :, :], over(a3_row), ALU.mult))
                                chain.wait()
                                chain.step(dve.tensor_tensor(u[l][:, :, :], u[l][:, :, :], xin[l][:, :, :], ALU.add))
                                chain.wait()
                                chain.step(dve.tensor_tensor(u[l][:, :, :], u[l][:, :, :], over(c3_row), ALU.add))
                            else:
                                chain.step(dve.tensor_tensor(u[l][:, :, :], xin[l][:, :, :], over(c3_row), ALU.add))
                            chain.wait()
                            ln_stats(dve, chain, l, u[l], "n1")
                        for l in on:
                            ln_scale(dve, chain, i, l, "n1")
                        for l in on:
                            dve.wait_ge(S("self_done", l), i + 1)
                            if edges:
                                dve.wait_ge(S("a1_in", l), i * 16 + 16)
                            add = t1[l][:, :, :] if edges else over(row["L1_gnn_b_self"])
                            dve.tensor_tensor(u[l][:, :, :], tiles(psU[l][:, :]), add, ALU.add).then_inc(S("u2", l), 1)
                            dve.wait_ge(S("u2", l), i + 1)
                            ln_stats(dve, chain, l, u[l], "n2")
                        for l in on:
                            ln_scale(dve, chain, i, l, "n2")
                        for l in on:
                            dve.wait_ge(S("n2_done", l), i + 1)
                            if edges:
                                dve.wait_ge(S("a2_in", l), i * 16 + 16)
                            add = t2[l][:, :, :] if edges else over(a2_row)
                            chain.step(dve.tensor_tensor(u[l][:, :, :], xa[l][:, :, :], add, ALU.add))
                            chain.wait()
                            ln_stats(dve, chain, l, u[l], "n3")
                        for l in on:
                            ln_scale(dve, chain, i, l, "n3")
                        for l in on:
                            if edges:
                                dve.wait_ge(S("a4_in", l), i * 16 + 16)
                            dve.wait_ge(S("n3_done", l), i + 1)
                            add = t4[l][:, :, :] if edges else over(row["L3_gnn_b2"])
                            chain.step(dve.tensor_tensor(u[l][:, :, :], xc[l][:, :, :], add, ALU.add))
                            chain.wait()
                            dve.wait_ge(S("sage_done", l), i + 1)
                            dve.tensor_tensor(u[l][:, :, :], tiles(psT[l][:, :]), u[l][:, :, :], ALU.add
                                              ).then_inc(S("u4", l), 1)
                            dve.wait_ge(S("u4", l), i + 1)
                            ln_stats(dve, chain, l, u[l], "n4")
                        for l in on:
                            ln_scale(dve, chain, i, l, "n4")
                        if edges:
                            for l in on:
                                if not first(i):
                                    dve.wait_ge(S("x_out", l), i * 64)
                                dve.tensor_scalar(put4[l][:, :], put_idx[:, bass.ds((i * 2 + l) * GT, GT)], 0, None,
                                                  ALU.add).then_inc(S("put_ready", l), 1)

                    if edges:
                        for l in range(2):
                            stage(0, l)
                    each(dve, body)

                @block.tensor
                def _(pe):
                    def turn_over(dst, src):
                        for j in range(GT):
                            last = pe.transpose(dst[:, j * P:(j + 1) * P], src[:, j, :], ident[:, :])
                        return last

                    def body(i, on):
                        for l in on:
                            pe.wait_ge(S("n1_done", l), i + 1)
                            if not first(i):
                                pe.wait_ge(S("xcT_ready", l), i)
                            turn_over(psX[l], xa[l]).then_inc(S("xa_turned", l), 1)
                        for l in on:
                            pe.wait_ge(S("xT_ready", l), i + 1)
                            if not first(i):
                                pe.wait_ge(S("hT_ready", l), i * 2)
                            for j in range(GT):
                                last = pe.matmul(psU[l][:, j * P:(j + 1) * P], xT[l][:, j * P:(j + 1) * P], wsI[:, :],
                                                 start=True, stop=True)
                            last.then_inc(S("self_done", l), 1)
                        if edges:
                            for l in on:
                                pe.wait_ge(S("n1_in", l), i * 16 + 16)
                                turn_over(psZ[l], tiles(tn[l][:, :])).then_inc(S("tn_turned", l), 1)
                        for l in on:
                            pe.wait_ge(S("n3_done", l), i + 1)
                            turn_over(psX[l], xc[l]).then_inc(S("xc_turned", l), 1)
                        for l in on:
                            pe.wait_ge(S("xcT_ready", l), i + 1)
                            pe.wait_ge(S("u2", l), i + 1)
                            if edges:
                                pe.wait_ge(S("nT_ready", l), i + 1)
                            for c, ps in ((0, psU[l]), (1, psZ[l])):
                                last = pe.matmul(ps[:, :], ws1[:, c * P:(c + 1) * P], xT[l][:, :], start=True,
                                                 stop=not edges)
                                if edges:
                                    last = pe.matmul(ps[:, :], wn1[:, c * P:(c + 1) * P], nT[l][:, :], start=False,
                                                     stop=True)
                                last.then_inc(S("hidden", l), 1)
                        for l in on:
                            pe.wait_ge(S("hT_ready", l), i * 2 + 2)
                            if not first(i):
                                pe.wait_ge(S("u4", l), i)
                            for j in range(GT):
                                for c in range(2):
                                    last = pe.matmul(psT[l][:, j * P:(j + 1) * P], hT[l][:, c, j * P:(j + 1) * P],
                                                     ws2[:, c, :], start=(c == 0), stop=(c == 1))
                            last.then_inc(S("sage_done", l), 1)
                    each(pe, body)
            S.close()

        nodes(False)
        nodes(True)


def kernel(**inputs):
    import numpy as _np
    import concourse.bacc as _bacc
    from concourse import mybir as _mybir
    from concourse.bass_utils import run_bass_kernel_spmd as _run

    nc = _bacc.Bacc("TRN2", target_bir_lowering=False, num_devices=1)
    arrays, aps = {}, {}
    for name, value in inputs.items():
        a = _np.ascontiguousarray(value)
        arrays[f"in_{name}_dram"] = a
        aps[name] = nc.dram_tensor(f"in_{name}_dram", a.shape, _mybir.dt.from_np(a.dtype), kind="ExternalInput").ap()
    y = nc.dram_tensor("out_0_dram", inputs["x"].shape, _mybir.dt.float32, kind="ExternalOutput").ap()
    gnn_stack(nc, aps, y)
    r = _run(nc, [arrays], core_ids=[0])
    return r.results[0]["out_0_dram"]
```

```python
from contextlib import ExitStack

import concourse.bass as bass
from concourse import mybir

F32 = mybir.dt.float32
I32 = mybir.dt.int32
BF16 = mybir.dt.bfloat16
F16 = mybir.dt.float16
ALU = mybir.AluOpType
ACT = mybir.ActivationFunctionType

P = 128
GT = 4
GE = GT * P
UT = 2 * GT
UE = UT * P
EPS = 1e-5
LO = 512
ABSENT = 1 << 20


class Signals:

    def __init__(self, nc):
        self.nc, self.sems, self.stage = nc, {}, 0

    def __call__(self, name, lane=0):
        key = f"{name}{lane}"
        if key not in self.sems:
            self.sems[key] = self.nc.alloc_semaphore(f"{key}_stage{self.stage}")
        return self.sems[key]

    def close(self):
        self.nc.clear_and_free_semaphores(list(self.sems.values()))
        self.nc.all_engine_barrier()
        self.sems = {}
        self.stage += 1

    def named(self, prefix):
        return lambda name, lane=0: self(f"{prefix}_{name}_", lane)


class Chain:

    def __init__(self, eng, sem):
        self.eng, self.sem, self.per_body, self.base, self.k = eng, sem, 0, 0, 0

    def body(self, i):
        if isinstance(i, int) and i == 0:
            self.k = 0
            self.base = 0
        else:
            if not self.per_body:
                self.per_body = self.k
            self.base, self.k = i * self.per_body, 0

    def step(self, ins):
        self.k += 1
        return ins.then_inc(self.sem, 1)

    def wait(self):
        self.eng.wait_ge(self.sem, self.base + self.k)


def first(i):
    return isinstance(i, int) and i == 0


class Unit:

    def __init__(self, half, parity):
        self.half, self.parity = half, parity
        self.no = half * 2 + parity
        self.done = half * 2 + (parity + 1)

    def back(self, by, origin=0):
        off = self.parity - by - origin
        return Unit(self.half + off // 2, off % 2)


def need(eng, sem, value):
    if isinstance(value, int) and value <= 0:
        return
    eng.wait_ge(sem, value)


def hold(eng, Q):
    eng.sem_inc(Q("turns_of_" + str(eng.engine.name)), 1)


def run(eng, n_bodies, steps):
    def states(b):
        out = []
        for _, skew, origin, units in steps:
            u = b - skew - origin
            out.append("off" if u < 0 or u >= units else "steady" if 3 <= u < units - 1 else b)
        return out

    def body(half, parity):
        b = half * 2 + parity if isinstance(half, int) else None
        for step, skew, origin, units in steps:
            if b is not None:
                on = 0 <= b - skew - origin < units
            else:
                on = 0 <= loop[0] * 2 + parity - skew - origin < units
            if on:
                step(Unit(half, parity).back(skew, origin))

    same = [h for h in range(n_bodies // 2)
            if all(x != y or x == "off" or x == "steady"
                   for x, y in zip(states(2 * h), states(2 * h + 1)))
            and not any(isinstance(x, int) for x in states(2 * h) + states(2 * h + 1))]
    loop, best = (0, 0), (0, 0)
    for h in same:
        e = h
        while e in same and states(2 * e) == states(2 * h) and states(2 * e + 1) == states(2 * h):
            e += 1
        if e - h > best[1] - best[0]:
            best = (h, e)
    loop = best
    if loop[1] - loop[0] < 2:
        loop = (n_bodies, n_bodies)
    for b in range(min(loop[0] * 2, n_bodies)):
        body(b // 2, b % 2)
    if loop[0] < n_bodies:
        with eng.Fori(loop[0], loop[1]) as half:
            body(half, 0)
            body(half, 1)
        for b in range(loop[1] * 2, n_bodies):
            body(b // 2, b % 2)


def gnn_stack(nc, A, out):
    N, E = A["x"].shape[0], A["src"].shape[0]
    NT = -(-E // P)
    NG = -(-NT // GT)
    EP = NG * GE
    assert NT == NG * GT
    NPAIR, ODD = NG // 2, NG % 2
    NU = -(-NT // UT)
    NUN = -(-N // UE)
    FIRST_NODES = N - (NUN - 1) * UE
    TAIL = E - (NT - 1) * P
    T1 = NT - P
    NHI = -(-N // LO)
    H1 = NHI - P
    NONE_ROW = EP
    CH = EP // 7
    assert CH * 7 == EP
    IDXW = NT + 2 * UT

    def dram(name, shape, dt):
        return nc.dram_tensor(name, shape, dt, kind="Internal").ap()

    dst_lin = dram("dst_lin", [EP + 1, 1], I32)
    cnt_lin = dram("cnt_lin", [NT, P], F32)
    w0_lin = dram("w0_lin", [NT, P], F32)
    node_tab = dram("node_tab", [NHI * LO, 2], I32)
    tabs = {n: dram(f"tab_{n}", [EP + 1, P], F32)
            for n in ("z1", "z2", "z3", "a1", "g1", "g2", "g3", "a2", "n1", "a4")}
    xs = {n: dram(f"xs_{n}", [EP, P], F32) for n in ("x0", "x1", "x2", "x3")}
    x0d = dram("x0d", [EP, P], F32)

    def tiles_in(u):
        return NT - (NU - 1) * UT if isinstance(u.no, int) and u.no == NU - 1 else UT

    def rows(ap, u):
        return ap[bass.ds(u.no * UE, tiles_in(u) * P), :].rearrange("(t p) f -> p t f", p=P)

    def rows_in_value(u):
        return u.half * (16 * UT) + 16 * tiles_in(u)

    with ExitStack() as ctx:
        def sb(name, shape, dt=F32):
            return ctx.enter_context(nc.sbuf_tensor(name, shape, dt))

        def lanes(name, shape, dt=F32):
            return [sb(f"{name}_{l}", shape, dt) for l in range(2)]

        wide = [ctx.enter_context(nc.psum_tensor(f"wide{b}", [P, 1024], F32)) for b in range(4)]
        bank = [wide[b // 2][:, (b % 2) * 512:(b % 2 + 1) * 512] for b in range(8)]

        ident = sb("ident", [P, P])
        ones_col = sb("ones_col", [P, 1])
        ones_mat = sb("ones_mat", [P, P])
        eps_col = sb("eps_col", [P, 1])
        zero_bf = sb("zero_bf", [P, LO], BF16)
        zero_f = sb("zero_f", [P, P])
        w = {n: sb(f"w_{n}", [P, P]) for n in
             ("L0_gnn_W1", "L0_gnn_W2", "L0_gnn_W3", "L2_gnn_W1", "L2_gnn_W2", "L2_gnn_W3", "L2_gnn_W4",
              "L1_gnn_w_neigh", "L1_gnn_w_self")}
        wnT = sb("wnT", [P, P])
        wsI = sb("wsI", [P, P])
        wsC = sb("wsC", [P, P])
        w4C = sb("w4C", [P, P])
        b4C = sb("b4C", [P, P])
        mean_mat = sb("mean_mat", [P, P])
        row_mean = sb("row_mean", [P, 2])
        ws1 = sb("ws1", [P, 2 * P])
        wn1 = sb("wn1", [P, 2 * P])
        ws2 = sb("ws2", [P, 2, P])
        wn2 = sb("wn2", [P, 2, P])
        row = {n: sb(f"r_{n}", [P, P]) for n in
               ("L1_gnn_b_self", "L2_gnn_b1", "L2_gnn_b2", "L2_gnn_b3", "L2_gnn_b4", "L2_gnn_gamma", "L2_gnn_beta",
                "L3_gnn_b2")}
        a3_row = sb("a3_row", [P, P])
        c3_row = sb("c3_row", [P, P])
        a2_row = sb("a2_row", [P, P])
        none_rows = sb("none_rows", [P, 4, P])
        gam_col = sb("gam_col", [P, 1])
        bet_col = sb("bet_col", [P, 1])
        b1_col = sb("b1_col", [P, 2])
        bn_a = sb("bn_a", [P, 1])
        bn_c = sb("bn_c", [P, 1])
        bn_na = sb("bn_na", [P, 1])
        bn_nc = sb("bn_nc", [P, 1])
        bn_t = sb("bn_t", [P, 8])
        raw = [sb(f"raw_{p}", [P, UT, P]) for p in range(2)]
        diag = sb("diag", [P, 2, P])

        same = sb("same", [P, EP], BF16)
        src_idx = sb("src_idx", [P, IDXW], I32)
        slot_idx = sb("slot_idx", [P, IDXW], I32)
        dst_idx = sb("dst_idx", [P, IDXW], I32)
        put_idx = sb("put_idx", [P, IDXW], I32)
        w0_c = sb("w0_c", [P, NT])
        nsrc_c = sb("nsrc_c", [P, NT])
        rdeg_c = sb("rdeg_c", [P, NT])
        nd_c = sb("nd_c", [P, NT])
        ndrep_c = sb("ndrep_c", [P, NT])
        rep_c = sb("rep_c", [P, NT])
        dst_c = sb("dst_c", [P, NT])
        ew_c = sb("ew_c", [P, NT])

        S = Signals(nc)

        with ExitStack() as scratch:
            def tmp(name, shape, dt=F32):
                return scratch.enter_context(nc.sbuf_tensor(name, shape, dt))

            src_t = tmp("src_t", [P, 2, P], I32)
            dst_t = tmp("dst_t", [P, 2, P], I32)
            nxt_t = tmp("nxt_t", [P, 2, P], I32)
            edge_f = tmp("edge_f", [P, 4, 2, P])
            nxt_f = tmp("nxt_f", [P, 2, P])
            with nc.Block() as block:
                @block.sync
                def _(sp):
                    sp.wait_ge(S("cleared"), 4)
                    n0 = P * P
                    for t, a, off in ((src_t, A["src"], 0), (dst_t, A["dst"], 0), (nxt_t, A["dst"], 1),
                                      (edge_f[:, 3], A["edge_weight"], 0)):
                        full = (T1 - 1) * P
                        sp.dma_start(t[:, 0, :], a[off:off + n0].rearrange("(t e) -> t e", e=P)
                                     ).then_inc(S("edges_in"), 16)
                        sp.dma_start(t[0:T1 - 1, 1, :], a[off + n0:off + n0 + full].rearrange("(t e) -> t e", e=P)
                                     ).then_inc(S("edges_in"), 16)
                        sp.dma_start(t[T1 - 1:T1, 1, 0:TAIL - off], a[off + n0 + full:E].rearrange("(t e) -> t e", t=1)
                                     ).then_inc(S("edges_in"), 16)
                    sp.wait_ge(S("edges_in"), 12 * 16)
                    body = dst_lin[1:EP + 1, :].rearrange("(t e) o -> t (e o)", e=P)
                    sp.dma_start(body[0:P, :], dst_t[:, 0, :]).then_inc(S("dst_out"), 16)
                    sp.dma_start(body[P:NT, :], dst_t[0:T1, 1, :]).then_inc(S("dst_out"), 16)
                    sp.dma_start(dst_lin[0:1, :], dst_t[T1:T1 + 1, 1, 0:1]).then_inc(S("dst_out"), 16)
                    sp.wait_ge(S("dst_out"), 48)

                @block.scalar
                def _(act):
                    for n in w:
                        act.dma_start(w[n][:, :], A[n]).then_inc(S("weights_in"), 16)
                    act.dma_start(ws1[:, :], A["L3_gnn_w_self1"]).then_inc(S("weights_in"), 16)
                    act.dma_start(wn1[:, :], A["L3_gnn_w_neigh1"]).then_inc(S("weights_in"), 16)
                    act.dma_start(ws2[:, :, :], A["L3_gnn_w_self2"].rearrange("(c p) f -> p c f", p=P)
                                  ).then_inc(S("weights_in"), 16)
                    act.dma_start(wn2[:, :, :], A["L3_gnn_w_neigh2"].rearrange("(c p) f -> p c f", p=P)
                                  ).then_inc(S("weights_in"), 16)
                    for n in row:
                        act.dma_start(row[n][:, :], A[n].rearrange("(o f) -> o f", o=1).broadcast_to([P, P])
                                      ).then_inc(S("weights_in"), 16)
                    act.dma_start(gam_col[:, :], A["L0_gnn_gamma"].rearrange("(p o) -> p o", o=1)
                                  ).then_inc(S("weights_in"), 16)
                    act.dma_start(bet_col[:, :], A["L0_gnn_beta"].rearrange("(p o) -> p o", o=1)
                                  ).then_inc(S("weights_in"), 16)
                    for c in range(2):
                        act.dma_start(b1_col[:, c:c + 1], A["L3_gnn_b1"][c * P:(c + 1) * P].rearrange("(p o) -> p o", o=1)
                                      ).then_inc(S("weights_in"), 16)
                    n_in = (len(w) + 4 + len(row) + 4) * 16
                    act.wait_ge(S("weights_in"), n_in)
                    act.sem_inc(S("weights_ready"), 1)

                @block.gpsimd
                def _(pool):
                    pool.memset(src_t[:, :, :], 0).then_inc(S("cleared"), 1)
                    pool.memset(dst_t[:, :, :], -1).then_inc(S("cleared"), 1)
                    pool.memset(nxt_t[:, :, :], -1).then_inc(S("cleared"), 1)
                    pool.memset(edge_f[:, 3], 0.0).then_inc(S("cleared"), 1)
                    pool.memset(ident[:, :], 0.0).then_inc(S("ident_zero"), 1)
                    pool.wait_ge(S("ident_zero"), 1)
                    pool.affine_select(out=ident[:, :], in_=ident[:, :], compare_op=ALU.not_equal, fill=1.0, base=0,
                                       pattern=[[-1, P]], channel_multiplier=1).then_inc(S("ident_ready"), 1)

                @block.vector
                def _(dve):
                    dve.memset(ones_col[:, :], 1.0)
                    dve.memset(ones_mat[:, :], 1.0)
                    dve.memset(mean_mat[:, :], 1.0 / P).then_inc(S("mean_mat_ready"), 1)
                    dve.memset(eps_col[:, :], EPS)
                    dve.memset(zero_f[:, :], 0.0)
                    dve.memset(zero_bf[:, :], 0.0)
                    dve.memset(src_idx[:, :], 0).then_inc(S("idx_zero"), 1)
                    dve.memset(slot_idx[:, :], 0)
                    dve.memset(dst_idx[:, :], 0)
                    dve.memset(put_idx[:, :], 0).then_inc(S("idx_zero"), 1)
                    dve.wait_ge(S("edges_in"), 12 * 16)
                    dve.tensor_copy(edge_f[:, 0], src_t[:, :, :])
                    dve.tensor_copy(edge_f[:, 1], dst_t[:, :, :]).then_inc(S("as_float"), 1)
                    dve.tensor_copy(nxt_f[:, :, :], nxt_t[:, :, :]).then_inc(S("as_float"), 1)
                    dve.wait_ge(S("as_float"), 2)
                    dve.tensor_tensor(edge_f[:, 2], edge_f[:, 1], nxt_f[:, :, :], ALU.not_equal
                                      ).then_inc(S("edges_float"), 1)
                    dve.wait_ge(S("turned"), 1)
                    dve.wait_ge(S("idx_zero"), 2)
                    dve.tensor_copy(src_idx[:, 0:NT], bank[0][:, 0:NT])
                    dve.tensor_copy(dst_c[:, :], bank[1][:, 0:NT])
                    dve.tensor_copy(rep_c[:, :], bank[2][:, 0:NT])
                    dve.tensor_copy(ew_c[:, :], bank[3][:, 0:NT])
                    dve.tensor_copy(wnT[:, :], bank[4][:, 0:P])
                    dve.tensor_tensor(wsI[:, :], bank[4][:, P:2 * P], ident[:, :], ALU.add
                                      ).then_inc(S("wsI_ready"), 1)
                    dve.wait_ge(S("weights_ready"), 1)
                    dve.tensor_reduce(row_mean[:, 0:1], w["L2_gnn_W4"][:, :], mybir.AxisListType.X, ALU.add)
                    dve.tensor_reduce(row_mean[:, 1:2], row["L2_gnn_b4"][:, :], mybir.AxisListType.X, ALU.add
                                      ).then_inc(S("sums_ready"), 1)
                    dve.wait_ge(S("sums_ready"), 1)
                    dve.tensor_scalar(row_mean[:, :], row_mean[:, :], 1.0 / P, None, ALU.mult
                                      ).then_inc(S("sums_ready"), 1)
                    dve.wait_ge(S("sums_ready"), 2)
                    dve.tensor_scalar(w4C[:, :], w["L2_gnn_W4"][:, :], row_mean[:, 0:1], None, ALU.subtract)
                    dve.tensor_scalar(b4C[:, :], row["L2_gnn_b4"][:, :], row_mean[:, 1:2], None, ALU.subtract)
                    dve.wait_ge(S("col_means"), 1)
                    dve.tensor_tensor(wsC[:, :], wsI[:, :], bank[5][:, 0:P], ALU.subtract)

                @block.tensor
                def _(pe):
                    pe.wait_ge(S("ident_ready"), 1)
                    pe.wait_ge(S("weights_ready"), 1)
                    pe.transpose(bank[4][:, 0:P], w["L1_gnn_w_neigh"][:, :], ident[:, :])
                    pe.transpose(bank[4][:, P:2 * P], w["L1_gnn_w_self"][:, :], ident[:, :])
                    pe.wait_ge(S("edges_float"), 1)
                    for n in range(4):
                        pe.transpose(bank[n][:, 0:P], edge_f[:, n, 0, :], ident[:, :])
                        last = pe.transpose(bank[n][:, P:NT], edge_f[0:T1, n, 1, :], ident[0:T1, 0:T1])
                    last.then_inc(S("turned"), 1)
                    pe.wait_ge(S("mean_mat_ready"), 1)
                    pe.wait_ge(S("wsI_ready"), 1)
                    pe.matmul(bank[5][:, 0:P], mean_mat[:, :], wsI[:, :], start=True, stop=True
                              ).then_inc(S("col_means"), 1)
            S.close()

        with ExitStack() as scratch:
            def tmp(name, shape, dt=F32):
                return scratch.enter_context(nc.sbuf_tensor(name, shape, dt))

            chunk = [tmp(f"chunk_{l}", [P, CH + 1], I32) for l in range(2)]
            ones_row = tmp("ones_row", [1, CH])
            cnt = [tmp(f"cnt_{l}", [1, CH]) for l in range(2)]
            cnt_t = tmp("cnt_t", [P, 2, P])
            with nc.Block() as block:
                @block.sync
                def _(sp):
                    def load(c):
                        l = c % 2
                        if c >= 2:
                            sp.wait_ge(S("mask_ready"), c - 1)
                        sp.dma_start(chunk[l][:, :], dst_lin[c * CH:(c + 1) * CH + 1, :].rearrange("e o -> o e")
                                     .broadcast_to([P, CH + 1])).then_inc(S("chunk_in", l), 16)

                    load(0)
                    load(1)
                    for c in range(7):
                        sp.wait_ge(S("count_ready"), c + 1)
                        sp.dma_start(cnt_lin.rearrange("t e -> (t e)")[c * CH:(c + 1) * CH].rearrange("(o e) -> o e", o=1),
                                     cnt[c % 2][:, :]).then_inc(S("count_out", c % 2), 16)
                        if c + 2 < 7:
                            load(c + 2)
                    sp.wait_ge(S("count_out", 0), 4 * 16)
                    sp.wait_ge(S("count_out", 1), 3 * 16)
                    sp.dma_start(cnt_t[:, 0, :], cnt_lin[0:P, :]).then_inc(S("count_in"), 16)
                    sp.dma_start(cnt_t[0:T1, 1, :], cnt_lin[P:NT, :]).then_inc(S("count_in"), 16)

                @block.vector
                def _(dve):
                    dve.memset(ones_row[:, :], 1.0)
                    for c in range(7):
                        l = c % 2
                        part = slice(c * CH, (c + 1) * CH)
                        dve.wait_ge(S("chunk_in", l), 16 * (c // 2 + 1))
                        dve.tensor_tensor(same[:, part], chunk[l][:, 1:CH + 1], chunk[l][:, 0:CH], ALU.is_equal
                                          ).then_inc(S("mask_ready"), 1)
                        dve.wait_ge(S("mask_ready"), c + 1)
                        if c:
                            dve.wait_ge(S("count_ready"), c)
                        if c >= 2:
                            dve.wait_ge(S("count_out", l), 16 * (c // 2))
                        dve.tensor_tensor_scan(cnt[l][:, :], same[0:1, part], ones_row[:, :],
                                               cnt[1 - l][:, CH - 1:CH] if c else 0.0, ALU.mult, ALU.add
                                               ).then_inc(S("count_ready"), 1)
                    dve.wait_ge(S("turned"), 1)
                    dve.reciprocal(rdeg_c[:, :], bank[0][:, 0:NT]).then_inc(S("rdeg_ready"), 1)
                    dve.wait_ge(S("nd_ready"), 1)
                    dve.tensor_tensor(ndrep_c[:, :], nd_c[:, :], rep_c[:, :], ALU.mult)

                @block.tensor
                def _(pe):
                    pe.wait_ge(S("count_in"), 32)
                    pe.transpose(bank[0][:, 0:P], cnt_t[:, 0, :], ident[:, :])
                    pe.transpose(bank[0][:, P:NT], cnt_t[0:T1, 1, :], ident[0:T1, 0:T1]).then_inc(S("turned"), 1)

                @block.scalar
                def _(act):
                    act.wait_ge(S("rdeg_ready"), 1)
                    act.activation(nd_c[:, :], rdeg_c[:, :], ACT.Sqrt).then_inc(S("nd_ready"), 1)
            S.close()

        with ExitStack() as scratch:
            def tmp(name, shape, dt=F32):
                return scratch.enter_context(nc.sbuf_tensor(name, shape, dt))

            iota_i = tmp("iota_i", [P, LO], I32)
            iota_h = tmp("iota_h", [P, LO], F16)
            tile_no = tmp("tile_no", [P, NT], I32)
            lane_no = tmp("lane_no", [P, NT], I32)
            tile_w = tmp("tile_w", [P, NT])
            lane_w = tmp("lane_w", [P, NT])
            bits = tmp("bits", [P, 4, NT], I32)
            part = tmp("part", [P, 4, NT])
            dst_i = tmp("dst_i", [P, NT], I32)
            hot = [tmp(f"hot_{l}", [P, 3, 2 * P], BF16) for l in range(2)]
            low = [tmp(f"low_{l}", [P, 2, LO], BF16) for l in range(2)]
            place = [tmp(f"place_{h}", [P, LO]) for h in range(2)]
            empty = [tmp(f"empty_{h}", [P, LO]) for h in range(2)]
            tab = [tmp(f"tab_{h}", [P, LO, 2], I32) for h in range(2)]
            got = [tmp(f"got_{l}", [P, GT, 2], I32) for l in range(2)]
            idx4 = [tmp(f"idx4n_{l}", [P, GT], I32) for l in range(2)]
            idx8 = [tmp(f"idx8n_{p}", [P, UT], I32) for p in range(2)]
            node = tmp("node", [P, NT + 2 * GT, 2], I32)
            f0 = tmp("f0", [P, NT])
            w0_t = tmp("w0_t", [P, 2, P])
            hi_rows = (P, H1)
            with nc.Block() as block:
                @block.gpsimd
                def _(pool):
                    pool.iota(iota_i[:, :], pattern=[[1, LO]], base=0, channel_multiplier=0).then_inc(S("iota_ready"), 1)
                    pool.iota(tile_no[:, :], pattern=[[1, NT]], base=1, channel_multiplier=0).then_inc(S("iota_ready"), 1)
                    pool.iota(lane_no[:, :], pattern=[[0, NT]], base=0, channel_multiplier=1).then_inc(S("iota_ready"), 1)

                @block.vector
                def _(dve):
                    chain = Chain(dve, S("dve_step"))
                    dve.wait_ge(S("iota_ready"), 3)
                    dve.tensor_copy(iota_h[:, :], iota_i[:, :])
                    dve.tensor_tensor(tile_w[:, :], tile_no[:, :], rep_c[:, :], ALU.mult)
                    dve.tensor_tensor(lane_w[:, :], lane_no[:, :], rep_c[:, :], ALU.mult)
                    chain.step(dve.tensor_copy(dst_i[:, :], dst_c[:, :]))
                    chain.wait()
                    for n, i in ((0, src_idx[:, 0:NT]), (2, dst_i[:, :])):
                        dve.tensor_scalar(bits[:, n, :], i, 9, None, ALU.arith_shift_right)
                        chain.step(dve.tensor_scalar(bits[:, n + 1, :], i, LO - 1, None, ALU.bitwise_and))
                    chain.wait()
                    chain.step(dve.tensor_copy(part[:, :, :], bits[:, :, :]))
                    chain.step(dve.tensor_scalar(f0[:, :], dst_c[:, :], -float(ABSENT), None, ALU.add))
                    chain.wait()
                    chain.step(dve.tensor_tensor(f0[:, :], f0[:, :], rep_c[:, :], ALU.mult))
                    chain.wait()
                    dve.tensor_scalar(put_idx[:, 0:NT], f0[:, :], float(ABSENT), None, ALU.add)
                    chain.step(dve.tensor_scalar(dst_idx[:, 0:NT], dst_c[:, :], 0.0, None, ALU.max))
                    chain.wait()

                    def one_hot(i):
                        for l in range(2):
                            t = i * 2 + l
                            if not first(i):
                                dve.wait_ge(S("counted", l), i)
                            col = [part[:, n, bass.ds(t, 1)] for n in range(4)]
                            dve.tensor_scalar(hot[l][:, 0, :], iota_h[:, 0:2 * P], col[0], None, ALU.is_equal)
                            dve.tensor_scalar(low[l][:, 0, :], iota_h[:, :], col[1], None, ALU.is_equal)
                            dve.tensor_scalar(hot[l][:, 1, :], iota_h[:, 0:2 * P], col[2], tile_w[:, bass.ds(t, 1)],
                                              ALU.is_equal, ALU.mult)
                            dve.tensor_scalar(hot[l][:, 2, :], iota_h[:, 0:2 * P], col[2], lane_w[:, bass.ds(t, 1)],
                                              ALU.is_equal, ALU.mult)
                            dve.tensor_scalar(low[l][:, 1, :], iota_h[:, :], col[3], None, ALU.is_equal
                                              ).then_inc(S("hot_ready", l), 1)

                    one_hot(0)
                    with dve.Fori(1, NT // 2) as i:
                        one_hot(i)
                    dve.wait_ge(S("all_counted"), 1)
                    for h in range(2):
                        chain.step(dve.tensor_copy(place[h][:, :], bank[4 + h][:, :]))
                    chain.wait()
                    for h in range(2):
                        chain.step(dve.scalar_tensor_tensor(place[h][:, :], bank[2 + h][:, :], float(P), place[h][:, :],
                                                            ALU.mult, ALU.add))
                    chain.wait()
                    for h in range(2):
                        chain.step(dve.tensor_scalar(empty[h][:, :], place[h][:, :], 0.0, float(NONE_ROW + P),
                                                     ALU.is_equal, ALU.mult))
                    chain.wait()
                    for h in range(2):
                        dve.scalar_tensor_tensor(tab[h][:, :, 0], place[h][:, :], -float(P), empty[h][:, :],
                                                 ALU.add, ALU.add)
                        dve.tensor_copy(tab[h][:, :, 1], bank[h][:, :]).then_inc(S("tab_ready"), 1)

                    def stage(i, l):
                        dve.tensor_scalar(idx4[l][:, :], src_idx[:, bass.ds((i * 2 + l) * GT, GT)], 0, None, ALU.add
                                          ).then_inc(S("idx_ready", l), 1)

                    def keep(i, on):
                        for l in on:
                            dve.wait_ge(S("got_in", l), i * 64 + 64)
                            dve.tensor_scalar(node[:, bass.ds((i * 2 + l) * GT, GT), :], got[l][:, :, :], 0, None, ALU.add
                                              ).then_inc(S("kept", l), 1)
                            stage(i + 1, l)

                    for l in range(2):
                        stage(0, l)
                    with dve.Fori(0, NPAIR) as i:
                        keep(i, (0, 1))
                    if ODD:
                        keep(NPAIR, (0,))
                    dve.wait_ge(S("kept", 0), NG - NPAIR)
                    dve.wait_ge(S("kept", 1), NPAIR)
                    dve.tensor_copy(slot_idx[:, 0:NT], node[:, 0:NT, 0])
                    chain.step(dve.tensor_copy(f0[:, :], node[:, 0:NT, 1]))
                    chain.wait()
                    chain.step(dve.tensor_scalar(f0[:, :], f0[:, :], 1.0, None, ALU.max))
                    chain.wait()
                    dve.reciprocal(f0[:, :], f0[:, :]).then_inc(S("rout_ready"), 1)
                    dve.wait_ge(S("nsrc_ready"), 1)
                    dve.tensor_tensor(w0_c[:, :], nsrc_c[:, :], ew_c[:, :], ALU.mult).then_inc(S("w0_ready"), 1)
                    dve.wait_ge(S("w0_turned"), 1)
                    dve.tensor_copy(w0_t[:, 0, :], bank[6][:, 0:P])
                    dve.tensor_copy(w0_t[0:T1, 1, :], bank[6][0:T1, P:2 * P]).then_inc(S("w0_rows"), 1)

                @block.tensor
                def _(pe):
                    for b in range(6):
                        pe.matmul(bank[b][:, :], zero_bf[:, 0:P], zero_bf[:, :], start=True, stop=False,
                                  skip_group_check=True)

                    def count(i):
                        for l in range(2):
                            pe.wait_ge(S("hot_ready", l), i + 1)
                            for n in range(3):
                                for h in range(2):
                                    last = pe.matmul(bank[2 * n + h][:, :], hot[l][:, n, h * P:(h + 1) * P],
                                                     low[l][:, min(n, 1), :], start=False, stop=False,
                                                     skip_group_check=True)
                            last.then_inc(S("counted", l), 1)

                    with pe.Fori(0, NT // 2) as i:
                        count(i)
                    for b in range(6):
                        last = pe.matmul(bank[b][:, :], zero_bf[:, 0:P], zero_bf[:, :], start=False, stop=True,
                                         skip_group_check=True)
                    last.then_inc(S("all_counted"), 1)
                    pe.wait_ge(S("w0_ready"), 1)
                    pe.transpose(bank[6][:, 0:P], w0_c[:, 0:P], ident[:, :])
                    pe.transpose(bank[6][0:T1, P:2 * P], w0_c[:, P:NT], ident[:, :]).then_inc(S("w0_turned"), 1)

                @block.scalar
                def _(act):
                    act.wait_ge(S("rout_ready"), 1)
                    act.activation(nsrc_c[:, :], f0[:, :], ACT.Sqrt).then_inc(S("nsrc_ready"), 1)

                @block.sync
                def _(sp):
                    def store_x(u):
                        sp.wait_ge(S("xs_in", u.parity), rows_in_value(u))
                        hold(sp, S)
                        sp.dma_start(rows(xs["x0"], u), raw[u.parity][:, 0:tiles_in(u), :]
                                     ).then_inc(S("xs_out", u.parity), 16)

                    run(sp, NU, ((store_x, 0, 0, NU),))
                    sp.wait_ge(S("xs_out", 0), 16 * (NU // 2 + NU % 2))
                    sp.wait_ge(S("xs_out", 1), 16 * (NU // 2))
                    sp.wait_ge(S("tab_ready"), 2)
                    nt = node_tab.rearrange("(h o) c -> h (o c)", o=LO)
                    sp.dma_start(nt[0:P, :], tab[0][:, :, :].rearrange("p o c -> p (o c)")).then_inc(S("tab_out"), 16)
                    sp.dma_start(nt[P:NHI, :], tab[1][0:H1, :, :].rearrange("p o c -> p (o c)")).then_inc(S("tab_out"), 16)
                    sp.wait_ge(S("w0_rows"), 1)
                    sp.dma_start(w0_lin[0:P, :], w0_t[:, 0, :]).then_inc(S("w0_out"), 16)
                    sp.dma_start(w0_lin[P:NT, :], w0_t[0:T1, 1, :]).then_inc(S("w0_out"), 16)
                    sp.wait_ge(S("w0_out"), 32)

                @block.gpsimd
                def _(pool):
                    def fetch(i, on):
                        for l in on:
                            if not first(i):
                                pool.wait_ge(S("kept", l), i)
                            pool.wait_ge(S("idx_ready", l), i + 1)
                            pool.sem_inc(S("fetching", l), 1)
                            for j in range(GT):
                                pool.indirect_dma_start(
                                    out=got[l][:, j, :], out_offset=None, in_=node_tab,
                                    in_offset=bass.IndirectOffsetOnAxis(ap=idx4[l][:, j:j + 1], axis=0)
                                ).then_inc(S("got_in", l), 16)

                    def index_x(u):
                        need(pool, S("xs_out", u.parity), u.half * 16)
                        pool.tensor_copy(idx8[u.parity][:, :], src_idx[:, bass.ds(u.no * UT, UT)]
                                         ).then_inc(S("xs_index"), 1)

                    def fetch_x(u):
                        pool.wait_ge(S("xs_index"), u.done)
                        pool.sem_inc(S("fetching_x"), 1)
                        for j in range(tiles_in(u)):
                            pool.indirect_dma_start(
                                out=raw[u.parity][:, j, :], out_offset=None, in_=A["x"],
                                in_offset=bass.IndirectOffsetOnAxis(ap=idx8[u.parity][:, j:j + 1], axis=0)
                            ).then_inc(S("xs_in", u.parity), 16)

                    run(pool, NU, ((index_x, 0, 0, NU), (fetch_x, 0, 0, NU)))
                    pool.wait_ge(S("tab_out"), 32)
                    fetch(0, (0, 1))
                    with pool.Fori(1, NPAIR) as i:
                        fetch(i, (0, 1))
                    if ODD:
                        fetch(NPAIR, (0,))
            S.close()

        def wide_sb(name, n=1):
            return [sb(f"{name}_{p}", [P, UT, P]) for p in range(n)] if n > 1 else sb(name, [P, UT, P])

        def flat(t, nt=UT):
            return t[:, 0:nt, :].rearrange("p t f -> p (t f)")

        def tiles(ps, nt=UT):
            return ps[:, 0:nt * P].rearrange("p (t f) -> p t f", f=P)

        def over(r, nt=UT):
            return r[:, :].rearrange("p (o f) -> p o f", o=1).broadcast_to([P, nt, P])

        psA, psB0, psB1, psH = wide

        idx8 = [sb(f"idx8_{p}", [P, UT], I32) for p in range(2)]
        put8 = [sb(f"put8_{p}", [P, UT], I32) for p in range(2)]
        xinh = wide_sb("xinh", 2)
        uh = wide_sb("uh")
        xnew = wide_sb("xnew")
        scaled = wide_sb("scaled")
        agg = wide_sb("agg", 2)
        outr = wide_sb("outr", 2)
        sq = wide_sb("sq")
        n_xin = wide_sb("n_xin")
        n_u0 = wide_sb("n_u0")
        n_xT = wide_sb("n_xT")
        n_u1 = wide_sb("n_u1")
        n_u2 = wide_sb("n_u2")
        n_x3 = wide_sb("n_x3")
        n_x3b = wide_sb("n_x3b")
        n_x3T = wide_sb("n_x3T")
        n_hT = [wide_sb("n_hT0"), wide_sb("n_hT1")]
        n_u3 = wide_sb("n_u3")
        n_out = wide_sb("n_out")

        class Norm:

            def __init__(self, name):
                self.name = name
                self.st = sb(f"{name}_st", [P, UT, 6])
                self.mv = sb(f"{name}_mv", [P, 5, UT])
                self.sd = sb(f"{name}_sd", [P, UT])
                self.rs = sb(f"{name}_rs", [P, UT])
                self.nm = sb(f"{name}_nm", [P, UT])

            def stats(self, dve, Q, u, src, nt=UT):
                st, mv = self.st, self.mv
                for j in range(nt):
                    last = dve.bn_stats(st[:, j, :], src[:, j, :])
                last.then_inc(Q(f"{self.name}_stats"), 1)
                dve.wait_ge(Q(f"{self.name}_stats"), u.done)
                dve.tensor_tensor(mv[:, 0, 0:nt], st[:, 0:nt, 1], st[:, 0:nt, 4], ALU.add)
                dve.tensor_tensor(mv[:, 1, 0:nt], st[:, 0:nt, 1], st[:, 0:nt, 4], ALU.subtract
                                  ).then_inc(Q(f"{self.name}_gap"), 1)
                dve.tensor_tensor(mv[:, 2, 0:nt], st[:, 0:nt, 2], st[:, 0:nt, 5], ALU.add)
                dve.wait_ge(Q(f"{self.name}_gap"), u.done)
                dve.scalar_tensor_tensor(mv[:, 3, 0:nt], mv[:, 1, 0:nt], P / 4.0, mv[:, 1, 0:nt], ALU.mult, ALU.mult
                                         ).then_inc(Q(f"{self.name}_gap2"), 1)
                dve.wait_ge(Q(f"{self.name}_gap2"), u.done)
                dve.tensor_tensor(mv[:, 4, 0:nt], mv[:, 3, 0:nt], mv[:, 2, 0:nt], ALU.add
                                  ).then_inc(Q(f"{self.name}_var"), 1)

            def root(self, act, Q, u, nt=UT):
                need(act, Q(f"{self.name}_scale"), u.done - 1)
                act.wait_ge(Q(f"{self.name}_var"), u.done)
                act.activation(self.sd[:, 0:nt], self.mv[:, 4, 0:nt], ACT.Sqrt, bias=eps_col[:, :], scale=1.0 / P
                               ).then_inc(Q(f"{self.name}_root"), 1)

            def scale(self, dve, Q, u, nt=UT, shift=True):
                dve.wait_ge(Q(f"{self.name}_root"), u.done)
                if not shift:
                    dve.reciprocal(self.rs[:, 0:nt], self.sd[:, 0:nt]).then_inc(Q(f"{self.name}_scale"), 1)
                    return
                dve.reciprocal(self.rs[:, 0:nt], self.sd[:, 0:nt]).then_inc(Q(f"{self.name}_rs"), 1)
                dve.wait_ge(Q(f"{self.name}_rs"), u.done)
                dve.scalar_tensor_tensor(self.nm[:, 0:nt], self.mv[:, 0, 0:nt], -0.5, self.rs[:, 0:nt],
                                         ALU.mult, ALU.mult).then_inc(Q(f"{self.name}_scale"), 1)

            def apply(self, act, Q, u, src, dst, done, nt=UT):
                act.wait_ge(Q(f"{self.name}_scale"), u.done)
                for j in range(nt):
                    last = act.activation(dst[:, j, :], src[:, j, :], ACT.Identity, bias=self.nm[:, j:j + 1],
                                          scale=self.rs[:, j:j + 1])
                last.then_inc(Q(done), 1)

        norm_h, norm_p = Norm("nh"), Norm("np")
        norm1, norm2, norm3, norm4 = Norm("n1"), Norm("n2"), Norm("n3"), Norm("n4")

        def turn_over(pe, dst, src, nt=UT):
            for j in range(nt):
                last = pe.transpose(dst[:, j * P:(j + 1) * P], src[:, j, :], ident[:, :])
            return last

        def products(pe, dst, lhs, rhs, nt=UT):
            for j in range(nt):
                last = pe.matmul(dst[:, j * P:(j + 1) * P], lhs[:, j, :], rhs, start=True, stop=True)
            return last

        def halves(nt):
            return [(b * GE, GE) for b in range(nt * P // GE)]

        class Hop:
            def __init__(self, name, front, weight, post, dest, table=None, idx=None, x_from=None, x_to=None,
                         col=None, bias=None, none=None, apart=True):
                self.name, self.front, self.weight, self.post, self.dest = name, front, weight, post, dest
                self.table, self.idx, self.x_from, self.x_to = table, idx, x_from, x_to
                self.col, self.bias, self.none = col, bias, none
                self.Q = S.named(name)
                self.ln = front in ("ln_bn", "ln_self", "ln_add")
                self.f = {"weight": 0}.get(front, 1)
                self.b = self.f + 1
                self.psT = psA if apart else psH
                self.alone = apart

            def index(self, pool, u):
                Q, p = self.Q, u.parity
                need(pool, Q("rows_in", p), u.half * (16 * UT))
                pool.tensor_copy(idx8[p][:, :], self.idx[:, bass.ds(u.no * UT, UT)]).then_inc(Q("index"), 1)

            def gather(self, pool, u):
                Q, p = self.Q, u.parity
                need(pool, Q("raw_used"), u.done - 2)
                pool.wait_ge(Q("index"), u.done)
                hold(pool, Q)
                for j in range(tiles_in(u)):
                    pool.indirect_dma_start(
                        out=raw[p][:, j, :], out_offset=None, in_=self.table,
                        in_offset=bass.IndirectOffsetOnAxis(ap=idx8[p][:, j:j + 1], axis=0)
                    ).then_inc(Q("rows_in", p), 16)

            def pool_steps(self, pool):
                if self.table is None:
                    return []
                return [(lambda u: self.index(pool, u), 0, 1), (lambda u: self.gather(pool, u), 0, 2)]

            def load(self, sp, u):
                Q, p, nt = self.Q, u.parity, tiles_in(u)
                if self.x_from is not None:
                    need(sp, Q("xin_used"), u.done - 2)
                    hold(sp, Q)
                    sp.dma_start(xinh[p][:, 0:nt, :], rows(self.x_from, u)).then_inc(Q("x_in", p), 16)
                if self.front == "bn_elu":
                    need(sp, Q("message"), u.done - 2)
                    to = (n_x3, n_x3b)[p]
                    hold(sp, Q)
                    sp.dma_start(flat(to, nt), w0_lin.rearrange("t e -> (t e)")[bass.ds(u.no * UE, nt * P)]
                                 .rearrange("(o e) -> o e", o=1).broadcast_to([P, nt * P])
                                 ).then_inc(Q("w0_in", p), 16)

            def store_x(self, sp, u):
                Q = self.Q
                sp.wait_ge(Q("x_done"), u.done)
                hold(sp, Q)
                sp.dma_start(rows(self.x_to, u), xnew[:, 0:tiles_in(u), :]).then_inc(Q("x_out"), 16)

            def store(self, sp, u):
                Q, p = self.Q, u.parity
                sp.wait_ge(Q("out_ready"), u.done)
                hold(sp, Q)
                sp.dma_start(rows(self.dest, u), outr[p][:, 0:tiles_in(u), :]).then_inc(Q("out_out", p), 16)

            def sp_steps(self, sp):
                last = self.b + (self.post == "affine")
                steps = []
                if self.x_from is not None or self.front == "bn_elu":
                    steps.append((lambda u: self.load(sp, u), 0, 1))
                if self.x_to is not None:
                    steps.append((lambda u: self.store_x(sp, u), self.f, 7.5))
                return steps + [(lambda u: self.store(sp, u), last, 5)]

            def stored(self, eng):
                Q = self.Q
                eng.wait_ge(Q("out_out", 0), 16 * (NU - NU // 2))
                eng.wait_ge(Q("out_out", 1), 16 * (NU // 2))
                if self.x_to is not None:
                    eng.wait_ge(Q("x_out"), 16 * NU)
                if self.none is not None:
                    eng.wait_ge(Q("none_out"), 16)

            def pe_steps(self, pe):
                Q, front = self.Q, self.front

                def product(u):
                    nt = tiles_in(u)
                    pe.wait_ge(Q("summed"), u.done)
                    need(pe, Q("psZ_used"), u.done - 1)
                    if front == "sage":
                        pe.wait_ge(Q("nT_ready"), min(u.done + 1, NU) if isinstance(u.done, int) else u.done + 1)
                    products(pe, psH, agg[u.parity], self.weight, nt).then_inc(Q("product"), 1)

                def statistics(u):
                    nt = tiles_in(u)
                    pe.wait_ge(Q("squared"), u.done)
                    for j in range(nt):
                        pe.matmul(psB0[:, 0:1], outr[u.parity][:, j, :], ones_col[:, :], start=False, stop=False,
                                  skip_group_check=True)
                    for j in range(nt):
                        last = pe.matmul(psB1[:, 0:1], sq[:, j, :], ones_col[:, :], start=False, stop=False,
                                         skip_group_check=True)
                    last.then_inc(Q("stats_read"), 1)

                def turn(u):
                    nt = tiles_in(u)
                    if front == "bn_elu":
                        pe.wait_ge(Q("rows_in", u.parity), rows_in_value(u))
                        need(pe, Q("elu_in"), u.done - 1)
                        turn_over(pe, self.psT, raw[u.parity], nt).then_inc(Q("raw_used"), 1)
                        return
                    pe.wait_ge(Q("scaled" if front in ("weight", "ln_self") else "x_done"), u.done)
                    if self.alone:
                        need(pe, Q("summed"), u.done - 1)
                    else:
                        need(pe, Q("psZ_used"), u.done - 1)
                    src = scaled if front in ("weight", "ln_self") else xnew
                    turn_over(pe, self.psT, src, nt).then_inc(Q("turned"), 1)

                def self_turn(u):
                    nt = tiles_in(u)
                    pe.wait_ge(Q("x_in", u.parity), u.half * 16 + 16)
                    need(pe, Q("xT_ready"), u.done - 1)
                    turn_over(pe, psB0, xinh[u.parity], nt).then_inc(Q("xin_used"), 1)

                def self_product(u):
                    pe.wait_ge(Q("xT_ready"), u.done)
                    need(pe, Q("psU_used"), u.done - 1)
                    products(pe, psB1, n_xT, wsI[:, :], tiles_in(u)).then_inc(Q("self_done"), 1)

                def sage_turn(u):
                    nt = tiles_in(u)
                    pe.wait_ge(Q("x_in", u.parity), u.half * 16 + 16)
                    need(pe, Q("summed"), u.done - 1)
                    turn_over(pe, psA, xinh[u.parity], nt).then_inc(Q("xin_used"), 1)
                    pe.wait_ge(Q("rows_in", u.parity), rows_in_value(u))
                    need(pe, Q("psZ_used"), u.done - 2)
                    turn_over(pe, psH, raw[u.parity], nt).then_inc(Q("raw_used"), 1)

                def sage_hidden(u):
                    nt = tiles_in(u)
                    pe.wait_ge(Q("nT_ready"), u.done)
                    need(pe, Q("hT_ready"), (u.done - 1) * 2)
                    for c, ps in enumerate((psB0, psB1)):
                        for at, n in halves(nt):
                            pe.matmul(ps[:, at:at + n], ws1[:, c * P:(c + 1) * P], flat(n_xT)[:, at:at + n],
                                      start=True, stop=False)
                            last = pe.matmul(ps[:, at:at + n], wn1[:, c * P:(c + 1) * P], flat(n_u1)[:, at:at + n],
                                             start=False, stop=True)
                        last.then_inc(Q("hidden"), 1)

                def sage_message(u):
                    pe.wait_ge(Q("hT_ready"), u.done * 2)
                    pe.wait_ge(Q("xT_ready"), u.done)
                    for at, n in halves(tiles_in(u)):
                        for c in range(2):
                            last = pe.matmul(psA[:, at:at + n], wn2[:, c, :], flat(n_hT[c])[:, at:at + n],
                                             start=(c == 0), stop=(c == 1))
                    last.then_inc(Q("turned"), 1)

                steps = [(product, self.b, 3)]
                if self.post == "stats":
                    steps += [(statistics, self.b, 4.5)]
                if front == "ln_self":
                    steps += [(turn, self.f, 10), (self_turn, 0, 13), (self_product, 0, 13.4)]
                elif front == "sage":
                    steps += [(sage_hidden, 1, 9), (sage_message, 1, 9.7), (sage_turn, 0, 11)]
                else:
                    steps += [(turn, 0 if front in ("weight", "bn_elu") else self.f, 10)]
                return steps

            def act_steps(self, act):
                Q, front, post = self.Q, self.front, self.post

                def scale_rows(u, src, dst, by):
                    for j in range(tiles_in(u)):
                        last = act.activation(dst[:, j, :], src[:, j, :], ACT.Copy, scale=by[:, bass.ds(u.no * UT + j, 1)])
                    return last

                def weigh(u):
                    if self.table is None:
                        act.wait_ge(Q("x_in", u.parity), u.half * 16 + 16)
                        src = xinh[u.parity]
                    else:
                        act.wait_ge(Q("rows_in", u.parity), rows_in_value(u))
                        src = raw[u.parity]
                    need(act, Q("turned"), u.done - 1)
                    scale_rows(u, src, scaled, self.col).then_inc(Q("scaled"), 1)

                def new_x(u):
                    need(act, Q("turned"), u.done - 1)
                    if self.x_to is not None:
                        need(act, Q("x_out"), (u.done - 1) * 16)
                    norm_h.apply(act, Q, u, uh, xnew, "x_done", tiles_in(u))
                    if front == "ln_self":
                        act.wait_ge(Q("x_done"), u.done)
                        scale_rows(u, xnew, scaled, nsrc_c).then_inc(Q("scaled"), 1)

                def self_copy(u):
                    nt = tiles_in(u)
                    act.wait_ge(Q("xin_used"), u.done)
                    need(act, Q("self_done"), u.done - 1)
                    act.activation(flat(n_xT, nt), psB0[:, 0:nt * P], ACT.Copy).then_inc(Q("xT_ready"), 1)

                def elu_parts(u):
                    nt = tiles_in(u)
                    act.wait_ge(Q("raw_used"), u.done)
                    need(act, Q("message"), u.done - 1)
                    y = self.psT[:, 0:nt * P]
                    act.activation(flat(n_u1, nt), y, ACT.Relu, bias=bn_c[:, :], scale=bn_a[:, :])
                    act.activation(flat(n_u2, nt), y, ACT.Relu, bias=bn_nc[:, :], scale=bn_na[:, :]
                                   ).then_inc(Q("elu_in"), 1)
                    act.wait_ge(Q("elu_in"), u.done)
                    act.activation(flat(n_u3, nt), flat(n_u2, nt), ACT.Exp, scale=-1.0).then_inc(Q("exp_done"), 1)

                def sage_copy(u):
                    nt = tiles_in(u)
                    act.wait_ge(Q("xin_used"), u.done)
                    need(act, Q("hidden"), (u.done - 1) * 2)
                    act.activation(flat(n_xT, nt), psA[:, 0:nt * P], ACT.Copy).then_inc(Q("xT_ready"), 1)
                    act.wait_ge(Q("raw_used"), u.done)
                    act.activation(flat(n_u1, nt), psH[:, 0:nt * P], ACT.Copy).then_inc(Q("nT_ready"), 1)

                def sage_relu(u):
                    nt = tiles_in(u)
                    need(act, Q("turned"), u.done - 1)
                    for c, ps in enumerate((psB0, psB1)):
                        act.wait_ge(Q("hidden"), (u.done - 1) * 2 + c + 1)
                        act.activation(flat(n_hT[c], nt), ps[:, 0:nt * P], ACT.Relu, bias=b1_col[:, c:c + 1]
                                       ).then_inc(Q("hT_ready"), 1)

                def out_rows(u):
                    act.wait_ge(Q("product"), u.done)
                    need(act, Q("out_out", u.parity), u.half * 16)
                    if post == "stats":
                        need(act, Q("stats_read"), u.done - 2)
                    scale_rows(u, tiles(psH), outr[u.parity], ndrep_c if post == "stats" else rdeg_c
                               ).then_inc(Q("out_ready"), 1)

                def gelu(u):
                    nt = tiles_in(u)
                    act.wait_ge(Q("psZ_used"), u.done)
                    need(act, Q("out_out", u.parity), u.half * 16)
                    act.activation(flat(outr[u.parity], nt), flat(sq, nt), ACT.Gelu).then_inc(Q("out_ready"), 1)

                steps = []
                if self.ln:
                    steps.append((new_x, self.f, 7))
                if front == "weight":
                    steps.append((weigh, 0, 7))
                if front == "ln_self":
                    steps.append((self_copy, 0, 13.2))
                if front == "bn_elu":
                    steps.append((elu_parts, 0, 10.5))
                if front == "sage":
                    steps += [(sage_relu, 1, 9.5), (sage_copy, 0, 11.5)]
                if post in ("stats", "scale"):
                    steps.append((out_rows, self.b, 4))
                if post == "gelu":
                    steps.append((gelu, self.b, 4.3))
                if self.ln:
                    steps.append((lambda u: norm_h.root(act, Q, u, tiles_in(u)), 0, 16))
                if post == "affine":
                    steps.append((lambda u: norm_p.root(act, Q, u, tiles_in(u)), self.b, 15))
                return steps

            def dve_steps(self, dve):
                Q, front, post = self.Q, self.front, self.post

                def before_norm(u):
                    nt, p = tiles_in(u), u.parity
                    need(dve, Q("x_done"), u.done - 1)
                    if front == "ln_self":
                        dve.wait_ge(Q("self_done"), u.done)
                        dve.wait_ge(Q("rows_in", p), rows_in_value(u))
                        dve.tensor_tensor(uh[:, 0:nt, :], tiles(psB1, nt), raw[p][:, 0:nt, :], ALU.add
                                          ).then_inc(Q("psU_used"), 1)
                        dve.wait_ge(Q("psU_used"), u.done)
                        dve.sem_inc(Q("raw_used"), 1)
                    if front == "ln_add":
                        dve.wait_ge(Q("rows_in", p), rows_in_value(u))
                        dve.wait_ge(Q("x_in", p), u.half * 16 + 16)
                        dve.tensor_tensor(uh[:, 0:nt, :], xinh[p][:, 0:nt, :], raw[p][:, 0:nt, :], ALU.add
                                          ).then_inc(Q("raw_used"), 1)
                        dve.wait_ge(Q("raw_used"), u.done)
                        dve.sem_inc(Q("xin_used"), 1)
                    if front == "ln_bn":
                        dve.wait_ge(Q("rows_in", p), rows_in_value(u))
                        dve.tensor_tensor(uh[:, 0:nt, :], raw[p][:, 0:nt, :], over(a3_row, nt), ALU.mult
                                          ).then_inc(Q("raw_used"), 1)
                        dve.wait_ge(Q("raw_used"), u.done)
                        dve.wait_ge(Q("x_in", p), u.half * 16 + 16)
                        dve.tensor_tensor(uh[:, 0:nt, :], uh[:, 0:nt, :], xinh[p][:, 0:nt, :], ALU.add
                                          ).then_inc(Q("xin_used"), 1)
                        dve.wait_ge(Q("xin_used"), u.done)
                        dve.tensor_tensor(uh[:, 0:nt, :], uh[:, 0:nt, :], over(c3_row, nt), ALU.add
                                          ).then_inc(Q("u_ready"), 1)
                        dve.wait_ge(Q("u_ready"), u.done)
                    norm_h.stats(dve, Q, u, uh, nt)

                def elu_message(u):
                    nt, p = tiles_in(u), u.parity
                    dve.wait_ge(Q("exp_done"), u.done)
                    dve.scalar_tensor_tensor(flat(n_u0, nt), flat(n_u3, nt), -1.0, flat(n_u1, nt), ALU.add, ALU.add
                                             ).then_inc(Q("elu_done"), 1)
                    dve.wait_ge(Q("elu_done"), u.done)
                    dve.wait_ge(Q("w0_in", p), u.half * 16 + 16)
                    dve.tensor_tensor(flat(n_u0, nt), flat(n_u0, nt), flat((n_x3, n_x3b)[p], nt), ALU.mult
                                      ).then_inc(Q("message"), 1)

                def total(u):
                    nt, p = tiles_in(u), u.parity
                    if front == "bn_elu":
                        dve.wait_ge(Q("message"), u.done)
                        src = flat(n_u0, nt)
                    else:
                        dve.wait_ge(Q("turned"), u.done)
                        src = self.psT[:, 0:nt * P]
                    need(dve, Q("product"), u.done - 2)
                    need(dve, Q("summed"), u.done - 1)
                    start = 0.0 if first(u.no) else agg[1 - p][:, UT - 1, P - 1:P]
                    dve.tensor_tensor_scan(flat(agg[p], nt), same[:, bass.ds(u.no * UE, nt * P)], src, start,
                                           ALU.mult, ALU.add).then_inc(Q("summed"), 1)

                def squares(u):
                    nt, p = tiles_in(u), u.parity
                    dve.wait_ge(Q("out_ready"), u.done)
                    dve.sem_inc(Q("psZ_used"), 1)
                    if post == "stats":
                        need(dve, Q("stats_read"), u.done - 1)
                        dve.tensor_tensor(sq[:, 0:nt, :], outr[p][:, 0:nt, :], outr[p][:, 0:nt, :], ALU.mult
                                          ).then_inc(Q("squared"), 1)

                def biased(u):
                    nt, p = tiles_in(u), u.parity
                    to = outr[p] if post == "bias" else sq
                    dve.wait_ge(Q("product"), u.done)
                    if post == "bias":
                        need(dve, Q("out_out", p), u.half * 16)
                    if post == "gelu":
                        need(dve, Q("out_ready"), u.done - 1)
                    if post == "affine":
                        need(dve, Q("normed"), u.done - 1)
                    by = rdeg_c if post == "bias" else nd_c
                    for j in range(nt):
                        last = dve.scalar_tensor_tensor(to[:, j, :], psH[:, j * P:(j + 1) * P],
                                                        by[:, bass.ds(u.no * UT + j, 1)], self.bias, ALU.mult, ALU.add)
                    if post == "bias":
                        last.then_inc(Q("out_ready"), 1)
                        dve.wait_ge(Q("out_ready"), u.done)
                        dve.sem_inc(Q("psZ_used"), 1)
                    else:
                        last.then_inc(Q("psZ_used"), 1)
                    if post == "affine":
                        dve.wait_ge(Q("psZ_used"), u.done)
                        norm_p.stats(dve, Q, u, sq, nt)

                def affine(u):
                    nt, p = tiles_in(u), u.parity
                    norm_p.scale(dve, Q, u, nt, shift=False)
                    dve.wait_ge(Q("np_scale"), u.done)
                    need(dve, Q("out_out", p), u.half * 16)
                    for j in range(nt):
                        last = dve.scalar_tensor_tensor(outr[p][:, j, :], sq[:, j, :], norm_p.rs[:, j:j + 1],
                                                        row["L2_gnn_gamma"][:, :], ALU.mult, ALU.mult)
                    last.then_inc(Q("normed"), 1)
                    dve.wait_ge(Q("normed"), u.done)
                    dve.tensor_tensor(outr[p][:, 0:nt, :], outr[p][:, 0:nt, :], over(row["L2_gnn_beta"], nt), ALU.add
                                      ).then_inc(Q("out_ready"), 1)

                steps = []
                if post == "affine":
                    steps.append((affine, self.b + 1, 2.5))
                if post in ("stats", "scale"):
                    steps.append((squares, self.b, 4.2))
                else:
                    steps.append((biased, self.b, 4))
                if self.ln:
                    steps.append((lambda u: norm_h.scale(dve, Q, u, tiles_in(u)), self.f, 2))
                if front == "bn_elu":
                    steps.append((elu_message, self.f, 6.6))
                if front == "weight":
                    def weighed(u):
                        dve.wait_ge(Q("scaled"), u.done)
                        dve.sem_inc(Q("raw_used" if self.table is not None else "xin_used"), 1)
                    steps.append((weighed, 0, 10.2))
                steps.append((total, self.f, 10.6))
                if self.ln:
                    steps.append((before_norm, 0, 14))
                return steps

        class Nodes:
            def __init__(self, edges):
                self.edges, self.units = edges, NU if edges else NUN
                self.Q = S.named("edge_nodes" if edges else "nodes")

            def tiles(self, u):
                return tiles_in(u) if self.edges else UT

            def span(self, ap, u):
                start = 0 if first(u.no) else (u.no - 1) * UE + FIRST_NODES
                return ap[bass.ds(start, UE), :].rearrange("(p t) f -> p t f", t=UT)

            def sp_steps(self, sp):
                Q = self.Q

                def load(u):
                    nt = self.tiles(u)
                    if not self.edges:
                        need(sp, Q("u0_ready"), u.done - 1)
                        hold(sp, Q)
                        sp.dma_start(n_xin[:, :, :], self.span(A["x"], u)).then_inc(Q("x_in"), 16)
                        return
                    need(sp, Q("u0_ready"), u.done - 1)
                    hold(sp, Q)
                    sp.dma_start(n_xin[:, 0:nt, :], rows(x0d, u)).then_inc(Q("x_in"), 16)
                    need(sp, Q("z3_used"), u.done - 1)
                    hold(sp, Q)
                    sp.dma_start(raw[0][:, 0:nt, :], rows(tabs["z3"], u)).then_inc(Q("z3_in"), 16)

                def load_a1(u):
                    need(sp, Q("n2_stats"), u.done - 1)
                    hold(sp, Q)
                    sp.dma_start(xinh[0][:, 0:self.tiles(u), :], rows(tabs["a1"], u)).then_inc(Q("a1_in"), 16)

                def load_a2(u):
                    need(sp, Q("n3_stats"), u.done - 1)
                    hold(sp, Q)
                    sp.dma_start(xinh[1][:, 0:self.tiles(u), :], rows(tabs["a2"], u)).then_inc(Q("a2_in"), 16)

                def load_last(u):
                    nt = self.tiles(u)
                    need(sp, Q("nT_turned"), u.done - 1)
                    hold(sp, Q)
                    sp.dma_start(raw[1][:, 0:nt, :], rows(tabs["n1"], u)).then_inc(Q("n1_in"), 16)
                    need(sp, Q("x3b_ready"), u.done - 1)
                    hold(sp, Q)
                    sp.dma_start(uh[:, 0:nt, :], rows(tabs["a4"], u)).then_inc(Q("a4_in"), 16)

                def store(u):
                    need(sp, Q("out_out"), (u.done - 1) * 16)
                    hold(sp, Q)
                    sp.wait_ge(Q("out_done"), u.done)
                    hold(sp, Q)
                    sp.dma_start(self.span(out, u), n_out[:, :, :]).then_inc(Q("out_out"), 16)

                if self.edges:
                    return [(load_last, 4, 15.5), (load_a2, 3, 15.6), (load_a1, 2, 15.7), (load, 0, 15.8)]
                return [(store, 7, 3.5), (load, 0, 15.8)]

            def pool_steps(self, pool):
                Q = self.Q

                def add0(u):
                    nt = self.tiles(u)
                    need(pool, Q("u0_turned"), u.done - 1)
                    need(pool, Q("n1_stats"), u.done - 1)
                    pool.wait_ge(Q("x_in"), u.done * 16)
                    if self.edges:
                        pool.wait_ge(Q("z3_used"), u.done)
                        pool.tensor_tensor(scaled[:, 0:nt, :], outr[0][:, 0:nt, :], n_xin[:, 0:nt, :], ALU.add
                                           ).then_inc(Q("u0_part"), 1)
                        pool.wait_ge(Q("u0_part"), u.done)
                        pool.tensor_tensor(n_u0[:, 0:nt, :], scaled[:, 0:nt, :], over(c3_row, nt), ALU.add
                                           ).then_inc(Q("u0_ready"), 1)
                    else:
                        pool.tensor_tensor(n_u0[:, :, :], n_xin[:, :, :], over(c3_row), ALU.add
                                           ).then_inc(Q("u0_ready"), 1)

                def add3(u):
                    nt = self.tiles(u)
                    need(pool, Q("n4_stats"), u.done - 1)
                    if self.edges:
                        pool.wait_ge(Q("a4_in"), u.done * 16)
                    pool.wait_ge(Q("x3_done"), u.done)
                    add = uh[:, 0:nt, :] if self.edges else over(row["L3_gnn_b2"])
                    pool.tensor_tensor(n_x3b[:, 0:nt, :], n_x3[:, 0:nt, :], add, ALU.add).then_inc(Q("x3b_ready"), 1)

                def put_index(u):
                    need(pool, Q("put_out"), (u.done - 1) * (16 * UT))
                    pool.tensor_copy(put8[0][:, :], put_idx[:, bass.ds(u.no * UT, UT)]).then_inc(Q("put_index"), 1)

                def put(u):
                    nt = self.tiles(u)
                    pool.wait_ge(Q("out_done"), u.done)
                    pool.wait_ge(Q("put_index"), u.done)
                    hold(pool, Q)
                    for j in range(nt):
                        pool.indirect_dma_start(
                            out=out, out_offset=bass.IndirectOffsetOnAxis(ap=put8[0][:, j:j + 1], axis=0),
                            in_=n_out[:, j, :], in_offset=None, bounds_check=N - 1, oob_is_err=False
                        ).then_inc(Q("put_out"), 16)

                steps = [(add3, 5, 5.5), (add0, 1, 15)]
                return [(put_index, 7, 3), (put, 7, 3.1)] + steps if self.edges else steps

            def pe_steps(self, pe):
                Q = self.Q

                def turn0(u):
                    pe.wait_ge(Q("u0_ready"), u.done)
                    need(pe, Q("u1_ready"), u.done - 1)
                    turn_over(pe, psA, n_u0, self.tiles(u)).then_inc(Q("u0_turned"), 1)

                def product0(u):
                    pe.wait_ge(Q("xT_ready"), u.done)
                    products(pe, psA, n_xT, wsC[:, :], self.tiles(u)).then_inc(Q("self_done"), 1)

                def turn3(u):
                    nt = self.tiles(u)
                    need(pe, Q("u3_ready"), u.done - 1)
                    pe.wait_ge(Q("x3_done"), u.done)
                    turn_over(pe, psB0, n_x3, nt).then_inc(Q("x3_turned"), 1)
                    if self.edges:
                        need(pe, Q("nT_ready"), u.done - 1)
                        pe.wait_ge(Q("n1_in"), u.done * 16)
                        turn_over(pe, psH, raw[1], nt).then_inc(Q("nT_turned"), 1)

                def hidden(u):
                    nt = self.tiles(u)
                    pe.wait_ge(Q("x3T_ready"), u.done)
                    if self.edges:
                        pe.wait_ge(Q("nT_ready"), u.done)
                    for c, ps in enumerate((psB0, psB1)):
                        for at, n in halves(nt):
                            last = pe.matmul(ps[:, at:at + n], ws1[:, c * P:(c + 1) * P], flat(n_x3T)[:, at:at + n],
                                             start=True, stop=not self.edges)
                            if self.edges:
                                last = pe.matmul(ps[:, at:at + n], wn1[:, c * P:(c + 1) * P], flat(xnew)[:, at:at + n],
                                                 start=False, stop=True)
                        last.then_inc(Q("hidden"), 1)

                def second(u):
                    pe.wait_ge(Q("hT_ready"), u.done * 2)
                    for j in range(self.tiles(u)):
                        for c in range(2):
                            last = pe.matmul(psB0[:, j * P:(j + 1) * P], n_hT[c][:, j, :], ws2[:, c, :],
                                             start=(c == 0), stop=(c == 1))
                    last.then_inc(Q("sage_done"), 1)

                return [(turn3, 5, 6), (hidden, 5, 9), (second, 5, 11), (turn0, 2, 13), (product0, 2, 13.5)]

            def act_steps(self, act):
                Q = self.Q

                def apply4(u):
                    if self.edges:
                        need(act, Q("put_out"), (u.done - 1) * (16 * UT))
                    else:
                        need(act, Q("out_out"), (u.done - 1) * 16)
                    norm4.apply(act, Q, u, n_u3, n_out, "out_done", self.tiles(u))

                def apply3(u):
                    need(act, Q("x3_turned"), u.done - 1)
                    need(act, Q("x3b_ready"), u.done - 1)
                    norm3.apply(act, Q, u, n_u2, n_x3, "x3_done", self.tiles(u))

                def copy3(u):
                    nt = self.tiles(u)
                    act.wait_ge(Q("x3_turned"), u.done)
                    need(act, Q("hidden"), (u.done - 1) * 2)
                    act.activation(flat(n_x3T, nt), psB0[:, 0:nt * P], ACT.Copy).then_inc(Q("x3T_ready"), 1)
                    if self.edges:
                        act.wait_ge(Q("nT_turned"), u.done)
                        act.activation(flat(xnew, nt), psH[:, 0:nt * P], ACT.Copy).then_inc(Q("nT_ready"), 1)

                def relu(u):
                    nt = self.tiles(u)
                    need(act, Q("sage_done"), u.done - 1)
                    for c, ps in enumerate((psB0, psB1)):
                        act.wait_ge(Q("hidden"), (u.done - 1) * 2 + c + 1)
                        act.activation(flat(n_hT[c], nt), ps[:, 0:nt * P], ACT.Relu, bias=b1_col[:, c:c + 1]
                                       ).then_inc(Q("hT_ready"), 1)

                def copy0(u):
                    nt = self.tiles(u)
                    act.wait_ge(Q("u0_turned"), u.done)
                    need(act, Q("self_done"), u.done - 1)
                    act.activation(flat(n_xT, nt), psA[:, 0:nt * P], ACT.Copy).then_inc(Q("xT_ready"), 1)

                def root(norm):
                    return lambda u: norm.root(act, Q, u, self.tiles(u))

                return [(apply3, 5, 2), (copy3, 5, 6.5), (apply4, 7, 2.5), (relu, 5, 9.5), (copy0, 2, 13.2),
                        (root(norm4), 6, 15), (root(norm3), 4, 15), (root(norm2), 3, 15), (root(norm1), 2, 15)]

            def dve_steps(self, dve):
                Q = self.Q

                def scale4(u):
                    norm4.scale(dve, Q, u, self.tiles(u))

                def scale3(u):
                    norm3.scale(dve, Q, u, self.tiles(u))

                def sum3(u):
                    nt = self.tiles(u)
                    need(dve, Q("out_done"), u.done - 1)
                    dve.wait_ge(Q("x3b_ready"), u.done)
                    dve.wait_ge(Q("sage_done"), u.done)
                    dve.tensor_tensor(n_u3[:, 0:nt, :], tiles(psB0, nt), n_x3b[:, 0:nt, :], ALU.add
                                      ).then_inc(Q("u3_ready"), 1)
                    dve.wait_ge(Q("u3_ready"), u.done)
                    norm4.stats(dve, Q, u, n_u3, nt)

                def sum2(u):
                    nt = self.tiles(u)
                    norm2.scale(dve, Q, u, nt, shift=False)
                    dve.wait_ge(Q("n2_scale"), u.done)
                    need(dve, Q("x3_done"), u.done - 1)
                    if self.edges:
                        dve.wait_ge(Q("a2_in"), u.done * 16)
                    for j in range(nt):
                        last = dve.scalar_tensor_tensor(n_u2[:, j, :], n_u1[:, j, :], norm2.rs[:, j:j + 1],
                                                        xinh[1][:, j, :] if self.edges else a2_row[:, :],
                                                        ALU.mult, ALU.add)
                    last.then_inc(Q("u2_ready"), 1)
                    dve.wait_ge(Q("u2_ready"), u.done)
                    norm3.stats(dve, Q, u, n_u2, nt)

                def sum1(u):
                    nt = self.tiles(u)
                    norm1.scale(dve, Q, u, nt, shift=False)
                    dve.wait_ge(Q("n1_scale"), u.done)
                    dve.wait_ge(Q("self_done"), u.done)
                    if self.edges:
                        dve.wait_ge(Q("a1_in"), u.done * 16)
                    for j in range(nt):
                        last = dve.scalar_tensor_tensor(n_u1[:, j, :], psA[:, j * P:(j + 1) * P], norm1.rs[:, j:j + 1],
                                                        xinh[0][:, j, :] if self.edges else row["L1_gnn_b_self"][:, :],
                                                        ALU.mult, ALU.add)
                    last.then_inc(Q("u1_ready"), 1)
                    dve.wait_ge(Q("u1_ready"), u.done)
                    norm2.stats(dve, Q, u, n_u1, nt)

                def stats1(u):
                    nt = self.tiles(u)
                    dve.wait_ge(Q("u0_ready"), u.done)
                    norm1.stats(dve, Q, u, n_u0, nt)

                def part0(u):
                    nt = self.tiles(u)
                    need(dve, Q("u0_ready"), u.done - 1)
                    dve.wait_ge(Q("z3_in"), u.done * 16)
                    dve.tensor_tensor(outr[0][:, 0:nt, :], raw[0][:, 0:nt, :], over(a3_row, nt), ALU.mult
                                      ).then_inc(Q("z3_used"), 1)

                steps = [(scale3, 5, 1), (sum3, 6, 5), (scale4, 7, 1.5), (sum2, 4, 12), (sum1, 3, 12.2), (stats1, 2, 14)]
                return steps + [(part0, 1, 14.5)] if self.edges else steps

        zero_row = zero_f[0:1, :]
        DRAIN = 2

        def segments(segs):
            def streams(seg, which):
                hop, nodes, origin = seg["hop"], seg["nodes"], seg["origin"]
                out = []
                if hop is not None:
                    out += [(order, (f, s, 0, NU)) for f, s, order in which(hop)]
                if nodes is not None:
                    out += [(order, (f, s, origin, nodes.units)) for f, s, order in which(nodes)]
                out = [step for _, step in sorted(out, key=lambda x: x[0])]
                return out

            with nc.Block() as block:
                @block.gpsimd
                def _(pool):
                    for n, seg in enumerate(segs):
                        if n and segs[n - 1]["hop"] is not None:
                            segs[n - 1]["hop"].stored(pool)
                        if seg["beside"] is not None:
                            seg["beside"].pool(pool)
                        steps = streams(seg, lambda x: x.pool_steps(pool))
                        if steps:
                            run(pool, seg["bodies"], steps)
                        if seg["nodes"] is not None and seg["nodes"].edges:
                            pool.wait_ge(seg["nodes"].Q("put_out"), 16 * NT)

                @block.sync
                def _(sp):
                    for n, seg in enumerate(segs):
                        hop = seg["hop"]
                        if n and segs[n - 1]["hop"] is not None:
                            segs[n - 1]["hop"].stored(sp)
                        if hop is not None and hop.none is not None:
                            sp.dma_start(hop.dest[NONE_ROW:NONE_ROW + 1, :], hop.none).then_inc(hop.Q("none_out"), 16)
                        steps = streams(seg, lambda x: x.sp_steps(sp))
                        if seg["beside"] is not None:
                            steps = steps + [(lambda u: seg["beside"].store(sp, u), 0, 0, NU)]
                        run(sp, seg["bodies"], steps)
                        if hop is not None and hop is segs[-1]["hop"]:
                            hop.stored(sp)
                        if seg["beside"] is not None:
                            seg["beside"].stored(sp)
                    for seg in segs:
                        if seg["nodes"] is not None and not seg["nodes"].edges:
                            sp.wait_ge(seg["nodes"].Q("out_out"), 16 * NUN)
                            break

                @block.tensor
                def _(pe):
                    for seg in segs:
                        hop = seg["hop"]
                        stats = hop is not None and hop.post == "stats"
                        if stats:
                            for ps in (psB0, psB1):
                                pe.matmul(ps[:, 0:1], zero_f[:, :], ones_col[:, :], start=True, stop=False,
                                          skip_group_check=True)
                        run(pe, seg["bodies"], streams(seg, lambda x: x.pe_steps(pe)))
                        if stats:
                            for ps in (psB0, psB1):
                                last = pe.matmul(ps[:, 0:1], zero_f[:, :], ones_col[:, :], start=False, stop=True,
                                                 skip_group_check=True)
                            last.then_inc(hop.Q("stats_done"), 1)

                @block.scalar
                def _(act):
                    for seg in segs:
                        run(act, seg["bodies"], streams(seg, lambda x: x.act_steps(act)))

                @block.vector
                def _(dve):
                    for seg in segs:
                        run(dve, seg["bodies"], streams(seg, lambda x: x.dve_steps(dve)))
                        if seg["hop"] is not None and seg["hop"].post == "stats":
                            bn_finish(dve, seg["hop"].Q)
            S.close()

        def segment(hop=None, nodes=None, origin=0, bodies=None, beside=None):
            return {"hop": hop, "nodes": nodes, "origin": origin, "bodies": bodies or NU + DRAIN, "beside": beside}

        class FetchDst:

            def __init__(self):
                self.Q = S.named("fetch_dst")

            def pool(self, pool):
                Q = self.Q

                def index(u):
                    need(pool, Q("rows_in", u.parity), u.half * (16 * UT))
                    pool.tensor_copy(idx8[u.parity][:, :], dst_idx[:, bass.ds(u.no * UT, UT)]).then_inc(Q("index"), 1)

                def gather(u):
                    need(pool, Q("rows_out", u.parity), u.half * 16)
                    pool.wait_ge(Q("index"), u.done)
                    hold(pool, Q)
                    for j in range(tiles_in(u)):
                        pool.indirect_dma_start(
                            out=raw[u.parity][:, j, :], out_offset=None, in_=A["x"],
                            in_offset=bass.IndirectOffsetOnAxis(ap=idx8[u.parity][:, j:j + 1], axis=0)
                        ).then_inc(Q("rows_in", u.parity), 16)

                run(pool, NU, [(index, 0, 0, NU), (gather, 0, 0, NU)])

            def store(self, sp, u):
                Q = self.Q
                sp.wait_ge(Q("rows_in", u.parity), rows_in_value(u))
                hold(sp, Q)
                sp.dma_start(rows(x0d, u), raw[u.parity][:, 0:tiles_in(u), :]).then_inc(Q("rows_out", u.parity), 16)

            def stored(self, eng):
                eng.wait_ge(self.Q("rows_out", 0), 16 * (NU - NU // 2))
                eng.wait_ge(self.Q("rows_out", 1), 16 * (NU // 2))

        def bn_finish(dve, Q):
            dve.wait_ge(Q("stats_done"), 1)
            dve.tensor_scalar(bn_t[:, 0:1], psB0[:, 0:1], 1.0 / N, None, ALU.mult)
            dve.tensor_scalar(bn_t[:, 1:2], psB1[:, 0:1], 1.0 / N, None, ALU.mult
                              ).then_inc(Q("moments"), 1)
            dve.wait_ge(Q("moments"), 1)
            dve.tensor_tensor(bn_t[:, 2:3], bn_t[:, 0:1], bn_t[:, 0:1], ALU.mult).then_inc(Q("moments"), 1)
            dve.wait_ge(Q("moments"), 2)
            dve.tensor_tensor(bn_t[:, 3:4], bn_t[:, 1:2], bn_t[:, 2:3], ALU.subtract)

        def bn_coefficients(rows_too):
            with nc.Block() as block:
                @block.scalar
                def _(act):
                    act.activation(bn_t[:, 4:5], bn_t[:, 3:4], ACT.Sqrt, bias=eps_col[:, :]).then_inc(S("bn_root"), 1)

                @block.vector
                def _(dve):
                    chain = Chain(dve, S("dve_step"))
                    dve.wait_ge(S("bn_root"), 1)
                    chain.step(dve.reciprocal(bn_t[:, 5:6], bn_t[:, 4:5]))
                    chain.wait()
                    chain.step(dve.tensor_tensor(bn_a[:, :], bn_t[:, 5:6], gam_col[:, :], ALU.mult))
                    chain.wait()
                    chain.step(dve.tensor_tensor(bn_t[:, 6:7], bn_a[:, :], bn_t[:, 0:1], ALU.mult))
                    chain.wait()
                    chain.step(dve.tensor_tensor(bn_c[:, :], bet_col[:, :], bn_t[:, 6:7], ALU.subtract))
                    dve.tensor_tensor(bn_nc[:, :], bn_t[:, 6:7], bet_col[:, :], ALU.subtract)
                    dve.tensor_scalar(bn_na[:, :], bn_a[:, :], -1.0, None, ALU.mult)
                    chain.wait()
                    if rows_too:
                        dve.tensor_scalar(diag[:, 0, :], ident[:, :], bn_a[:, :], None, ALU.mult)
                        dve.tensor_scalar(diag[:, 1, :], ident[:, :], bn_c[:, :], None, ALU.mult
                                          ).then_inc(S("diag_ready"), 1)
                        dve.wait_ge(S("bn_rows"), 1)
                        dve.tensor_copy(a3_row[:, :], psA[:, 0:P])
                        dve.tensor_copy(c3_row[:, :], psA[:, P:2 * P])

                @block.tensor
                def _(pe):
                    if rows_too:
                        pe.wait_ge(S("diag_ready"), 1)
                        pe.matmul(psA[:, 0:P], ones_mat[:, :], diag[:, 0, :], start=True, stop=True)
                        pe.matmul(psA[:, P:2 * P], ones_mat[:, :], diag[:, 1, :], start=True, stop=True
                                  ).then_inc(S("bn_rows"), 1)
            S.close()

        with nc.Block() as block:
            @block.scalar
            def _(act):
                for k, n in enumerate(("L2_gnn_b1", "L2_gnn_b2", "L2_gnn_b3")):
                    act.activation(none_rows[:, k, :], row[n][:, :], ACT.Gelu)
                norm_h.root(act, S.named("c"), Unit(0, 0))
                norm_h.apply(act, S.named("c"), Unit(0, 0), over(row["L2_gnn_b4"]), sq, "done")

            @block.vector
            def _(dve):
                norm_h.stats(dve, S.named("c"), Unit(0, 0), over(row["L2_gnn_b4"]))
                norm_h.scale(dve, S.named("c"), Unit(0, 0))
                dve.wait_ge(S.named("c")("done"), 1)
                dve.tensor_tensor(a2_row[:, :], sq[:, 0, :], row["L2_gnn_gamma"][:, :], ALU.mult
                                  ).then_inc(S("scaled"), 1)
                dve.wait_ge(S("scaled"), 1)
                dve.tensor_tensor(a2_row[:, :], a2_row[:, :], row["L2_gnn_beta"][:, :], ALU.add)
        S.close()

        segments([segment(Hop("h0", "weight", w["L0_gnn_W1"][:, :], "stats", tabs["z1"], x_from=xs["x0"], col=w0_c,
                              none=zero_row), beside=FetchDst())])
        bn_coefficients(False)
        segments([segment(Hop("h1", "bn_elu", w["L0_gnn_W2"][:, :], "stats", tabs["z2"], table=tabs["z1"], idx=slot_idx,
                              none=zero_row))])
        bn_coefficients(False)
        segments([segment(Hop("h2", "bn_elu", w["L0_gnn_W3"][:, :], "stats", tabs["z3"], table=tabs["z2"], idx=slot_idx,
                              none=zero_row))])
        bn_coefficients(True)

        BODIES = NU + DRAIN
        nodes = Nodes(False)
        NODE_SKEW = 7
        start = 4 * BODIES - NUN - NODE_SKEW
        assert 0 <= start < BODIES - NODE_SKEW
        beside = [dict(nodes=nodes, origin=start - k * BODIES) for k in range(4)]
        segments([
            segment(Hop("h3", "ln_bn", wnT[:, :], "bias", tabs["a1"], table=tabs["z3"], idx=slot_idx, x_from=xs["x0"],
                        x_to=xs["x1"], bias=row["L1_gnn_b_self"][:, :], none=row["L1_gnn_b_self"][0:1, :])),
            segment(Hop("h4", "ln_self", w["L2_gnn_W1"][:, :], "gelu", tabs["g1"], table=tabs["a1"], idx=slot_idx,
                        x_from=xs["x1"], x_to=xs["x2"], bias=row["L2_gnn_b1"][:, :], none=none_rows[0:1, 0, :])),
        ])
        segments([
            segment(Hop("h5", "weight", w["L2_gnn_W2"][:, :], "gelu", tabs["g2"], table=tabs["g1"], idx=slot_idx,
                        col=nsrc_c, bias=row["L2_gnn_b2"][:, :], none=none_rows[0:1, 1, :], apart=False), **beside[0]),
            segment(Hop("h6", "weight", w["L2_gnn_W3"][:, :], "gelu", tabs["g3"], table=tabs["g2"], idx=slot_idx,
                        col=nsrc_c, bias=row["L2_gnn_b3"][:, :], none=none_rows[0:1, 2, :], apart=False), **beside[1]),
            segment(Hop("h7", "weight", w4C[:, :], "affine", tabs["a2"], table=tabs["g3"], idx=slot_idx,
                        col=nsrc_c, bias=b4C[:, :], none=a2_row[0:1, :], apart=False), **beside[2]),
            segment(Hop("h8", "ln_add", ident[:, :], "scale", tabs["n1"], table=tabs["a2"], idx=slot_idx,
                        x_from=xs["x2"], x_to=xs["x3"], none=zero_row, apart=False), **beside[3]),
        ])
        segments([segment(Hop("h9", "sage", ident[:, :], "bias", tabs["a4"], table=tabs["n1"], idx=slot_idx,
                              x_from=xs["x3"], bias=row["L3_gnn_b2"][:, :]))])
        segments([segment(nodes=Nodes(True), bodies=NU + NODE_SKEW)])


def kernel(**inputs):
    import numpy as _np
    import concourse.bacc as _bacc
    from concourse import mybir as _mybir
    from concourse.bass_utils import run_bass_kernel_spmd as _run

    nc = _bacc.Bacc("TRN2", target_bir_lowering=False, num_devices=1)
    arrays, aps = {}, {}
    for name, value in inputs.items():
        a = _np.ascontiguousarray(value)
        arrays[f"in_{name}_dram"] = a
        aps[name] = nc.dram_tensor(f"in_{name}_dram", a.shape, _mybir.dt.from_np(a.dtype), kind="ExternalInput").ap()
    y = nc.dram_tensor("out_0_dram", inputs["x"].shape, _mybir.dt.float32, kind="ExternalOutput").ap()
    gnn_stack(nc, aps, y)
    r = _run(nc, [arrays], core_ids=[0])
    return r.results[0]["out_0_dram"]
```

```python
from contextlib import ExitStack

import concourse.bass as bass
from concourse import mybir

F32 = mybir.dt.float32
I32 = mybir.dt.int32
BF16 = mybir.dt.bfloat16
F16 = mybir.dt.float16
ALU = mybir.AluOpType
ACT = mybir.ActivationFunctionType

P = 128
GT = 4
GE = GT * P
UT = 2 * GT
UE = UT * P
EPS = 1e-5
DT = 2
LO = 512
ABSENT = 1 << 20


class Signals:

    def __init__(self, nc):
        self.nc, self.sems, self.stage = nc, {}, 0

    def __call__(self, name, lane=0):
        key = f"{name}{lane}"
        if key not in self.sems:
            self.sems[key] = self.nc.alloc_semaphore(f"{key}_stage{self.stage}")
        return self.sems[key]

    def close(self):
        self.nc.clear_and_free_semaphores(list(self.sems.values()))
        self.nc.all_engine_barrier()
        self.sems = {}
        self.stage += 1

    def named(self, prefix):
        return lambda name, lane=0: self(f"{prefix}_{name}_", lane)


class Chain:

    def __init__(self, eng, sem):
        self.eng, self.sem, self.per_body, self.base, self.k = eng, sem, 0, 0, 0

    def body(self, i):
        if isinstance(i, int) and i == 0:
            self.k = 0
            self.base = 0
        else:
            if not self.per_body:
                self.per_body = self.k
            self.base, self.k = i * self.per_body, 0

    def step(self, ins):
        self.k += 1
        return ins.then_inc(self.sem, 1)

    def wait(self):
        self.eng.wait_ge(self.sem, self.base + self.k)


def first(i):
    return isinstance(i, int) and i == 0


class Unit:

    def __init__(self, half, parity):
        self.half, self.parity = half, parity
        self.no = half * 2 + parity
        self.done = half * 2 + (parity + 1)

    def back(self, by, origin=0):
        off = self.parity - by - origin
        return Unit(self.half + off // 2, off % 2)


def need(eng, sem, value):
    if isinstance(value, int) and value <= 0:
        return
    eng.wait_ge(sem, value)


def hold(eng, Q):
    eng.sem_inc(Q("turns_of_" + str(eng.engine.name)), 1)


def run(eng, n_bodies, steps):
    def states(b):
        out = []
        for _, skew, origin, units in steps:
            u = b - skew - origin
            out.append("off" if u < 0 or u >= units else "steady" if 3 <= u < units - 1 else b)
        return out

    def body(half, parity):
        b = half * 2 + parity if isinstance(half, int) else None
        for step, skew, origin, units in steps:
            if b is not None:
                on = 0 <= b - skew - origin < units
            else:
                on = 0 <= loop[0] * 2 + parity - skew - origin < units
            if on:
                step(Unit(half, parity).back(skew, origin))

    same = [h for h in range(n_bodies // 2)
            if all(x != y or x == "off" or x == "steady"
                   for x, y in zip(states(2 * h), states(2 * h + 1)))
            and not any(isinstance(x, int) for x in states(2 * h) + states(2 * h + 1))]
    loop, best = (0, 0), (0, 0)
    for h in same:
        e = h
        while e in same and states(2 * e) == states(2 * h) and states(2 * e + 1) == states(2 * h):
            e += 1
        if e - h > best[1] - best[0]:
            best = (h, e)
    loop = best
    if loop[1] - loop[0] < 2:
        loop = (n_bodies, n_bodies)
    for b in range(min(loop[0] * 2, n_bodies)):
        body(b // 2, b % 2)
    if loop[0] < n_bodies:
        with eng.Fori(loop[0], loop[1]) as half:
            body(half, 0)
            body(half, 1)
        for b in range(loop[1] * 2, n_bodies):
            body(b // 2, b % 2)


PLAN = {
    ("weight", "stats", True): {
        "src_weights": (1, 1), "out_rows": (3, 2), "product": (3, 3), "slots": (0, 4), "store": (3, 5),
        "slot_index": (0, 6), "slot_gather": (0, 7), "total": (2, 8), "squares": (3, 9), "nsrc_root": (0, 10),
        "sums": (3, 11), "load": (0, 12), "turn": (2, 13), "weigh": (1, 14),
    },
    ("bn_elu", "stats", True): {
        "elu_message": (1, 1), "sums": (3, 2), "product": (3, 3), "out_rows": (3, 4), "elu_parts": (1, 5),
        "index": (1, 6), "gather": (1, 7), "store": (3, 8), "squares": (3, 9), "total": (1, 10),
        "turn": (1, 11), "load": (1, 12),
    },
    ("ln_bn", "bias", True): {
        "load": (0, 1), "before_norm": (1, 2), "index": (0, 3), "gather": (0, 4), "root_h": (1, 5),
        "scale_h": (1, 6), "new_x": (1, 7), "turn": (2, 8), "store_x": (1, 9), "total": (2, 10),
        "product": (3, 11), "biased": (3, 12), "store": (3, 13),
    },
    ("ln_self", "gelu", True): {
        "self_copy": (0, 1), "root_h": (1, 2), "biased": (4, 3), "load": (0, 4), "product": (4, 5),
        "scale_h": (1, 6), "store_x": (2, 7), "index": (0, 8), "gather": (0, 9), "self_turn": (0, 10),
        "turn": (3, 11), "total": (3, 12), "self_product": (0, 13), "scale_x": (2, 14), "store": (5, 15),
        "new_x": (1, 16), "before_norm": (0, 17), "gelu": (4, 18),
    },
    ("weight", "gelu", False): {
        "index": (0, 2.27), "gather": (0, 2.27), "turn": (1, 4.14), "weigh": (0, 8.29), "total": (1, 14.31),
        "gelu": (2, 15.42), "store": (2, 15.46), "product": (1, 18.36), "biased": (1, 19.11),
    },
    ("weight", "affine", False): {
        "product": (2, 4.05), "total": (2, 6.67), "index": (0, 11.62), "gather": (0, 11.63),
        "shift": (3, 13.89), "weigh": (1, 15.81), "biased": (2, 17.00), "root_p": (2, 18.21),
        "affine": (2, 19.28), "turn": (1, 19.31), "store": (3, 19.48),
    },
    ("ln_add", "scale", False): {
        "store": (4, 1.35), "store_x": (1, 3.89), "root_h": (1, 4.39), "new_x": (1, 5.22), "index": (0, 5.83),
        "gather": (0, 5.83), "out_rows": (2, 6.52), "scale_h": (1, 9.35), "product": (2, 11.72),
        "load": (0, 15.60), "turn": (1, 16.49), "before_norm": (0, 18.07), "total": (1, 18.85),
    },
    ("sage", "bias", True): {
        "message": (2, 1), "total": (2, 2), "product": (2, 3), "sage_relu": (1, 4), "index": (0, 5),
        "gather": (0, 6), "biased": (2, 7), "sage_copy": (0, 8), "load": (0, 9), "store": (2, 10),
        "hidden": (1, 11), "sage_turn": (0, 12),
    },
    "nodes": {
        "dst_store": (1, 0.01), "dst_index": (0, 19.98), "dst_gather": (0, 19.99),
        "store": (7, 1.93), "second": (6, 2.21), "apply4": (7, 3.18), "apply3": (5, 3.34), "stats1": (2, 3.40),
        "load": (1, 4.15), "add0": (2, 4.25), "copy3": (5, 5.41), "product0": (3, 5.85), "sum3": (6, 7.89),
        "sum2": (4, 11.61), "turn3": (5, 12.03), "hidden1": (5, 12.25), "relu1": (5, 12.36), "sum1": (3, 13.04),
        "hidden0": (5, 14.69), "var": (0, 15.50), "turn0": (2, 16.38), "root": (0, 16.74), "relu0": (5, 16.94),
        "scale": (0, 17.46), "add3": (5, 17.61), "copy0": (2, 19.70),
    },
    "edge_nodes": {
        "relu1": (6, 1), "turn_n": (5, 2), "apply3": (5, 3), "hidden0": (6, 4), "apply4": (7, 5),
        "part0": (2, 6), "turn3": (5, 7), "sum2": (4, 8), "second": (6, 9), "relu0": (6, 10), "copy_n": (5, 11),
        "sum1": (3, 12), "add3": (6, 13), "turn0": (2, 14), "stats1": (2, 15), "load_a1": (3, 16),
        "sum3": (6, 17), "load_n1": (5, 18), "load": (2, 19), "add0": (2, 20), "copy3": (5, 21),
        "hidden1": (5, 22), "load_a2": (3, 23), "copy0": (2, 24), "load_a4": (5, 25), "var": (0, 26),
        "root": (0, 27), "put_index": (7, 28), "put": (7, 29), "scale": (0, 30), "product0": (2, 31),
    },
}


def gnn_stack(nc, A, out):
    N, E = A["x"].shape[0], A["src"].shape[0]
    NT = -(-E // P)
    NG = -(-NT // GT)
    EP = NG * GE
    assert NT == NG * GT
    NU = -(-NT // UT)
    NUN = -(-N // UE)
    FIRST_NODES = N - (NUN - 1) * UE
    TAIL = E - (NT - 1) * P
    T1 = NT - P
    NHI = -(-N // LO)
    H1 = NHI - P
    NONE_ROW = EP
    CH = EP // 7
    assert CH * 7 == EP
    IDXW = NT + 2 * UT

    def dram(name, shape, dt):
        return nc.dram_tensor(name, shape, dt, kind="Internal").ap()

    dst_lin = dram("dst_lin", [EP + 1, 1], I32)
    cnt_lin = dram("cnt_lin", [NT, P], F32)
    w0_lin = dram("w0_lin", [NT, P], F32)
    node_tab = dram("node_tab", [NHI * LO, 2], I32)
    tabs = {n: dram(f"tab_{n}", [EP + 1, P], F32)
            for n in ("z1", "z2", "z3", "a1", "g1", "g2", "g3", "a2", "n1", "a4")}
    xs = {n: dram(f"xs_{n}", [EP, P], F32) for n in ("x0", "x1", "x2", "x3")}
    x0d = dram("x0d", [EP, P], F32)

    def tiles_in(u):
        return NT - (NU - 1) * UT if isinstance(u.no, int) and u.no == NU - 1 else UT

    def rows(ap, u):
        return ap[bass.ds(u.no * UE, tiles_in(u) * P), :].rearrange("(t p) f -> p t f", p=P)

    def rows_in_value(u):
        return u.half * (16 * UT) + 16 * tiles_in(u)

    with ExitStack() as ctx:
        def sb(name, shape, dt=F32):
            return ctx.enter_context(nc.sbuf_tensor(name, shape, dt))

        def lanes(name, shape, dt=F32):
            return [sb(f"{name}_{l}", shape, dt) for l in range(2)]

        wide = [ctx.enter_context(nc.psum_tensor(f"wide{b}", [P, 1024], F32)) for b in range(4)]
        bank = [wide[b // 2][:, (b % 2) * 512:(b % 2 + 1) * 512] for b in range(8)]

        ident = sb("ident", [P, P])
        ones_col = sb("ones_col", [P, 1])
        ones_mat = sb("ones_mat", [P, P])
        eps_col = sb("eps_col", [P, 1])
        zero_bf = sb("zero_bf", [P, LO], BF16)
        zero_f = sb("zero_f", [P, P])
        w = {n: sb(f"w_{n}", [P, P]) for n in
             ("L0_gnn_W1", "L0_gnn_W2", "L0_gnn_W3", "L2_gnn_W1", "L2_gnn_W2", "L2_gnn_W3", "L2_gnn_W4",
              "L1_gnn_w_neigh", "L1_gnn_w_self")}
        wnT = sb("wnT", [P, P])
        wsI = sb("wsI", [P, P])
        wsC = sb("wsC", [P, P])
        w4C = sb("w4C", [P, P])
        b4C = sb("b4C", [P, P])
        mean_mat = sb("mean_mat", [P, P])
        row_mean = sb("row_mean", [P, 2])
        ws1 = sb("ws1", [P, 2 * P])
        wn1 = sb("wn1", [P, 2 * P])
        ws2 = sb("ws2", [P, 2, P])
        wn2 = sb("wn2", [P, 2, P])
        row = {n: sb(f"r_{n}", [P, P]) for n in
               ("L1_gnn_b_self", "L2_gnn_b1", "L2_gnn_b2", "L2_gnn_b3", "L2_gnn_b4", "L2_gnn_gamma", "L2_gnn_beta",
                "L3_gnn_b2")}
        a3_row = sb("a3_row", [P, P])
        c3_row = sb("c3_row", [P, P])
        a2_row = sb("a2_row", [P, P])
        none_rows = sb("none_rows", [P, 4, P])
        gam_col = sb("gam_col", [P, 1])
        bet_col = sb("bet_col", [P, 1])
        b1_col = sb("b1_col", [P, 2])
        bn_a = sb("bn_a", [P, 1])
        bn_c = sb("bn_c", [P, 1])
        bn_na = sb("bn_na", [P, 1])
        bn_nc = sb("bn_nc", [P, 1])
        bn_t = sb("bn_t", [P, 8])
        raw = [sb(f"raw_{p}", [P, UT, P]) for p in range(2)]
        diag = sb("diag", [P, 2, P])

        same = sb("same", [P, EP], BF16)
        src_idx = sb("src_idx", [P, IDXW], I32)
        slot_idx = sb("slot_idx", [P, IDXW], I32)
        dst_idx = sb("dst_idx", [P, IDXW], I32)
        put_idx = sb("put_idx", [P, IDXW], I32)
        w0_c = sb("w0_c", [P, NT])
        nsrc_c = sb("nsrc_c", [P, NT])
        rdeg_c = sb("rdeg_c", [P, NT])
        nd_c = sb("nd_c", [P, NT])
        ndrep_c = sb("ndrep_c", [P, NT])
        rep_c = sb("rep_c", [P, NT])
        dst_c = sb("dst_c", [P, NT])
        ew_c = sb("ew_c", [P, NT])

        S = Signals(nc)

        with ExitStack() as scratch:
            def tmp(name, shape, dt=F32):
                return scratch.enter_context(nc.sbuf_tensor(name, shape, dt))

            src_t = tmp("src_t", [P, 2, P], I32)
            dst_t = tmp("dst_t", [P, 2, P], I32)
            nxt_t = tmp("nxt_t", [P, 2, P], I32)
            edge_f = tmp("edge_f", [P, 4, 2, P])
            nxt_f = tmp("nxt_f", [P, 2, P])
            with nc.Block() as block:
                @block.sync
                def _(sp):
                    sp.wait_ge(S("cleared"), 4)
                    n0 = P * P
                    for t, a, off in ((src_t, A["src"], 0), (dst_t, A["dst"], 0), (nxt_t, A["dst"], 1),
                                      (edge_f[:, 3], A["edge_weight"], 0)):
                        full = (T1 - 1) * P
                        sp.dma_start(t[:, 0, :], a[off:off + n0].rearrange("(t e) -> t e", e=P)
                                     ).then_inc(S("edges_in"), 16)
                        sp.dma_start(t[0:T1 - 1, 1, :], a[off + n0:off + n0 + full].rearrange("(t e) -> t e", e=P)
                                     ).then_inc(S("edges_in"), 16)
                        sp.dma_start(t[T1 - 1:T1, 1, 0:TAIL - off], a[off + n0 + full:E].rearrange("(t e) -> t e", t=1)
                                     ).then_inc(S("edges_in"), 16)
                    sp.wait_ge(S("edges_in"), 12 * 16)
                    body = dst_lin[1:EP + 1, :].rearrange("(t e) o -> t (e o)", e=P)
                    sp.dma_start(body[0:P, :], dst_t[:, 0, :]).then_inc(S("dst_out"), 16)
                    sp.dma_start(body[P:NT, :], dst_t[0:T1, 1, :]).then_inc(S("dst_out"), 16)
                    sp.dma_start(dst_lin[0:1, :], dst_t[T1:T1 + 1, 1, 0:1]).then_inc(S("dst_out"), 16)
                    sp.wait_ge(S("dst_out"), 48)

                @block.scalar
                def _(act):
                    for n in w:
                        act.dma_start(w[n][:, :], A[n]).then_inc(S("weights_in"), 16)
                    act.dma_start(ws1[:, :], A["L3_gnn_w_self1"]).then_inc(S("weights_in"), 16)
                    act.dma_start(wn1[:, :], A["L3_gnn_w_neigh1"]).then_inc(S("weights_in"), 16)
                    act.dma_start(ws2[:, :, :], A["L3_gnn_w_self2"].rearrange("(c p) f -> p c f", p=P)
                                  ).then_inc(S("weights_in"), 16)
                    act.dma_start(wn2[:, :, :], A["L3_gnn_w_neigh2"].rearrange("(c p) f -> p c f", p=P)
                                  ).then_inc(S("weights_in"), 16)
                    for n in row:
                        act.dma_start(row[n][:, :], A[n].rearrange("(o f) -> o f", o=1).broadcast_to([P, P])
                                      ).then_inc(S("weights_in"), 16)
                    act.dma_start(gam_col[:, :], A["L0_gnn_gamma"].rearrange("(p o) -> p o", o=1)
                                  ).then_inc(S("weights_in"), 16)
                    act.dma_start(bet_col[:, :], A["L0_gnn_beta"].rearrange("(p o) -> p o", o=1)
                                  ).then_inc(S("weights_in"), 16)
                    for c in range(2):
                        act.dma_start(b1_col[:, c:c + 1], A["L3_gnn_b1"][c * P:(c + 1) * P].rearrange("(p o) -> p o", o=1)
                                      ).then_inc(S("weights_in"), 16)
                    n_in = (len(w) + 4 + len(row) + 4) * 16
                    act.wait_ge(S("weights_in"), n_in)
                    act.sem_inc(S("weights_ready"), 1)

                @block.gpsimd
                def _(pool):
                    pool.memset(src_t[:, :, :], 0).then_inc(S("cleared"), 1)
                    pool.memset(dst_t[:, :, :], -1).then_inc(S("cleared"), 1)
                    pool.memset(nxt_t[:, :, :], -1).then_inc(S("cleared"), 1)
                    pool.memset(edge_f[:, 3], 0.0).then_inc(S("cleared"), 1)
                    pool.memset(ident[:, :], 0.0).then_inc(S("ident_zero"), 1)
                    pool.wait_ge(S("ident_zero"), 1)
                    pool.affine_select(out=ident[:, :], in_=ident[:, :], compare_op=ALU.not_equal, fill=1.0, base=0,
                                       pattern=[[-1, P]], channel_multiplier=1).then_inc(S("ident_ready"), 1)

                @block.vector
                def _(dve):
                    dve.memset(ones_col[:, :], 1.0)
                    dve.memset(ones_mat[:, :], 1.0)
                    dve.memset(mean_mat[:, :], 1.0 / P).then_inc(S("mean_mat_ready"), 1)
                    dve.memset(eps_col[:, :], EPS)
                    dve.memset(zero_f[:, :], 0.0)
                    dve.memset(zero_bf[:, :], 0.0)
                    dve.memset(src_idx[:, :], 0).then_inc(S("idx_zero"), 1)
                    dve.memset(slot_idx[:, :], 0)
                    dve.memset(dst_idx[:, :], 0)
                    dve.memset(put_idx[:, :], 0).then_inc(S("idx_zero"), 1)
                    dve.wait_ge(S("edges_in"), 12 * 16)
                    dve.tensor_copy(edge_f[:, 0], src_t[:, :, :])
                    dve.tensor_copy(edge_f[:, 1], dst_t[:, :, :]).then_inc(S("as_float"), 1)
                    dve.tensor_copy(nxt_f[:, :, :], nxt_t[:, :, :]).then_inc(S("as_float"), 1)
                    dve.wait_ge(S("as_float"), 2)
                    dve.tensor_tensor(edge_f[:, 2], edge_f[:, 1], nxt_f[:, :, :], ALU.not_equal
                                      ).then_inc(S("edges_float"), 1)
                    dve.wait_ge(S("turned"), 1)
                    dve.wait_ge(S("idx_zero"), 2)
                    dve.tensor_copy(src_idx[:, 0:NT], bank[0][:, 0:NT])
                    dve.tensor_copy(dst_c[:, :], bank[1][:, 0:NT])
                    dve.tensor_copy(rep_c[:, :], bank[2][:, 0:NT])
                    dve.tensor_copy(ew_c[:, :], bank[3][:, 0:NT])
                    dve.tensor_copy(wnT[:, :], bank[4][:, 0:P])
                    dve.tensor_tensor(wsI[:, :], bank[4][:, P:2 * P], ident[:, :], ALU.add
                                      ).then_inc(S("wsI_ready"), 1)
                    dve.wait_ge(S("weights_ready"), 1)
                    dve.tensor_reduce(row_mean[:, 0:1], w["L2_gnn_W4"][:, :], mybir.AxisListType.X, ALU.add)
                    dve.tensor_reduce(row_mean[:, 1:2], row["L2_gnn_b4"][:, :], mybir.AxisListType.X, ALU.add
                                      ).then_inc(S("sums_ready"), 1)
                    dve.wait_ge(S("sums_ready"), 1)
                    dve.tensor_scalar(row_mean[:, :], row_mean[:, :], 1.0 / P, None, ALU.mult
                                      ).then_inc(S("sums_ready"), 1)
                    dve.wait_ge(S("sums_ready"), 2)
                    dve.tensor_scalar(w4C[:, :], w["L2_gnn_W4"][:, :], row_mean[:, 0:1], None, ALU.subtract)
                    dve.tensor_scalar(b4C[:, :], row["L2_gnn_b4"][:, :], row_mean[:, 1:2], None, ALU.subtract)
                    dve.wait_ge(S("col_means"), 1)
                    dve.tensor_tensor(wsC[:, :], wsI[:, :], bank[5][:, 0:P], ALU.subtract)

                @block.tensor
                def _(pe):
                    pe.wait_ge(S("ident_ready"), 1)
                    pe.wait_ge(S("weights_ready"), 1)
                    pe.transpose(bank[4][:, 0:P], w["L1_gnn_w_neigh"][:, :], ident[:, :])
                    pe.transpose(bank[4][:, P:2 * P], w["L1_gnn_w_self"][:, :], ident[:, :])
                    pe.wait_ge(S("edges_float"), 1)
                    for n in range(4):
                        pe.transpose(bank[n][:, 0:P], edge_f[:, n, 0, :], ident[:, :])
                        last = pe.transpose(bank[n][:, P:NT], edge_f[0:T1, n, 1, :], ident[0:T1, 0:T1])
                    last.then_inc(S("turned"), 1)
                    pe.wait_ge(S("mean_mat_ready"), 1)
                    pe.wait_ge(S("wsI_ready"), 1)
                    pe.matmul(bank[5][:, 0:P], mean_mat[:, :], wsI[:, :], start=True, stop=True
                              ).then_inc(S("col_means"), 1)
            S.close()

        with ExitStack() as scratch:
            def tmp(name, shape, dt=F32):
                return scratch.enter_context(nc.sbuf_tensor(name, shape, dt))

            chunk = [tmp(f"chunk_{l}", [P, CH + 1], I32) for l in range(2)]
            ones_row = tmp("ones_row", [1, CH])
            cnt = [tmp(f"cnt_{l}", [1, CH]) for l in range(2)]
            cnt_t = tmp("cnt_t", [P, 2, P])
            with nc.Block() as block:
                @block.sync
                def _(sp):
                    def load(c):
                        l = c % 2
                        if c >= 2:
                            sp.wait_ge(S("mask_ready"), c - 1)
                        sp.dma_start(chunk[l][:, :], dst_lin[c * CH:(c + 1) * CH + 1, :].rearrange("e o -> o e")
                                     .broadcast_to([P, CH + 1])).then_inc(S("chunk_in", l), 16)

                    load(0)
                    load(1)
                    for c in range(7):
                        sp.wait_ge(S("count_ready"), c + 1)
                        sp.dma_start(cnt_lin.rearrange("t e -> (t e)")[c * CH:(c + 1) * CH].rearrange("(o e) -> o e", o=1),
                                     cnt[c % 2][:, :]).then_inc(S("count_out", c % 2), 16)
                        if c + 2 < 7:
                            load(c + 2)
                    sp.wait_ge(S("count_out", 0), 4 * 16)
                    sp.wait_ge(S("count_out", 1), 3 * 16)
                    sp.dma_start(cnt_t[:, 0, :], cnt_lin[0:P, :]).then_inc(S("count_in"), 16)
                    sp.dma_start(cnt_t[0:T1, 1, :], cnt_lin[P:NT, :]).then_inc(S("count_in"), 16)

                @block.vector
                def _(dve):
                    dve.memset(ones_row[:, :], 1.0)
                    for c in range(7):
                        l = c % 2
                        part = slice(c * CH, (c + 1) * CH)
                        dve.wait_ge(S("chunk_in", l), 16 * (c // 2 + 1))
                        dve.tensor_tensor(same[:, part], chunk[l][:, 1:CH + 1], chunk[l][:, 0:CH], ALU.is_equal
                                          ).then_inc(S("mask_ready"), 1)
                        dve.wait_ge(S("mask_ready"), c + 1)
                        if c:
                            dve.wait_ge(S("count_ready"), c)
                        if c >= 2:
                            dve.wait_ge(S("count_out", l), 16 * (c // 2))
                        dve.tensor_tensor_scan(cnt[l][:, :], same[0:1, part], ones_row[:, :],
                                               cnt[1 - l][:, CH - 1:CH] if c else 0.0, ALU.mult, ALU.add
                                               ).then_inc(S("count_ready"), 1)
                    dve.wait_ge(S("turned"), 1)
                    dve.reciprocal(rdeg_c[:, :], bank[0][:, 0:NT]).then_inc(S("rdeg_ready"), 1)
                    dve.wait_ge(S("nd_ready"), 1)
                    dve.tensor_tensor(ndrep_c[:, :], nd_c[:, :], rep_c[:, :], ALU.mult)

                @block.tensor
                def _(pe):
                    pe.wait_ge(S("count_in"), 32)
                    pe.transpose(bank[0][:, 0:P], cnt_t[:, 0, :], ident[:, :])
                    pe.transpose(bank[0][:, P:NT], cnt_t[0:T1, 1, :], ident[0:T1, 0:T1]).then_inc(S("turned"), 1)

                @block.scalar
                def _(act):
                    act.wait_ge(S("rdeg_ready"), 1)
                    act.activation(nd_c[:, :], rdeg_c[:, :], ACT.Sqrt).then_inc(S("nd_ready"), 1)
            S.close()

        with ExitStack() as scratch:
            def tmp(name, shape, dt=F32):
                return scratch.enter_context(nc.sbuf_tensor(name, shape, dt))

            iota_i = tmp("iota_i", [P, LO], I32)
            iota_h = tmp("iota_h", [P, LO], F16)
            tile_no = tmp("tile_no", [P, NT], I32)
            lane_no = tmp("lane_no", [P, NT], I32)
            tile_w = tmp("tile_w", [P, NT])
            lane_w = tmp("lane_w", [P, NT])
            bits = tmp("bits", [P, 4, NT], I32)
            part = tmp("part", [P, 4, NT])
            dst_i = tmp("dst_i", [P, NT], I32)
            hot = [tmp(f"hot_{l}", [P, 3, 2 * P], BF16) for l in range(2)]
            low = [tmp(f"low_{l}", [P, 2, LO], BF16) for l in range(2)]
            place = [tmp(f"place_{h}", [P, LO]) for h in range(2)]
            empty = [tmp(f"empty_{h}", [P, LO]) for h in range(2)]
            tab = [tmp(f"tab_{h}", [P, LO, 2], I32) for h in range(2)]
            idx8 = [tmp(f"idx8n_{p}", [P, UT], I32) for p in range(2)]
            f0 = tmp("f0", [P, NT])
            hi_rows = (P, H1)
            with nc.Block() as block:
                @block.gpsimd
                def _(pool):
                    pool.iota(iota_i[:, :], pattern=[[1, LO]], base=0, channel_multiplier=0).then_inc(S("iota_ready"), 1)
                    pool.iota(tile_no[:, :], pattern=[[1, NT]], base=1, channel_multiplier=0).then_inc(S("iota_ready"), 1)
                    pool.iota(lane_no[:, :], pattern=[[0, NT]], base=0, channel_multiplier=1).then_inc(S("iota_ready"), 1)

                @block.vector
                def _(dve):
                    chain = Chain(dve, S("dve_step"))
                    dve.wait_ge(S("iota_ready"), 3)
                    dve.tensor_copy(iota_h[:, :], iota_i[:, :])
                    dve.tensor_tensor(tile_w[:, :], tile_no[:, :], rep_c[:, :], ALU.mult)
                    dve.tensor_tensor(lane_w[:, :], lane_no[:, :], rep_c[:, :], ALU.mult)
                    chain.step(dve.tensor_copy(dst_i[:, :], dst_c[:, :]))
                    chain.wait()
                    for n, i in ((0, src_idx[:, 0:NT]), (2, dst_i[:, :])):
                        dve.tensor_scalar(bits[:, n, :], i, 9, None, ALU.arith_shift_right)
                        chain.step(dve.tensor_scalar(bits[:, n + 1, :], i, LO - 1, None, ALU.bitwise_and))
                    chain.wait()
                    chain.step(dve.tensor_copy(part[:, :, :], bits[:, :, :]))
                    chain.step(dve.tensor_scalar(f0[:, :], dst_c[:, :], -float(ABSENT), None, ALU.add))
                    chain.wait()
                    chain.step(dve.tensor_tensor(f0[:, :], f0[:, :], rep_c[:, :], ALU.mult))
                    chain.wait()
                    dve.tensor_scalar(put_idx[:, 0:NT], f0[:, :], float(ABSENT), None, ALU.add)
                    chain.step(dve.tensor_scalar(dst_idx[:, 0:NT], dst_c[:, :], 0.0, None, ALU.max))
                    chain.wait()

                    def one_hot(i):
                        for l in range(2):
                            t = i * 2 + l
                            if not first(i):
                                dve.wait_ge(S("counted", l), i)
                            col = [part[:, n, bass.ds(t, 1)] for n in range(4)]
                            dve.tensor_scalar(hot[l][:, 0, :], iota_h[:, 0:2 * P], col[0], None, ALU.is_equal)
                            dve.tensor_scalar(low[l][:, 0, :], iota_h[:, :], col[1], None, ALU.is_equal)
                            dve.tensor_scalar(hot[l][:, 1, :], iota_h[:, 0:2 * P], col[2], tile_w[:, bass.ds(t, 1)],
                                              ALU.is_equal, ALU.mult)
                            dve.tensor_scalar(hot[l][:, 2, :], iota_h[:, 0:2 * P], col[2], lane_w[:, bass.ds(t, 1)],
                                              ALU.is_equal, ALU.mult)
                            dve.tensor_scalar(low[l][:, 1, :], iota_h[:, :], col[3], None, ALU.is_equal
                                              ).then_inc(S("hot_ready", l), 1)

                    one_hot(0)
                    with dve.Fori(1, NT // 2) as i:
                        one_hot(i)
                    dve.wait_ge(S("all_counted"), 1)
                    for h in range(2):
                        chain.step(dve.tensor_copy(place[h][:, :], bank[4 + h][:, :]))
                    chain.wait()
                    for h in range(2):
                        chain.step(dve.scalar_tensor_tensor(place[h][:, :], bank[2 + h][:, :], float(P), place[h][:, :],
                                                            ALU.mult, ALU.add))
                    chain.wait()
                    for h in range(2):
                        chain.step(dve.tensor_scalar(empty[h][:, :], place[h][:, :], 0.0, float(NONE_ROW + P),
                                                     ALU.is_equal, ALU.mult))
                    chain.wait()
                    for h in range(2):
                        dve.scalar_tensor_tensor(tab[h][:, :, 0], place[h][:, :], -float(P), empty[h][:, :],
                                                 ALU.add, ALU.add)
                        dve.tensor_copy(tab[h][:, :, 1], bank[h][:, :]).then_inc(S("tab_ready"), 1)

                @block.tensor
                def _(pe):
                    for b in range(6):
                        pe.matmul(bank[b][:, :], zero_bf[:, 0:P], zero_bf[:, :], start=True, stop=False,
                                  skip_group_check=True)

                    def count(i):
                        for l in range(2):
                            pe.wait_ge(S("hot_ready", l), i + 1)
                            for n in range(3):
                                for h in range(2):
                                    last = pe.matmul(bank[2 * n + h][:, :], hot[l][:, n, h * P:(h + 1) * P],
                                                     low[l][:, min(n, 1), :], start=False, stop=False,
                                                     skip_group_check=True)
                            last.then_inc(S("counted", l), 1)

                    with pe.Fori(0, NT // 2) as i:
                        count(i)
                    for b in range(6):
                        last = pe.matmul(bank[b][:, :], zero_bf[:, 0:P], zero_bf[:, :], start=False, stop=True,
                                         skip_group_check=True)
                    last.then_inc(S("all_counted"), 1)

                @block.sync
                def _(sp):
                    def store_x(u):
                        sp.wait_ge(S("xs_in", u.parity), rows_in_value(u))
                        hold(sp, S)
                        sp.dma_start(rows(xs["x0"], u), raw[u.parity][:, 0:tiles_in(u), :]
                                     ).then_inc(S("xs_out", u.parity), 16)

                    run(sp, NU, ((store_x, 0, 0, NU),))
                    sp.wait_ge(S("xs_out", 0), 16 * (NU // 2 + NU % 2))
                    sp.wait_ge(S("xs_out", 1), 16 * (NU // 2))
                    sp.wait_ge(S("tab_ready"), 2)
                    nt = node_tab.rearrange("(h o) c -> h (o c)", o=LO)
                    sp.dma_start(nt[0:P, :], tab[0][:, :, :].rearrange("p o c -> p (o c)")).then_inc(S("tab_out"), 16)
                    sp.dma_start(nt[P:NHI, :], tab[1][0:H1, :, :].rearrange("p o c -> p (o c)")).then_inc(S("tab_out"), 16)
                    sp.wait_ge(S("tab_out"), 32)

                @block.gpsimd
                def _(pool):
                    def index_x(u):
                        need(pool, S("xs_out", u.parity), u.half * 16)
                        pool.tensor_copy(idx8[u.parity][:, :], src_idx[:, bass.ds(u.no * UT, UT)]
                                         ).then_inc(S("xs_index"), 1)

                    def fetch_x(u):
                        pool.wait_ge(S("xs_index"), u.done)
                        pool.sem_inc(S("fetching_x"), 1)
                        for j in range(tiles_in(u)):
                            pool.indirect_dma_start(
                                out=raw[u.parity][:, j, :], out_offset=None, in_=A["x"],
                                in_offset=bass.IndirectOffsetOnAxis(ap=idx8[u.parity][:, j:j + 1], axis=0)
                            ).then_inc(S("xs_in", u.parity), 16)

                    run(pool, NU, ((index_x, 0, 0, NU), (fetch_x, 0, 0, NU)))
            S.close()

        def wide_sb(name, n=1):
            return [sb(f"{name}_{p}", [P, UT, P]) for p in range(n)] if n > 1 else sb(name, [P, UT, P])

        def flat(t, nt=UT):
            return t[:, 0:nt, :].rearrange("p t f -> p (t f)")

        def tiles(ps, nt=UT):
            return ps[:, 0:nt * P].rearrange("p (t f) -> p t f", f=P)

        def over(r, nt=UT):
            return r[:, :].rearrange("p (o f) -> p o f", o=1).broadcast_to([P, nt, P])

        psA, psB0, psB1, psH = wide

        idx8 = [sb(f"idx8_{p}", [P, UT], I32) for p in range(2)]
        put8 = sb("put8", [P, UT], I32)
        xinh = wide_sb("xinh", 2)
        uh = wide_sb("uh")
        xnew = wide_sb("xnew", 2)
        scaled = wide_sb("scaled")
        agg = wide_sb("agg", 2)
        outr = wide_sb("outr", 2)
        sq = wide_sb("sq")
        sq2 = wide_sb("sq2")
        n_xin = wide_sb("n_xin")
        n_u0 = wide_sb("n_u0")
        n_xT = wide_sb("n_xT")
        n_u1 = wide_sb("n_u1")
        n_u2 = wide_sb("n_u2")
        n_x3 = wide_sb("n_x3")
        n_x3b = wide_sb("n_x3b")
        n_x3T = wide_sb("n_x3T")
        n_hT = [wide_sb("n_hT0"), wide_sb("n_hT1")]
        n_u3 = wide_sb("n_u3")
        z_sum, sq_sum = n_hT
        n_out = wide_sb("n_out")
        got8 = [sb(f"got8_{p}", [P, UT, 2], I32) for p in range(2)]
        deg8 = sb("deg8", [P, UT])
        deg8b = sb("deg8b", [P, UT])
        rdeg8 = sb("rdeg8", [P, UT])
        nsrc8 = sb("nsrc8", [P, UT])
        dst2 = [sb(f"dst2_{p}", [P, DT], I32) for p in range(2)]
        xdst = [sb(f"xdst_{p}", [P, DT, P]) for p in range(2)]
        w0_t = sb("w0_t", [P, 2, P])

        class Norm:

            def __init__(self, name):
                self.name = name
                self.st = sb(f"{name}_st", [P, UT, 6])
                self.mv = sb(f"{name}_mv", [P, 5, UT])
                self.sd = sb(f"{name}_sd", [P, UT])
                self.rs = sb(f"{name}_rs", [P, UT])
                self.nm = sb(f"{name}_nm", [P, UT])

            def stats(self, dve, Q, u, src, nt=UT):
                st, mv = self.st, self.mv
                for j in range(nt):
                    last = dve.bn_stats(st[:, j, :], src[:, j, :])
                last.then_inc(Q(f"{self.name}_stats"), 1)
                dve.wait_ge(Q(f"{self.name}_stats"), u.done)
                dve.tensor_tensor(mv[:, 0, 0:nt], st[:, 0:nt, 1], st[:, 0:nt, 4], ALU.add)
                dve.tensor_tensor(mv[:, 1, 0:nt], st[:, 0:nt, 1], st[:, 0:nt, 4], ALU.subtract
                                  ).then_inc(Q(f"{self.name}_gap"), 1)
                dve.tensor_tensor(mv[:, 2, 0:nt], st[:, 0:nt, 2], st[:, 0:nt, 5], ALU.add)
                dve.wait_ge(Q(f"{self.name}_gap"), u.done)
                dve.scalar_tensor_tensor(mv[:, 3, 0:nt], mv[:, 1, 0:nt], P / 4.0, mv[:, 1, 0:nt], ALU.mult, ALU.mult
                                         ).then_inc(Q(f"{self.name}_gap2"), 1)
                dve.wait_ge(Q(f"{self.name}_gap2"), u.done)
                dve.tensor_tensor(mv[:, 4, 0:nt], mv[:, 3, 0:nt], mv[:, 2, 0:nt], ALU.add
                                  ).then_inc(Q(f"{self.name}_var"), 1)

            def root(self, act, Q, u, nt=UT):
                need(act, Q(f"{self.name}_scale"), u.done - 1)
                act.wait_ge(Q(f"{self.name}_var"), u.done)
                act.activation(self.sd[:, 0:nt], self.mv[:, 4, 0:nt], ACT.Sqrt, bias=eps_col[:, :], scale=1.0 / P
                               ).then_inc(Q(f"{self.name}_root"), 1)

            def scale(self, dve, Q, u, nt=UT, shift=True):
                dve.wait_ge(Q(f"{self.name}_root"), u.done)
                if not shift:
                    dve.reciprocal(self.rs[:, 0:nt], self.sd[:, 0:nt]).then_inc(Q(f"{self.name}_scale"), 1)
                    return
                dve.reciprocal(self.rs[:, 0:nt], self.sd[:, 0:nt]).then_inc(Q(f"{self.name}_rs"), 1)
                dve.wait_ge(Q(f"{self.name}_rs"), u.done)
                dve.scalar_tensor_tensor(self.nm[:, 0:nt], self.mv[:, 0, 0:nt], -0.5, self.rs[:, 0:nt],
                                         ALU.mult, ALU.mult).then_inc(Q(f"{self.name}_scale"), 1)

            def apply(self, act, Q, u, src, dst, done, nt=UT):
                act.wait_ge(Q(f"{self.name}_scale"), u.done)
                for j in range(nt):
                    last = act.activation(dst[:, j, :], src[:, j, :], ACT.Identity, bias=self.nm[:, j:j + 1],
                                          scale=self.rs[:, j:j + 1])
                last.then_inc(Q(done), 1)

        norm_h, norm_p = Norm("nh"), Norm("np")
        n_st = sb("n_st", [P, 4 * UT, 6])
        n_mv = sb("n_mv", [P, 5, 4 * UT])
        n_sd = sb("n_sd", [P, 4 * UT])
        n_rs = [sb(f"n_rs{p}", [P, 4 * UT]) for p in range(2)]
        n_nm = [sb(f"n_nm{p}", [P, 4 * UT]) for p in range(2)]

        def variances(dve, Q, u, st, mv, name):
            n = mv.shape[-1]
            dve.tensor_tensor(mv[:, 0, :], st[:, 0:n, 1], st[:, 0:n, 4], ALU.add)
            dve.tensor_tensor(mv[:, 1, :], st[:, 0:n, 1], st[:, 0:n, 4], ALU.subtract).then_inc(Q(f"{name}_gap"), 1)
            dve.tensor_tensor(mv[:, 2, :], st[:, 0:n, 2], st[:, 0:n, 5], ALU.add)
            dve.wait_ge(Q(f"{name}_gap"), u.done)
            dve.scalar_tensor_tensor(mv[:, 3, :], mv[:, 1, :], P / 4.0, mv[:, 1, :], ALU.mult, ALU.mult
                                     ).then_inc(Q(f"{name}_gap2"), 1)
            dve.wait_ge(Q(f"{name}_gap2"), u.done)
            dve.tensor_tensor(mv[:, 4, :], mv[:, 3, :], mv[:, 2, :], ALU.add).then_inc(Q(f"{name}_var"), 1)

        def turn_over(pe, dst, src, nt=UT):
            for j in range(nt):
                last = pe.transpose(dst[:, j * P:(j + 1) * P], src[:, j, :], ident[:, :])
            return last

        def products(pe, dst, lhs, rhs, nt=UT):
            for j in range(nt):
                last = pe.matmul(dst[:, j * P:(j + 1) * P], lhs[:, j, :], rhs, start=True, stop=True)
            return last

        def halves(nt):
            return [(b * GE, GE) for b in range(nt * P // GE)]

        class Hop:
            def __init__(self, name, front, weight, post, dest, table=None, idx=None, x_from=None, x_to=None,
                         col=None, bias=None, none=None, apart=True):
                self.name, self.front, self.weight, self.post, self.dest = name, front, weight, post, dest
                self.table, self.idx, self.x_from, self.x_to = table, idx, x_from, x_to
                self.col, self.bias, self.none = col, bias, none
                self.Q = S.named(name)
                self.ln = front in ("ln_bn", "ln_self", "ln_add")
                self.plan = PLAN[front, post, apart]
                self.raw_read = {"weight": "scaled", "ln_self": "psU_used"}.get(front, "raw_used")
                self.xin_read = {"weight": "scaled", "ln_add": "raw_used"}.get(front, "xin_used")
                self.psZ_read = "psZ_used" if post in ("gelu", "affine") else "out_ready"
                self.psT = psA if apart else psH
                self.alone = apart

            def index(self, pool, u):
                Q, p = self.Q, u.parity
                need(pool, Q("rows_in", p), u.half * (16 * UT))
                pool.tensor_copy(idx8[p][:, :], self.idx[:, bass.ds(u.no * UT, UT)]).then_inc(Q("index"), 1)

            def gather(self, pool, u):
                Q, p = self.Q, u.parity
                need(pool, Q(self.raw_read), u.done - 2)
                pool.wait_ge(Q("index"), u.done)
                hold(pool, Q)
                for j in range(tiles_in(u)):
                    pool.indirect_dma_start(
                        out=raw[p][:, j, :], out_offset=None, in_=self.table,
                        in_offset=bass.IndirectOffsetOnAxis(ap=idx8[p][:, j:j + 1], axis=0)
                    ).then_inc(Q("rows_in", p), 16)

            def pool_steps(self, pool):
                def slot_index(u):
                    need(pool, self.Q("slots_in", u.parity), u.half * (16 * UT))
                    pool.tensor_copy(idx8[u.parity][:, :], src_idx[:, bass.ds(u.no * UT, UT)]
                                     ).then_inc(self.Q("slot_index"), 1)

                def slot_gather(u):
                    need(pool, self.Q("slots_kept"), u.done - 2)
                    pool.wait_ge(self.Q("slot_index"), u.done)
                    hold(pool, self.Q)
                    for j in range(tiles_in(u)):
                        pool.indirect_dma_start(
                            out=got8[u.parity][:, j, :], out_offset=None, in_=node_tab,
                            in_offset=bass.IndirectOffsetOnAxis(ap=idx8[u.parity][:, j:j + 1], axis=0)
                        ).then_inc(self.Q("slots_in", u.parity), 16)

                def shift(u):
                    nt, p = tiles_in(u), u.parity
                    pool.wait_ge(self.Q("normed"), u.done)
                    need(pool, self.Q("out_out", p), u.half * 16)
                    pool.tensor_tensor(outr[p][:, 0:nt, :], sq2[:, 0:nt, :], over(row["L2_gnn_beta"], nt), ALU.add
                                       ).then_inc(self.Q("out_ready"), 1)

                return {"index": lambda u: self.index(pool, u), "gather": lambda u: self.gather(pool, u),
                        "shift": shift, "slot_index": slot_index, "slot_gather": slot_gather}

            def load(self, sp, u):
                Q, p, nt = self.Q, u.parity, tiles_in(u)
                if self.x_from is not None:
                    need(sp, Q(self.xin_read), u.done - 2)
                    hold(sp, Q)
                    sp.dma_start(xinh[p][:, 0:nt, :], rows(self.x_from, u)).then_inc(Q("x_in", p), 16)
                if self.front == "bn_elu":
                    need(sp, Q("message"), u.done - 2)
                    to = (n_x3, n_x3b)[p]
                    hold(sp, Q)
                    sp.dma_start(flat(to, nt), w0_lin.rearrange("t e -> (t e)")[bass.ds(u.no * UE, nt * P)]
                                 .rearrange("(o e) -> o e", o=1).broadcast_to([P, nt * P])
                                 ).then_inc(Q("w0_in", p), 16)

            def store_x(self, sp, u):
                Q = self.Q
                sp.wait_ge(Q("x_done"), u.done)
                hold(sp, Q)
                sp.dma_start(rows(self.x_to, u), xnew[u.parity][:, 0:tiles_in(u), :]
                             ).then_inc(Q("x_out", u.parity), 16)

            def store(self, sp, u):
                Q, p = self.Q, u.parity
                sp.wait_ge(Q("out_ready"), u.done)
                hold(sp, Q)
                sp.dma_start(rows(self.dest, u), outr[p][:, 0:tiles_in(u), :]).then_inc(Q("out_out", p), 16)

            def sp_steps(self, sp):
                return {"load": lambda u: self.load(sp, u), "store_x": lambda u: self.store_x(sp, u),
                        "store": lambda u: self.store(sp, u)}

            def stored(self, eng):
                Q = self.Q
                eng.wait_ge(Q("out_out", 0), 16 * (NU - NU // 2))
                eng.wait_ge(Q("out_out", 1), 16 * (NU // 2))
                if self.x_to is not None:
                    eng.wait_ge(Q("x_out", 0), 16 * (NU - NU // 2))
                    eng.wait_ge(Q("x_out", 1), 16 * (NU // 2))
                if self.none is not None:
                    eng.wait_ge(Q("none_out"), 16)

            def pe_steps(self, pe):
                Q, front = self.Q, self.front

                def product(u):
                    nt = tiles_in(u)
                    pe.wait_ge(Q("summed"), u.done)
                    need(pe, Q(self.psZ_read), u.done - 1)
                    if front == "sage":
                        pe.wait_ge(Q("nT_ready"), min(u.done + 1, NU) if isinstance(u.done, int) else u.done + 1)
                    products(pe, psH, agg[u.parity], self.weight, nt).then_inc(Q("product"), 1)

                def turn(u):
                    nt = tiles_in(u)
                    if front == "bn_elu":
                        pe.wait_ge(Q("rows_in", u.parity), rows_in_value(u))
                        need(pe, Q("elu_in"), u.done - 1)
                        turn_over(pe, self.psT, raw[u.parity], nt).then_inc(Q("raw_used"), 1)
                        return
                    pe.wait_ge(Q("scaled" if front in ("weight", "ln_self") else "x_done"), u.done)
                    if self.alone:
                        need(pe, Q("summed"), u.done - 1)
                    else:
                        need(pe, Q(self.psZ_read), u.done - 1)
                    src = scaled if front in ("weight", "ln_self") else xnew[u.parity]
                    turn_over(pe, self.psT, src, nt).then_inc(Q("turned"), 1)

                def self_turn(u):
                    nt = tiles_in(u)
                    pe.wait_ge(Q("x_in", u.parity), u.half * 16 + 16)
                    need(pe, Q("xT_ready"), u.done - 1)
                    turn_over(pe, psB0, xinh[u.parity], nt).then_inc(Q("xin_used"), 1)

                def self_product(u):
                    pe.wait_ge(Q("xT_ready"), u.done)
                    need(pe, Q("psU_used"), u.done - 1)
                    products(pe, psB1, n_xT, wsI[:, :], tiles_in(u)).then_inc(Q("self_done"), 1)

                def sage_turn(u):
                    nt = tiles_in(u)
                    pe.wait_ge(Q("x_in", u.parity), u.half * 16 + 16)
                    need(pe, Q("summed"), u.done - 2)
                    need(pe, Q("xT_ready"), u.done - 1)
                    turn_over(pe, psA, xinh[u.parity], nt).then_inc(Q("xin_used"), 1)
                    pe.wait_ge(Q("rows_in", u.parity), rows_in_value(u))
                    need(pe, Q(self.psZ_read), u.done - 2)
                    turn_over(pe, psH, raw[u.parity], nt).then_inc(Q("raw_used"), 1)

                def sage_hidden(u):
                    nt = tiles_in(u)
                    pe.wait_ge(Q("nT_ready"), u.done)
                    need(pe, Q("hT_ready"), (u.done - 1) * 2)
                    for c, ps in enumerate((psB0, psB1)):
                        for at, n in halves(nt):
                            pe.matmul(ps[:, at:at + n], ws1[:, c * P:(c + 1) * P], flat(n_xT)[:, at:at + n],
                                      start=True, stop=False)
                            last = pe.matmul(ps[:, at:at + n], wn1[:, c * P:(c + 1) * P], flat(n_u1)[:, at:at + n],
                                             start=False, stop=True)
                        last.then_inc(Q("hidden"), 1)

                def sage_message(u):
                    pe.wait_ge(Q("hT_ready"), u.done * 2)
                    pe.wait_ge(Q("xT_ready"), min(u.done + 1, NU) if isinstance(u.done, int) else u.done + 1)
                    for at, n in halves(tiles_in(u)):
                        for c in range(2):
                            last = pe.matmul(psA[:, at:at + n], wn2[:, c, :], flat(n_hT[c])[:, at:at + n],
                                             start=(c == 0), stop=(c == 1))
                    last.then_inc(Q("turned"), 1)

                return {"product": product, "turn": turn, "self_turn": self_turn,
                        "self_product": self_product, "hidden": sage_hidden, "message": sage_message,
                        "sage_turn": sage_turn}

            def act_steps(self, act):
                Q, front, post = self.Q, self.front, self.post

                def scale_rows(u, src, dst, by):
                    for j in range(tiles_in(u)):
                        last = act.activation(dst[:, j, :], src[:, j, :], ACT.Copy, scale=by[:, bass.ds(u.no * UT + j, 1)])
                    return last

                def nsrc_root(u):
                    nt = tiles_in(u)
                    need(act, Q("w0_ready"), u.done - 1)
                    act.wait_ge(Q("rdeg_ready"), u.done)
                    act.activation(nsrc8[:, 0:nt], rdeg8[:, 0:nt], ACT.Sqrt).then_inc(Q("nsrc_root"), 1)

                def weigh(u):
                    if self.table is None:
                        act.wait_ge(Q("x_in", u.parity), u.half * 16 + 16)
                        act.wait_ge(Q("w0_ready"), u.done)
                        src = xinh[u.parity]
                    else:
                        act.wait_ge(Q("rows_in", u.parity), rows_in_value(u))
                        src = raw[u.parity]
                    need(act, Q("turned"), u.done - 1)
                    scale_rows(u, src, scaled, self.col).then_inc(Q("scaled"), 1)

                def new_x(u):
                    need(act, Q("scaled" if front == "ln_self" else "turned"), u.done - 2)
                    if self.x_to is not None:
                        need(act, Q("x_out", u.parity), u.half * 16)
                    norm_h.apply(act, Q, u, uh, xnew[u.parity], "x_done", tiles_in(u))

                def self_copy(u):
                    nt = tiles_in(u)
                    act.wait_ge(Q("xin_used"), u.done)
                    need(act, Q("self_done"), u.done - 1)
                    act.activation(flat(n_xT, nt), psB0[:, 0:nt * P], ACT.Copy).then_inc(Q("xT_ready"), 1)

                def elu_parts(u):
                    nt = tiles_in(u)
                    act.wait_ge(Q("raw_used"), u.done)
                    need(act, Q("message"), u.done - 1)
                    y = self.psT[:, 0:nt * P]
                    act.activation(flat(n_u1, nt), y, ACT.Relu, bias=bn_c[:, :], scale=bn_a[:, :])
                    act.activation(flat(n_u2, nt), y, ACT.Relu, bias=bn_nc[:, :], scale=bn_na[:, :]
                                   ).then_inc(Q("elu_in"), 1)
                    act.wait_ge(Q("elu_in"), u.done)
                    act.activation(flat(n_u3, nt), flat(n_u2, nt), ACT.Exp, scale=-1.0).then_inc(Q("exp_done"), 1)

                def sage_copy(u):
                    nt = tiles_in(u)
                    act.wait_ge(Q("xin_used"), u.done)
                    need(act, Q("hidden"), (u.done - 1) * 2)
                    act.activation(flat(n_xT, nt), psA[:, 0:nt * P], ACT.Copy).then_inc(Q("xT_ready"), 1)
                    act.wait_ge(Q("raw_used"), u.done)
                    act.activation(flat(n_u1, nt), psH[:, 0:nt * P], ACT.Copy).then_inc(Q("nT_ready"), 1)

                def sage_relu(u):
                    nt = tiles_in(u)
                    need(act, Q("turned"), u.done - 1)
                    for c, ps in enumerate((psB0, psB1)):
                        act.wait_ge(Q("hidden"), (u.done - 1) * 2 + c + 1)
                        act.activation(flat(n_hT[c], nt), ps[:, 0:nt * P], ACT.Relu, bias=b1_col[:, c:c + 1]
                                       ).then_inc(Q("hT_ready"), 1)

                def out_rows(u):
                    act.wait_ge(Q("product"), u.done)
                    need(act, Q("out_out", u.parity), u.half * 16)
                    if post == "stats":
                        need(act, Q("sums"), u.done - 2)
                    scale_rows(u, tiles(psH), outr[u.parity], ndrep_c if post == "stats" else rdeg_c
                               ).then_inc(Q("out_ready"), 1)

                def squares(u):
                    nt = tiles_in(u)
                    act.wait_ge(Q("out_ready"), u.done)
                    need(act, Q("sums"), u.done - 1)
                    act.activation(flat(sq, nt), flat(outr[u.parity], nt), ACT.Square).then_inc(Q("squared"), 1)

                def gelu(u):
                    nt = tiles_in(u)
                    act.wait_ge(Q("psZ_used"), u.done)
                    need(act, Q("out_out", u.parity), u.half * 16)
                    act.activation(flat(outr[u.parity], nt), flat(sq, nt), ACT.Gelu).then_inc(Q("out_ready"), 1)

                return {"new_x": new_x, "weigh": weigh, "self_copy": self_copy, "elu_parts": elu_parts,
                        "sage_relu": sage_relu, "sage_copy": sage_copy, "out_rows": out_rows, "gelu": gelu,
                        "squares": squares,
                        "nsrc_root": nsrc_root,
                        "root_h": lambda u: norm_h.root(act, Q, u, tiles_in(u)),
                        "root_p": lambda u: norm_p.root(act, Q, u, tiles_in(u))}

            def dve_steps(self, dve):
                Q, front, post = self.Q, self.front, self.post

                def before_norm(u):
                    nt, p = tiles_in(u), u.parity
                    need(dve, Q("x_done"), u.done - 1)
                    if front == "ln_self":
                        dve.wait_ge(Q("self_done"), u.done)
                        dve.wait_ge(Q("rows_in", p), rows_in_value(u))
                        dve.tensor_tensor(uh[:, 0:nt, :], tiles(psB1, nt), raw[p][:, 0:nt, :], ALU.add
                                          ).then_inc(Q("psU_used"), 1)
                    if front == "ln_add":
                        dve.wait_ge(Q("rows_in", p), rows_in_value(u))
                        dve.wait_ge(Q("x_in", p), u.half * 16 + 16)
                        dve.tensor_tensor(uh[:, 0:nt, :], xinh[p][:, 0:nt, :], raw[p][:, 0:nt, :], ALU.add
                                          ).then_inc(Q("raw_used"), 1)
                    if front == "ln_bn":
                        dve.wait_ge(Q("rows_in", p), rows_in_value(u))
                        dve.tensor_tensor(uh[:, 0:nt, :], raw[p][:, 0:nt, :], over(a3_row, nt), ALU.mult
                                          ).then_inc(Q("raw_used"), 1)
                        dve.wait_ge(Q("raw_used"), u.done)
                        dve.wait_ge(Q("x_in", p), u.half * 16 + 16)
                        dve.tensor_tensor(uh[:, 0:nt, :], uh[:, 0:nt, :], xinh[p][:, 0:nt, :], ALU.add
                                          ).then_inc(Q("xin_used"), 1)
                        dve.wait_ge(Q("xin_used"), u.done)
                        dve.tensor_tensor(uh[:, 0:nt, :], uh[:, 0:nt, :], over(c3_row, nt), ALU.add
                                          ).then_inc(Q("u_ready"), 1)
                        dve.wait_ge(Q("u_ready"), u.done)
                    else:
                        dve.wait_ge(Q(self.raw_read), u.done)
                    norm_h.stats(dve, Q, u, uh, nt)

                def scale_x(u):
                    nt = tiles_in(u)
                    dve.wait_ge(Q("x_done"), u.done)
                    need(dve, Q("turned"), u.done - 1)
                    for j in range(nt):
                        last = dve.tensor_scalar(scaled[:, j, :], xnew[u.parity][:, j, :],
                                                 nsrc_c[:, bass.ds(u.no * UT + j, 1)], None, ALU.mult)
                    last.then_inc(Q("scaled"), 1)

                def slots(u):
                    nt, p = tiles_in(u), u.parity
                    dve.wait_ge(Q("slots_in", p), rows_in_value(u))
                    dve.tensor_scalar(slot_idx[:, bass.ds(u.no * UT, nt)], got8[p][:, 0:nt, 0], 0, None, ALU.add)
                    need(dve, Q("deg_1"), u.done - 1)
                    dve.tensor_copy(deg8[:, 0:nt], got8[p][:, 0:nt, 1]).then_inc(Q("slots_kept"), 1)
                    dve.wait_ge(Q("slots_kept"), u.done)
                    need(dve, Q("rdeg_ready"), u.done - 1)
                    dve.tensor_scalar(deg8b[:, 0:nt], deg8[:, 0:nt], 1.0, None, ALU.max).then_inc(Q("deg_1"), 1)
                    dve.wait_ge(Q("deg_1"), u.done)
                    need(dve, Q("nsrc_root"), u.done - 1)
                    dve.reciprocal(rdeg8[:, 0:nt], deg8b[:, 0:nt]).then_inc(Q("rdeg_ready"), 1)

                def src_weights(u):
                    nt = tiles_in(u)
                    at = bass.ds(u.no * UT, nt)
                    dve.wait_ge(Q("nsrc_root"), u.done)
                    dve.tensor_scalar(nsrc_c[:, at], nsrc8[:, 0:nt], 1.0, None, ALU.mult)
                    dve.tensor_tensor(w0_c[:, at], nsrc8[:, 0:nt], ew_c[:, at], ALU.mult).then_inc(Q("w0_ready"), 1)

                def elu_message(u):
                    nt, p = tiles_in(u), u.parity
                    dve.wait_ge(Q("exp_done"), u.done)
                    need(dve, Q("summed"), u.done - 1)
                    dve.scalar_tensor_tensor(flat(n_u0, nt), flat(n_u3, nt), -1.0, flat(n_u1, nt), ALU.add, ALU.add
                                             ).then_inc(Q("elu_done"), 1)
                    dve.wait_ge(Q("elu_done"), u.done)
                    dve.wait_ge(Q("w0_in", p), u.half * 16 + 16)
                    dve.tensor_tensor(flat(n_u0, nt), flat(n_u0, nt), flat((n_x3, n_x3b)[p], nt), ALU.mult
                                      ).then_inc(Q("message"), 1)

                def total(u):
                    nt, p = tiles_in(u), u.parity
                    if front == "bn_elu":
                        dve.wait_ge(Q("message"), u.done)
                        src = flat(n_u0, nt)
                    else:
                        dve.wait_ge(Q("turned"), u.done)
                        src = self.psT[:, 0:nt * P]
                    need(dve, Q("product"), u.done - 2)
                    need(dve, Q("summed"), u.done - 1)
                    start = 0.0 if first(u.no) else agg[1 - p][:, UT - 1, P - 1:P]
                    dve.tensor_tensor_scan(flat(agg[p], nt), same[:, bass.ds(u.no * UE, nt * P)], src, start,
                                           ALU.mult, ALU.add).then_inc(Q("summed"), 1)

                def sums(u):
                    nt = tiles_in(u)
                    dve.wait_ge(Q("squared"), u.done)
                    need(dve, Q("sums"), u.done - 1)
                    for to, x in ((z_sum, outr[u.parity]), (sq_sum, sq)):
                        last = dve.tensor_tensor(to[:, 0:nt, :], to[:, 0:nt, :], x[:, 0:nt, :], ALU.add)
                    last.then_inc(Q("sums"), 1)

                def biased(u):
                    nt, p = tiles_in(u), u.parity
                    to = outr[p] if post == "bias" else sq
                    dve.wait_ge(Q("product"), u.done)
                    if post == "bias":
                        need(dve, Q("out_out", p), u.half * 16)
                    if post == "gelu":
                        need(dve, Q("out_ready"), u.done - 1)
                    if post == "affine":
                        need(dve, Q("normed"), u.done - 1)
                    by = rdeg_c if post == "bias" else nd_c
                    for j in range(nt):
                        last = dve.scalar_tensor_tensor(to[:, j, :], psH[:, j * P:(j + 1) * P],
                                                        by[:, bass.ds(u.no * UT + j, 1)], self.bias, ALU.mult, ALU.add)
                    if post == "bias":
                        last.then_inc(Q("out_ready"), 1)
                    else:
                        last.then_inc(Q("psZ_used"), 1)
                    if post == "affine":
                        dve.wait_ge(Q("psZ_used"), u.done)
                        norm_p.stats(dve, Q, u, sq, nt)

                def affine(u):
                    nt, p = tiles_in(u), u.parity
                    norm_p.scale(dve, Q, u, nt, shift=False)
                    dve.wait_ge(Q("np_scale"), u.done)
                    need(dve, Q("out_ready"), u.done - 1)
                    for j in range(nt):
                        last = dve.scalar_tensor_tensor(sq2[:, j, :], sq[:, j, :], norm_p.rs[:, j:j + 1],
                                                        row["L2_gnn_gamma"][:, :], ALU.mult, ALU.mult)
                    last.then_inc(Q("normed"), 1)

                return {"scale_x": scale_x, "slots": slots, "src_weights": src_weights, "affine": affine, "sums": sums, "biased": biased, "elu_message": elu_message,
                        "total": total, "before_norm": before_norm,
                        "scale_h": lambda u: norm_h.scale(dve, Q, u, tiles_in(u))}

        class Nodes:
            def __init__(self, edges):
                self.edges, self.units = edges, NU if edges else NUN
                self.Q = S.named("edge_nodes" if edges else "nodes")
                self.plan = PLAN["edge_nodes" if edges else "nodes"]
                self.psS = psH if edges else psB0
                self.skew = {step: skew for step, (skew, _) in self.plan.items()}
                last = max(self.skew.values())
                self.bodies = self.units + last
                self.first = self.skew["stats1"]
                self.norm_units = self.units + self.skew["apply4"] - 1 - self.first

            def count(self, v, step):
                n = v.no + (1 + self.first - self.skew[step])
                return min(max(n, 0), self.units) if isinstance(n, int) else n

            def scaled(self, eng, u, step):
                off = self.skew[step] - self.first
                eng.wait_ge(self.Q("scales"), u.no + off)
                return (u.parity + off - 1) % 2

            def stats(self, dve, u, lane, src, nt):
                for j in range(nt):
                    last = dve.bn_stats(n_st[:, lane * UT + j, :], src[:, j, :])
                last.then_inc(self.Q(f"n{lane + 1}_stats"), 1)

            def apply(self, act, u, lane, step, src, dst, done, nt):
                p = self.scaled(act, u, step)
                for j in range(nt):
                    at = lane * UT + j
                    last = act.activation(dst[:, j, :], src[:, j, :], ACT.Identity, bias=n_nm[p][:, at:at + 1],
                                          scale=n_rs[p][:, at:at + 1])
                last.then_inc(self.Q(done), 1)

            def tiles(self, u):
                return tiles_in(u) if self.edges else UT

            def span(self, ap, u):
                start = 0 if first(u.no) else (u.no - 1) * UE + FIRST_NODES
                return ap[bass.ds(start, UE), :].rearrange("(p t) f -> p t f", t=UT)

            def sp_steps(self, sp):
                Q = self.Q

                def load(u):
                    nt = self.tiles(u)
                    if not self.edges:
                        need(sp, Q("u0_ready"), u.done - 1)
                        hold(sp, Q)
                        sp.dma_start(n_xin[:, :, :], self.span(A["x"], u)).then_inc(Q("x_in"), 16)
                        return
                    need(sp, Q("u0_ready"), u.done - 1)
                    hold(sp, Q)
                    sp.dma_start(n_xin[:, 0:nt, :], rows(x0d, u)).then_inc(Q("x_in"), 16)
                    need(sp, Q("z3_used"), u.done - 1)
                    hold(sp, Q)
                    sp.dma_start(raw[0][:, 0:nt, :], rows(tabs["z3"], u)).then_inc(Q("z3_in"), 16)

                def load_a1(u):
                    need(sp, Q("u1_ready"), u.done - 1)
                    hold(sp, Q)
                    sp.dma_start(xinh[0][:, 0:self.tiles(u), :], rows(tabs["a1"], u)).then_inc(Q("a1_in"), 16)

                def load_a2(u):
                    need(sp, Q("u2_ready"), u.done - 1)
                    hold(sp, Q)
                    sp.dma_start(xinh[1][:, 0:self.tiles(u), :], rows(tabs["a2"], u)).then_inc(Q("a2_in"), 16)

                def load_n1(u):
                    nt = self.tiles(u)
                    need(sp, Q("nT_turned"), u.done - 1)
                    hold(sp, Q)
                    sp.dma_start(raw[1][:, 0:nt, :], rows(tabs["n1"], u)).then_inc(Q("n1_in"), 16)

                def load_a4(u):
                    nt = self.tiles(u)
                    need(sp, Q("x3b_ready"), u.done - 1)
                    hold(sp, Q)
                    sp.dma_start(uh[:, 0:nt, :], rows(tabs["a4"], u)).then_inc(Q("a4_in"), 16)

                def store(u):
                    need(sp, Q("out_out"), (u.done - 1) * 16)
                    hold(sp, Q)
                    sp.wait_ge(Q("out_done"), u.done)
                    hold(sp, Q)
                    sp.dma_start(self.span(out, u), n_out[:, :, :]).then_inc(Q("out_out"), 16)

                def dst_store(u):
                    sp.wait_ge(Q("dst_in", u.parity), u.half * (16 * DT) + 16 * DT)
                    hold(sp, Q)
                    sp.dma_start(x0d[bass.ds(u.no * (DT * P), DT * P), :].rearrange("(t p) f -> p t f", p=P),
                                 xdst[u.parity][:, :, :]).then_inc(Q("dst_out", u.parity), 16)

                return {"dst_store": dst_store, "load_n1": load_n1, "load_a4": load_a4, "load_a2": load_a2, "load_a1": load_a1, "load": load, "store": store}

            def pool_steps(self, pool):
                Q = self.Q

                def add0(u):
                    nt = self.tiles(u)
                    need(pool, Q("u0_turned"), u.done - 1)
                    need(pool, Q("n1_stats"), u.done - 1)
                    pool.wait_ge(Q("x_in"), u.done * 16)
                    if self.edges:
                        pool.wait_ge(Q("u0_part"), u.done)
                        pool.tensor_tensor(n_u0[:, 0:nt, :], outr[0][:, 0:nt, :], n_xin[:, 0:nt, :], ALU.add
                                           ).then_inc(Q("u0_ready"), 1)
                    else:
                        pool.tensor_tensor(n_u0[:, :, :], n_xin[:, :, :], over(c3_row), ALU.add
                                           ).then_inc(Q("u0_ready"), 1)

                def add3(u):
                    nt = self.tiles(u)
                    need(pool, Q("u3_ready"), u.done - 1)
                    if self.edges:
                        pool.wait_ge(Q("a4_in"), u.done * 16)
                    pool.wait_ge(Q("x3_done"), u.done)
                    add = uh[:, 0:nt, :] if self.edges else over(row["L3_gnn_b2"])
                    pool.tensor_tensor(n_x3b[:, 0:nt, :], n_x3[:, 0:nt, :], add, ALU.add).then_inc(Q("x3b_ready"), 1)

                def put_index(u):
                    need(pool, Q("put_out"), (u.done - 1) * (16 * UT))
                    pool.tensor_copy(put8[:, :], put_idx[:, bass.ds(u.no * UT, UT)]).then_inc(Q("put_index"), 1)

                def put(u):
                    nt = self.tiles(u)
                    pool.wait_ge(Q("out_done"), u.done)
                    pool.wait_ge(Q("put_index"), u.done)
                    hold(pool, Q)
                    for j in range(nt):
                        pool.indirect_dma_start(
                            out=out, out_offset=bass.IndirectOffsetOnAxis(ap=put8[:, j:j + 1], axis=0),
                            in_=n_out[:, j, :], in_offset=None, bounds_check=N - 1, oob_is_err=False
                        ).then_inc(Q("put_out"), 16)

                def dst_index(u):
                    need(pool, Q("dst_in", u.parity), u.half * (16 * DT))
                    pool.tensor_copy(dst2[u.parity][:, :], dst_idx[:, bass.ds(u.no * DT, DT)]
                                     ).then_inc(Q("dst_index"), 1)

                def dst_gather(u):
                    need(pool, Q("dst_out", u.parity), u.half * 16)
                    pool.wait_ge(Q("dst_index"), u.done)
                    hold(pool, Q)
                    for j in range(DT):
                        pool.indirect_dma_start(
                            out=xdst[u.parity][:, j, :], out_offset=None, in_=A["x"],
                            in_offset=bass.IndirectOffsetOnAxis(ap=dst2[u.parity][:, j:j + 1], axis=0)
                        ).then_inc(Q("dst_in", u.parity), 16)

                return {"dst_index": dst_index, "dst_gather": dst_gather, "add3": add3, "add0": add0, "put_index": put_index, "put": put}

            def pe_steps(self, pe):
                Q = self.Q

                def turn0(u):
                    pe.wait_ge(Q("u0_ready"), u.done)
                    need(pe, Q("u1_ready"), u.done - 1)
                    turn_over(pe, psA, n_u0, self.tiles(u)).then_inc(Q("u0_turned"), 1)

                def product0(u):
                    pe.wait_ge(Q("xT_ready"), u.done)
                    products(pe, psA, n_xT, wsC[:, :], self.tiles(u)).then_inc(Q("self_done"), 1)

                def turn3(u):
                    nt = self.tiles(u)
                    if self.edges:
                        need(pe, Q("hT_ready", 0), u.done - 1)
                    else:
                        need(pe, Q("u3_ready"), u.done - 1)
                    pe.wait_ge(Q("x3_done"), u.done)
                    turn_over(pe, psB0, n_x3, nt).then_inc(Q("x3_turned"), 1)

                def turn_n(u):
                    need(pe, Q("nT_ready"), u.done - 1)
                    need(pe, Q("u3_ready"), u.done - 2)
                    pe.wait_ge(Q("n1_in"), u.done * 16)
                    turn_over(pe, psH, raw[1], self.tiles(u)).then_inc(Q("nT_turned"), 1)

                def hidden(u, c):
                    nt, ps = self.tiles(u), (psB0, psB1)[c]
                    pe.wait_ge(Q("x3T_ready"), u.done)
                    if self.edges:
                        pe.wait_ge(Q("nT_ready"), u.done)
                    if c == 1:
                        need(pe, Q("hT_ready", 1), u.done - 1)
                    for at, n in halves(nt):
                        last = pe.matmul(ps[:, at:at + n], ws1[:, c * P:(c + 1) * P], flat(n_x3T)[:, at:at + n],
                                         start=True, stop=not self.edges)
                        if self.edges:
                            last = pe.matmul(ps[:, at:at + n], wn1[:, c * P:(c + 1) * P], flat(xnew[0])[:, at:at + n],
                                             start=False, stop=True)
                    last.then_inc(Q("hidden", c), 1)

                def second(u):
                    pe.wait_ge(Q("hT_ready", 0), u.done)
                    pe.wait_ge(Q("hT_ready", 1), u.done)
                    if self.edges:
                        pe.wait_ge(Q("nT_ready"), min(u.done + 1, NU) if isinstance(u.done, int) else u.done + 1)
                        need(pe, Q("u3_ready"), u.done - 1)
                    for j in range(self.tiles(u)):
                        for c in range(2):
                            last = pe.matmul(self.psS[:, j * P:(j + 1) * P], n_hT[c][:, j, :], ws2[:, c, :],
                                             start=(c == 0), stop=(c == 1))
                    last.then_inc(Q("sage_done"), 1)

                return {"turn3": turn3, "turn_n": turn_n, "hidden0": lambda u: hidden(u, 0), "hidden1": lambda u: hidden(u, 1),
                        "second": second, "turn0": turn0, "product0": product0}

            def act_steps(self, act):
                Q = self.Q

                def apply4(u):
                    if self.edges:
                        need(act, Q("put_out"), (u.done - 1) * (16 * UT))
                    else:
                        need(act, Q("out_out"), (u.done - 1) * 16)
                    self.apply(act, u, 3, "apply4", n_u3, n_out, "out_done", self.tiles(u))

                def apply3(u):
                    need(act, Q("x3_turned"), u.done - 1)
                    need(act, Q("x3b_ready"), u.done - 1)
                    self.apply(act, u, 2, "apply3", n_u2, n_x3, "x3_done", self.tiles(u))

                def copy3(u):
                    nt = self.tiles(u)
                    act.wait_ge(Q("x3_turned"), u.done)
                    need(act, Q("hidden", 0), u.done - 1)
                    need(act, Q("hidden", 1), u.done - 1)
                    act.activation(flat(n_x3T, nt), psB0[:, 0:nt * P], ACT.Copy).then_inc(Q("x3T_ready"), 1)

                def copy_n(u):
                    nt = self.tiles(u)
                    act.wait_ge(Q("nT_turned"), u.done)
                    for c in range(2):
                        need(act, Q("hidden", c), u.done - 1)
                    act.activation(flat(xnew[0], nt), psH[:, 0:nt * P], ACT.Copy).then_inc(Q("nT_ready"), 1)

                def relu(u, c):
                    nt, ps = self.tiles(u), (psB0, psB1)[c]
                    need(act, Q("sage_done"), u.done - 1)
                    act.wait_ge(Q("hidden", c), u.done)
                    act.activation(flat(n_hT[c], nt), ps[:, 0:nt * P], ACT.Relu, bias=b1_col[:, c:c + 1]
                                   ).then_inc(Q("hT_ready", c), 1)

                def copy0(u):
                    nt = self.tiles(u)
                    act.wait_ge(Q("u0_turned"), u.done)
                    need(act, Q("self_done"), u.done - 1)
                    act.activation(flat(n_xT, nt), psA[:, 0:nt * P], ACT.Copy).then_inc(Q("xT_ready"), 1)

                def root(v):
                    need(act, Q("scales"), v.done - 1)
                    act.wait_ge(Q("nodes_var"), v.done)
                    act.activation(n_sd[:, :], n_mv[:, 4, :], ACT.Sqrt, bias=eps_col[:, :], scale=1.0 / P
                                   ).then_inc(Q("roots"), 1)

                return {"apply3": apply3, "copy3": copy3, "copy_n": copy_n, "apply4": apply4, "copy0": copy0, "root": root,
                        "relu0": lambda u: relu(u, 0), "relu1": lambda u: relu(u, 1)}

            def dve_steps(self, dve):
                Q = self.Q

                def var(v):
                    for lane, step in enumerate(("stats1", "sum1", "sum2", "sum3")):
                        need(dve, Q(f"n{lane + 1}_stats"), self.count(v, step))
                    variances(dve, Q, v, n_st, n_mv, "nodes")

                def scale(v):
                    rs, nm = n_rs[v.parity], n_nm[v.parity]
                    dve.wait_ge(Q("roots"), v.done)
                    if not first(v.no):
                        before = Unit(v.half, v.parity).back(1)
                        need(dve, Q("x3_done"), self.count(before, "apply3"))
                        need(dve, Q("out_done"), self.count(before, "apply4"))
                    dve.reciprocal(rs[:, :], n_sd[:, :]).then_inc(Q("nodes_rs"), 1)
                    dve.wait_ge(Q("nodes_rs"), v.done)
                    dve.scalar_tensor_tensor(nm[:, :], n_mv[:, 0, :], -0.5, rs[:, :], ALU.mult, ALU.mult
                                             ).then_inc(Q("scales"), 1)

                def sum3(u):
                    nt = self.tiles(u)
                    need(dve, Q("out_done"), u.done - 1)
                    dve.wait_ge(Q("x3b_ready"), u.done)
                    dve.wait_ge(Q("sage_done"), u.done)
                    dve.tensor_tensor(n_u3[:, 0:nt, :], tiles(self.psS, nt), n_x3b[:, 0:nt, :], ALU.add
                                      ).then_inc(Q("u3_ready"), 1)
                    dve.wait_ge(Q("u3_ready"), u.done)
                    self.stats(dve, u, 3, n_u3, nt)

                def sum2(u):
                    nt = self.tiles(u)
                    rs = n_rs[self.scaled(dve, u, "sum2")]
                    need(dve, Q("x3_done"), u.done - 1)
                    if self.edges:
                        dve.wait_ge(Q("a2_in"), u.done * 16)
                    for j in range(nt):
                        last = dve.scalar_tensor_tensor(n_u2[:, j, :], n_u1[:, j, :], rs[:, UT + j:UT + j + 1],
                                                        xinh[1][:, j, :] if self.edges else a2_row[:, :],
                                                        ALU.mult, ALU.add)
                    last.then_inc(Q("u2_ready"), 1)
                    dve.wait_ge(Q("u2_ready"), u.done)
                    self.stats(dve, u, 2, n_u2, nt)

                def sum1(u):
                    nt = self.tiles(u)
                    rs = n_rs[self.scaled(dve, u, "sum1")]
                    dve.wait_ge(Q("self_done"), u.done)
                    need(dve, Q("u2_ready"), u.done - 1)
                    if self.edges:
                        dve.wait_ge(Q("a1_in"), u.done * 16)
                    for j in range(nt):
                        last = dve.scalar_tensor_tensor(n_u1[:, j, :], psA[:, j * P:(j + 1) * P], rs[:, j:j + 1],
                                                        xinh[0][:, j, :] if self.edges else row["L1_gnn_b_self"][:, :],
                                                        ALU.mult, ALU.add)
                    last.then_inc(Q("u1_ready"), 1)
                    dve.wait_ge(Q("u1_ready"), u.done)
                    self.stats(dve, u, 1, n_u1, nt)

                def stats1(u):
                    nt = self.tiles(u)
                    dve.wait_ge(Q("u0_ready"), u.done)
                    self.stats(dve, u, 0, n_u0, nt)

                def part0(u):
                    nt = self.tiles(u)
                    need(dve, Q("u0_ready"), u.done - 1)
                    dve.wait_ge(Q("z3_in"), u.done * 16)
                    dve.tensor_tensor(outr[0][:, 0:nt, :], raw[0][:, 0:nt, :], over(a3_row, nt), ALU.mult
                                      ).then_inc(Q("z3_used"), 1)
                    dve.wait_ge(Q("z3_used"), u.done)
                    dve.tensor_tensor(outr[0][:, 0:nt, :], outr[0][:, 0:nt, :], over(c3_row, nt), ALU.add
                                      ).then_inc(Q("u0_part"), 1)

                return {"sum3": sum3, "sum2": sum2, "sum1": sum1, "stats1": stats1, "part0": part0,
                        "var": var, "scale": scale}

        zero_row = zero_f[0:1, :]

        def segments(segs):
            def streams(seg, which):
                hop, nodes, origin = seg["hop"], seg["nodes"], seg["origin"]
                out = []
                if hop is not None:
                    out += [(hop.plan[step][1], (f, hop.plan[step][0], 0, NU))
                            for step, f in which(hop).items() if step in hop.plan]
                if nodes is not None:
                    for step, f in which(nodes).items():
                        if step in ("var", "root", "scale"):
                            out.append((nodes.plan[step][1], (f, 0, origin + nodes.first, nodes.norm_units)))
                        elif step in nodes.plan:
                            out.append((nodes.plan[step][1], (f, nodes.plan[step][0], origin, nodes.units)))
                out = [step for _, step in sorted(out, key=lambda x: x[0])]
                return out

            with nc.Block() as block:
                @block.gpsimd
                def _(pool):
                    for n, seg in enumerate(segs):
                        if n and segs[n - 1]["hop"] is not None:
                            segs[n - 1]["hop"].stored(pool)
                        steps = streams(seg, lambda x: x.pool_steps(pool))
                        if steps:
                            run(pool, seg["bodies"], steps)
                        if seg["nodes"] is not None and seg["nodes"].edges:
                            pool.wait_ge(seg["nodes"].Q("put_out"), 16 * NT)

                @block.sync
                def _(sp):
                    for n, seg in enumerate(segs):
                        hop = seg["hop"]
                        if n and segs[n - 1]["hop"] is not None:
                            segs[n - 1]["hop"].stored(sp)
                        if hop is not None and hop.none is not None:
                            sp.dma_start(hop.dest[NONE_ROW:NONE_ROW + 1, :], hop.none).then_inc(hop.Q("none_out"), 16)
                        steps = streams(seg, lambda x: x.sp_steps(sp))
                        run(sp, seg["bodies"], steps)
                        if hop is not None and hop is segs[-1]["hop"]:
                            hop.stored(sp)
                    for seg in segs:
                        if seg["nodes"] is not None and not seg["nodes"].edges:
                            sp.wait_ge(seg["nodes"].Q("out_out"), 16 * NUN)
                            for p in range(2):
                                sp.wait_ge(seg["nodes"].Q("dst_out", p), 16 * ((NUN + 1 - p) // 2))
                            break

                @block.tensor
                def _(pe):
                    for seg in segs:
                        hop = seg["hop"]
                        stats = hop is not None and hop.post == "stats"
                        run(pe, seg["bodies"], streams(seg, lambda x: x.pe_steps(pe)))
                        if stats:
                            pe.wait_ge(hop.Q("sums"), NU)
                            for ps, x in ((psB0, z_sum), (psB1, sq_sum)):
                                for j in range(UT):
                                    last = pe.matmul(ps[:, 0:1], x[:, j, :], ones_col[:, :],
                                                     start=(j == 0), stop=(j == UT - 1))
                            last.then_inc(hop.Q("stats_done"), 1)

                @block.scalar
                def _(act):
                    for seg in segs:
                        run(act, seg["bodies"], streams(seg, lambda x: x.act_steps(act)))

                @block.vector
                def _(dve):
                    for seg in segs:
                        if seg["hop"] is not None and seg["hop"].post == "stats":
                            dve.memset(z_sum[:, :, :], 0.0)
                            dve.memset(sq_sum[:, :, :], 0.0).then_inc(seg["hop"].Q("sums_clear"), 1)
                            dve.wait_ge(seg["hop"].Q("sums_clear"), 1)
                        run(dve, seg["bodies"], streams(seg, lambda x: x.dve_steps(dve)))
                        if seg["hop"] is not None and seg["hop"].post == "stats":
                            bn_finish(dve, seg["hop"].Q)
            S.close()

        def segment(hop=None, nodes=None, origin=0, bodies=None):
            bodies = bodies or NU + max(skew for skew, _ in hop.plan.values())
            return {"hop": hop, "nodes": nodes, "origin": origin, "bodies": bodies}

        def bn_finish(dve, Q):
            dve.wait_ge(Q("stats_done"), 1)
            dve.tensor_scalar(bn_t[:, 0:1], psB0[:, 0:1], 1.0 / N, None, ALU.mult)
            dve.tensor_scalar(bn_t[:, 1:2], psB1[:, 0:1], 1.0 / N, None, ALU.mult
                              ).then_inc(Q("moments"), 1)
            dve.wait_ge(Q("moments"), 1)
            dve.tensor_tensor(bn_t[:, 2:3], bn_t[:, 0:1], bn_t[:, 0:1], ALU.mult).then_inc(Q("moments"), 1)
            dve.wait_ge(Q("moments"), 2)
            dve.tensor_tensor(bn_t[:, 3:4], bn_t[:, 1:2], bn_t[:, 2:3], ALU.subtract)

        def bn_coefficients(rows_too):
            with nc.Block() as block:
                @block.scalar
                def _(act):
                    act.activation(bn_t[:, 4:5], bn_t[:, 3:4], ACT.Sqrt, bias=eps_col[:, :]).then_inc(S("bn_root"), 1)

                @block.vector
                def _(dve):
                    chain = Chain(dve, S("dve_step"))
                    dve.wait_ge(S("bn_root"), 1)
                    chain.step(dve.reciprocal(bn_t[:, 5:6], bn_t[:, 4:5]))
                    chain.wait()
                    chain.step(dve.tensor_tensor(bn_a[:, :], bn_t[:, 5:6], gam_col[:, :], ALU.mult))
                    chain.wait()
                    chain.step(dve.tensor_tensor(bn_t[:, 6:7], bn_a[:, :], bn_t[:, 0:1], ALU.mult))
                    chain.wait()
                    chain.step(dve.tensor_tensor(bn_c[:, :], bet_col[:, :], bn_t[:, 6:7], ALU.subtract))
                    dve.tensor_tensor(bn_nc[:, :], bn_t[:, 6:7], bet_col[:, :], ALU.subtract)
                    dve.tensor_scalar(bn_na[:, :], bn_a[:, :], -1.0, None, ALU.mult)
                    chain.wait()
                    if rows_too:
                        dve.tensor_scalar(diag[:, 0, :], ident[:, :], bn_a[:, :], None, ALU.mult)
                        dve.tensor_scalar(diag[:, 1, :], ident[:, :], bn_c[:, :], None, ALU.mult
                                          ).then_inc(S("diag_ready"), 1)
                        dve.wait_ge(S("bn_rows"), 1)
                        dve.tensor_copy(a3_row[:, :], psA[:, 0:P])
                        dve.tensor_copy(c3_row[:, :], psA[:, P:2 * P])

                @block.tensor
                def _(pe):
                    if rows_too:
                        pe.wait_ge(S("diag_ready"), 1)
                        pe.matmul(psA[:, 0:P], ones_mat[:, :], diag[:, 0, :], start=True, stop=True)
                        pe.matmul(psA[:, P:2 * P], ones_mat[:, :], diag[:, 1, :], start=True, stop=True
                                  ).then_inc(S("bn_rows"), 1)
            S.close()

        with nc.Block() as block:
            @block.scalar
            def _(act):
                for k, n in enumerate(("L2_gnn_b1", "L2_gnn_b2", "L2_gnn_b3")):
                    act.activation(none_rows[:, k, :], row[n][:, :], ACT.Gelu)
                norm_h.root(act, S.named("c"), Unit(0, 0))
                norm_h.apply(act, S.named("c"), Unit(0, 0), over(row["L2_gnn_b4"]), sq, "done")

            @block.vector
            def _(dve):
                dve.memset(n_st[:, :, :], 0.0)
                norm_h.stats(dve, S.named("c"), Unit(0, 0), over(row["L2_gnn_b4"]))
                norm_h.scale(dve, S.named("c"), Unit(0, 0))
                dve.wait_ge(S.named("c")("done"), 1)
                dve.tensor_tensor(a2_row[:, :], sq[:, 0, :], row["L2_gnn_gamma"][:, :], ALU.mult
                                  ).then_inc(S("scaled"), 1)
                dve.wait_ge(S("scaled"), 1)
                dve.tensor_tensor(a2_row[:, :], a2_row[:, :], row["L2_gnn_beta"][:, :], ALU.add)
        S.close()

        segments([segment(Hop("h0", "weight", w["L0_gnn_W1"][:, :], "stats", tabs["z1"], x_from=xs["x0"], col=w0_c,
                              none=zero_row))])
        with nc.Block() as block:
            @block.tensor
            def _(pe):
                pe.transpose(psA[:, 0:P], w0_c[:, 0:P], ident[:, :])
                pe.transpose(psA[0:T1, P:2 * P], w0_c[:, P:NT], ident[:, :]).then_inc(S("w0_turned"), 1)

            @block.vector
            def _(dve):
                dve.wait_ge(S("w0_turned"), 1)
                dve.tensor_copy(w0_t[:, 0, :], psA[:, 0:P])
                dve.tensor_copy(w0_t[0:T1, 1, :], psA[0:T1, P:2 * P]).then_inc(S("w0_rows"), 1)

            @block.sync
            def _(sp):
                sp.wait_ge(S("w0_rows"), 1)
                sp.dma_start(w0_lin[0:P, :], w0_t[:, 0, :]).then_inc(S("w0_out"), 16)
                sp.dma_start(w0_lin[P:NT, :], w0_t[0:T1, 1, :]).then_inc(S("w0_out"), 16)
                sp.wait_ge(S("w0_out"), 32)
        S.close()
        bn_coefficients(False)
        segments([segment(Hop("h1", "bn_elu", w["L0_gnn_W2"][:, :], "stats", tabs["z2"], table=tabs["z1"], idx=slot_idx,
                              none=zero_row))])
        bn_coefficients(False)
        segments([segment(Hop("h2", "bn_elu", w["L0_gnn_W3"][:, :], "stats", tabs["z3"], table=tabs["z2"], idx=slot_idx,
                              none=zero_row))])
        bn_coefficients(True)

        def hops(which):
            return [NU + max(skew for skew, _ in PLAN[k].values()) for k in which]

        nodes = Nodes(False)
        beside_bodies = hops([("weight", "gelu", False)] * 2 + [("weight", "affine", False), ("ln_add", "scale", False)])
        start = sum(beside_bodies) - nodes.bodies
        assert 0 <= start < NU and NT == DT * NUN
        beside = [dict(nodes=nodes, origin=start - sum(beside_bodies[:k])) for k in range(4)]
        segments([
            segment(Hop("h3", "ln_bn", wnT[:, :], "bias", tabs["a1"], table=tabs["z3"], idx=slot_idx, x_from=xs["x0"],
                        x_to=xs["x1"], bias=row["L1_gnn_b_self"][:, :], none=row["L1_gnn_b_self"][0:1, :])),
            segment(Hop("h4", "ln_self", w["L2_gnn_W1"][:, :], "gelu", tabs["g1"], table=tabs["a1"], idx=slot_idx,
                        x_from=xs["x1"], x_to=xs["x2"], bias=row["L2_gnn_b1"][:, :], none=none_rows[0:1, 0, :])),
        ])
        segments([
            segment(Hop("h5", "weight", w["L2_gnn_W2"][:, :], "gelu", tabs["g2"], table=tabs["g1"], idx=slot_idx,
                        col=nsrc_c, bias=row["L2_gnn_b2"][:, :], none=none_rows[0:1, 1, :], apart=False), **beside[0]),
            segment(Hop("h6", "weight", w["L2_gnn_W3"][:, :], "gelu", tabs["g3"], table=tabs["g2"], idx=slot_idx,
                        col=nsrc_c, bias=row["L2_gnn_b3"][:, :], none=none_rows[0:1, 2, :], apart=False), **beside[1]),
            segment(Hop("h7", "weight", w4C[:, :], "affine", tabs["a2"], table=tabs["g3"], idx=slot_idx,
                        col=nsrc_c, bias=b4C[:, :], none=a2_row[0:1, :], apart=False), **beside[2]),
            segment(Hop("h8", "ln_add", ident[:, :], "scale", tabs["n1"], table=tabs["a2"], idx=slot_idx,
                        x_from=xs["x2"], x_to=xs["x3"], none=zero_row, apart=False), **beside[3]),
        ])
        segments([segment(Hop("h9", "sage", ident[:, :], "bias", tabs["a4"], table=tabs["n1"], idx=slot_idx,
                              x_from=xs["x3"], bias=row["L3_gnn_b2"][:, :]))])
        edge_nodes = Nodes(True)
        segments([segment(nodes=edge_nodes, bodies=edge_nodes.bodies)])


def kernel(**inputs):
    import numpy as _np
    import concourse.bacc as _bacc
    from concourse import mybir as _mybir
    from concourse.bass_utils import run_bass_kernel_spmd as _run

    nc = _bacc.Bacc("TRN2", target_bir_lowering=False, num_devices=1)
    arrays, aps = {}, {}
    for name, value in inputs.items():
        a = _np.ascontiguousarray(value)
        arrays[f"in_{name}_dram"] = a
        aps[name] = nc.dram_tensor(f"in_{name}_dram", a.shape, _mybir.dt.from_np(a.dtype), kind="ExternalInput").ap()
    y = nc.dram_tensor("out_0_dram", inputs["x"].shape, _mybir.dt.float32, kind="ExternalOutput").ap()
    gnn_stack(nc, aps, y)
    r = _run(nc, [arrays], core_ids=[0])
    return r.results[0]["out_0_dram"]
```
